# Optimizing a Trainium2 kernel written in Bass

```python
import numpy as np
import jax
import jax.numpy as jnp

def _softmax(x, axis=-1):
    return jax.nn.softmax(x, axis=axis)

def _gelu(x):
    return jax.nn.gelu(x, approximate=True)

def _silu(x):
    return jax.nn.silu(x)

def _sigmoid(x):
    return jax.nn.sigmoid(x)

def _layernorm(x, axis=-1, eps=1e-05):
    m = jnp.mean(x, axis=axis, keepdims=True)
    v = jnp.var(x, axis=axis, keepdims=True)
    return (x - m) / jnp.sqrt(v + eps)

def _scatter_add(tgt, idx, src, axis=0):
    return tgt.at[idx].add(src)

def _segment_sum(src, seg, n):
    return jax.ops.segment_sum(src, seg, n)
kernel_name = 'mk_seq_postln_d2_jaxref_r8_d7958b'

def setup_inputs(seed: int=0):
    np.random.seed(seed)
    _w = jnp.asarray

    def _L0_attn_setup():
        import jax, jax.numpy as jnp
        import numpy as np
        from jax import lax
        D_MODEL = 128
        D_STATE = 128
        D_CONV = 4
        EXPAND = 2
        HEADDIM = 64
        D_INNER = EXPAND * D_MODEL
        NHEADS = D_INNER // HEADDIM
        CONV_DIM = D_INNER + 2 * D_STATE
        D_IN_PROJ = 2 * D_INNER + 2 * D_STATE + NHEADS
        B_SZ, L_SEQ = (4, 256)
        EPS = 1e-05

        def _mamba_block(x, in_proj_w, conv_w, conv_b, dt_bias, A_log, D, norm_w, out_proj_w, ln_w, ln_b):
            b, l, _ = x.shape
            zxbcdt = jnp.einsum('bld,ed->ble', x, in_proj_w)
            z = zxbcdt[..., :D_INNER]
            xBC = zxbcdt[..., D_INNER:D_INNER + CONV_DIM]
            dt = jax.nn.softplus(zxbcdt[..., D_INNER + CONV_DIM:] + dt_bias)
            xBC_t = xBC.transpose(0, 2, 1)
            conv = lax.conv_general_dilated(xBC_t, conv_w[:, None, :], (1,), [(D_CONV - 1, 0)], feature_group_count=CONV_DIM, dimension_numbers=('NCW', 'OIW', 'NCW'))
            xBC = jax.nn.silu(conv + conv_b[:, None]).transpose(0, 2, 1)
            x_ssm = xBC[..., :D_INNER].reshape(b, l, NHEADS, HEADDIM)
            Bm = xBC[..., D_INNER:D_INNER + D_STATE]
            Cm = xBC[..., D_INNER + D_STATE:]
            A = -jnp.exp(A_log)
            dA = jnp.exp(dt * A)

            def step(h, inp):
                dA_t, x_t, B_t, C_t, dt_t = inp
                dBx = dt_t[:, :, None, None] * x_t[..., None] * B_t[:, None, None, :]
                h = h * dA_t[:, :, None, None] + dBx
                y = jnp.einsum('bhpn,bn->bhp', h, C_t)
                return (h, y)
            h0 = jnp.zeros((b, NHEADS, HEADDIM, D_STATE), dtype=x.dtype)
            inputs = (dA.transpose(1, 0, 2), x_ssm.transpose(1, 0, 2, 3), Bm.transpose(1, 0, 2), Cm.transpose(1, 0, 2), dt.transpose(1, 0, 2))
            _, ys = lax.scan(step, h0, inputs)
            y = ys.transpose(1, 0, 2, 3) + D[None, None, :, None] * x_ssm
            y = y.reshape(b, l, D_INNER)
            y = y * jax.nn.silu(z)
            y = y * lax.rsqrt(jnp.mean(y * y, axis=-1, keepdims=True) + EPS) * norm_w
            y = jnp.einsum('bld,ed->ble', y, out_proj_w) + x
            mu = jnp.mean(y, axis=-1, keepdims=True)
            var = jnp.mean((y - mu) ** 2, axis=-1, keepdims=True)
            return (y - mu) * lax.rsqrt(var + EPS) * ln_w + ln_b
        key = jax.random.key(seed)
        ks = jax.random.split(key, 10)
        x = jax.random.normal(ks[0], (B_SZ, L_SEQ, D_MODEL), dtype=jnp.float32)
        in_proj_w = jax.random.normal(ks[1], (D_IN_PROJ, D_MODEL), dtype=jnp.float32) * 0.02
        conv_w = jax.random.normal(ks[2], (CONV_DIM, D_CONV), dtype=jnp.float32) * 0.2
        conv_b = jax.random.normal(ks[3], (CONV_DIM,), dtype=jnp.float32) * 0.02
        dt_bias = jax.random.normal(ks[4], (NHEADS,), dtype=jnp.float32) * 0.5
        A_log = jnp.log(jax.random.uniform(ks[5], (NHEADS,), minval=1.0, maxval=16.0, dtype=jnp.float32))
        D = 1.0 + 0.1 * jax.random.normal(ks[6], (NHEADS,), dtype=jnp.float32)
        norm_w = jnp.ones((D_INNER,), dtype=jnp.float32)
        out_proj_w = jax.random.normal(ks[7], (D_MODEL, D_INNER), dtype=jnp.float32) * 0.02
        ln_w = jnp.ones((D_MODEL,), dtype=jnp.float32)
        ln_b = jnp.zeros((D_MODEL,), dtype=jnp.float32)
        return {'x': x, 'in_proj_w': in_proj_w, 'conv_w': conv_w, 'conv_b': conv_b, 'dt_bias': dt_bias, 'A_log': A_log, 'D': D, 'norm_w': norm_w, 'out_proj_w': out_proj_w, 'ln_w': ln_w, 'ln_b': ln_b}
    _L0_attn_in = _L0_attn_setup()

    def _L0_ffn_setup():
        import jax, jax.numpy as jnp
        import numpy as np
        DIM = 128
        DEPTH = 2
        HEADS = 8
        DIM_HEAD = 64
        WINDOW = 64
        INNER = HEADS * DIM_HEAD
        HID = int(DIM * 4 * 2 / 3)
        B, N = (2, 1024)
        QK_SCALE = 8.0

        def shift_token(t):
            t1, t2 = jnp.split(t, 2, axis=-1)
            t2 = jnp.pad(t2, ((0, 0), (1, 0), (0, 0)))[:, :-1]
            return jnp.concatenate([t1, t2], axis=-1)

        def l2norm(t):
            return t / jnp.clip(jnp.linalg.norm(t, axis=-1, keepdims=True), 1e-12)

        def rotate_half(x):
            x1, x2 = jnp.split(x, 2, axis=-1)
            return jnp.concatenate([-x2, x1], axis=-1)

        def rotary_xpos(q, k):
            n = q.shape[-2]
            half_idx = jnp.arange(0, DIM_HEAD, 2, dtype=jnp.float32)
            inv_freq = 1.0 / 10000.0 ** (half_idx / DIM_HEAD)
            t = jnp.arange(n, dtype=jnp.float32)
            freqs = t[:, None] * inv_freq[None, :]
            freqs = jnp.concatenate([freqs, freqs], axis=-1)
            base = (half_idx + 0.4 * DIM_HEAD) / (1.4 * DIM_HEAD)
            power = (t - n // 2) / float(WINDOW // 2)
            scale = base[None, :] ** power[:, None]
            scale = jnp.concatenate([scale, scale], axis=-1)
            cos, sin = (jnp.cos(freqs), jnp.sin(freqs))
            q = q * cos * scale + rotate_half(q) * sin * scale
            k = k * cos / scale + rotate_half(k) * sin / scale
            return (q, k)

        def local_attention(q, k, v):
            b, h, n, d = q.shape
            w = n // WINDOW
            bq = q.reshape(b, h, w, WINDOW, d) * QK_SCALE
            bk = k.reshape(b, h, w, WINDOW, d)
            bv = v.reshape(b, h, w, WINDOW, d)

            def look_around(t):
                p = jnp.pad(t, ((0, 0), (0, 0), (1, 0), (0, 0), (0, 0)))
                return jnp.concatenate([p[:, :, :w], p[:, :, 1:]], axis=3)
            bk, bv = (look_around(bk), look_around(bv))
            bt = jnp.arange(n).reshape(w, WINDOW)
            btp = jnp.pad(bt, ((1, 0), (0, 0)), constant_values=-1)
            btk = jnp.concatenate([btp[:w], btp[1:]], axis=1)
            sim = jnp.einsum('bhwid,bhwjd->bhwij', bq, bk)
            i = bt[:, :, None]
            j = btk[:, None, :]
            mask = (i < j) | (i > j + WINDOW) | (j == -1)
            sim = jnp.where(mask, -jnp.finfo(sim.dtype).max, sim)
            attn = jax.nn.softmax(sim, axis=-1)
            out = jnp.einsum('bhwij,bhwjd->bhwid', attn, bv)
            return out.reshape(b, h, n, d)

        def _layer(x, wqkv, qs, ksc, wo, lg, lb, w1, b1, w2, b2):
            b, n, _ = x.shape
            h = shift_token(x)
            qkv = h @ wqkv
            q, k, v = jnp.split(qkv, 3, axis=-1)
            to_heads = lambda t: t.reshape(b, n, HEADS, DIM_HEAD).transpose(0, 2, 1, 3)
            q, k, v = (to_heads(q), to_heads(k), to_heads(v))
            q = l2norm(q) * qs
            k = l2norm(k) * ksc
            q, k = rotary_xpos(q, k)
            o = local_attention(q, k, v)
            o = o.transpose(0, 2, 1, 3).reshape(b, n, INNER)
            x = x + o @ wo
            h = shift_token(x)
            mu = h.mean(-1, keepdims=True)
            var = h.var(-1, keepdims=True)
            h = (h - mu) / jnp.sqrt(var + 1e-05) * lg + lb
            h = h @ w1 + b1
            a, g = jnp.split(h, 2, axis=-1)
            h = a * jax.nn.gelu(g, approximate=False)
            x = x + h @ w2 + b2
            return x
        key = jax.random.key(seed)
        ks = jax.random.split(key, 6)
        return {'x': jax.random.normal(ks[0], (B, N, DIM), jnp.float32), 'wqkv': jax.random.normal(ks[1], (DEPTH, DIM, 3 * INNER), jnp.float32) * 0.02, 'q_scale': jnp.ones((DEPTH, DIM_HEAD), jnp.float32), 'k_scale': jnp.ones((DEPTH, DIM_HEAD), jnp.float32), 'wo': jax.random.normal(ks[2], (DEPTH, INNER, DIM), jnp.float32) * 0.02, 'ln_g': jnp.ones((DEPTH, DIM), jnp.float32), 'ln_b': jnp.zeros((DEPTH, DIM), jnp.float32), 'w1': jax.random.normal(ks[3], (DEPTH, DIM, 2 * HID), jnp.float32) * 0.02, 'b1': jnp.zeros((DEPTH, 2 * HID), jnp.float32), 'w2': jax.random.normal(ks[4], (DEPTH, HID, DIM), jnp.float32) * 0.02, 'b2': jnp.zeros((DEPTH, DIM), jnp.float32)}
    _L0_ffn_in = _L0_ffn_setup()

    def _L1_attn_setup():
        import jax, jax.numpy as jnp
        import numpy as np
        B, S, D = (2, 256, 128)
        H, DH = (16, 64)
        DQL, DKVL = (64, 64)
        DR = 64
        TOPK = 64
        LN_EPS = 1e-05
        ROPE_BASE = 10000.0

        def _rope_tables(seq_len, dim):
            inv_freq = 1.0 / ROPE_BASE ** (np.arange(0, dim, 2, dtype=np.float32) / dim)
            t = np.arange(seq_len, dtype=np.float32)
            freqs = np.outer(t, inv_freq)
            cos = np.concatenate([np.cos(freqs), np.cos(freqs)], -1)[:, ::2]
            sin = np.concatenate([np.sin(freqs), np.sin(freqs)], -1)[:, ::2]
            return (jnp.asarray(cos), jnp.asarray(sin))

        def _apply_rope_subspace(x, d_rope):
            s = x.shape[-2]
            cos, sin = _rope_tables(s, d_rope)
            xr, xp = (x[..., :d_rope], x[..., d_rope:])
            e, o = (xr[..., 0::2], xr[..., 1::2])
            rot = jnp.stack([e * cos - o * sin, e * sin + o * cos], axis=-1).reshape(xr.shape)
            return jnp.concatenate([rot, xp], axis=-1)

        def _reference_tuple_inner(x, w_down_q, w_down_kv, w_up_q, w_up_k, w_up_v, w_out, ln_scale, ln_bias):
            b, s, d = x.shape
            residual = x
            mu = jnp.mean(x, axis=-1, keepdims=True)
            var = jnp.mean((x - mu) ** 2, axis=-1, keepdims=True)
            h = (x - mu) * jax.lax.rsqrt(var + LN_EPS) * ln_scale + ln_bias
            c_q = h @ w_down_q.T
            c_kv = h @ w_down_kv.T
            q = (c_q @ w_up_q.T).reshape(b, s, H, DH).transpose(0, 2, 1, 3)
            k = (c_kv @ w_up_k.T).reshape(b, s, H, DH).transpose(0, 2, 1, 3)
            v = (c_kv @ w_up_v.T).reshape(b, s, H, DH).transpose(0, 2, 1, 3)
            q = _apply_rope_subspace(q, DR)
            k = _apply_rope_subspace(k, DR)
            scale = 1.0 / np.sqrt(DH).astype(np.float32)
            scores = jnp.einsum('bhqd,bhkd->bhqk', q, k) * scale
            _, indices = jax.lax.top_k(scores, min(TOPK, s))
            attn = jax.nn.softmax(scores, axis=-1)
            out = jnp.einsum('bhqk,bhkd->bhqd', attn, v)
            out = out.transpose(0, 2, 1, 3).reshape(b, s, H * DH)
            out = out @ w_out.T + residual
            return (out, indices.astype(jnp.int64))
        key = jax.random.key(seed)
        ks = jax.random.split(key, 7)
        init = lambda k, shape: jax.random.normal(k, shape, jnp.float32) * 0.02
        return {'x': jax.random.normal(ks[0], (B, S, D), jnp.float32), 'w_down_q': init(ks[1], (DQL, D)), 'w_down_kv': init(ks[2], (DKVL, D)), 'w_up_q': init(ks[3], (H * DH, DQL)), 'w_up_k': init(ks[4], (H * DH, DKVL)), 'w_up_v': init(ks[5], (H * DH, DKVL)), 'w_out': init(ks[6], (D, H * DH)), 'ln_scale': jnp.ones((D,), jnp.float32), 'ln_bias': jnp.zeros((D,), jnp.float32)}
    _L1_attn_in = _L1_attn_setup()

    def _L1_ffn_setup():
        import jax, jax.numpy as jnp
        import numpy as np
        from jax import lax
        DIM = 128
        INTER = 64
        N_EXPERTS = 16
        TOPK = 4
        ROUTE_SCALE = 2.5
        VOCAB = 4000

        def _silu_and_mul(gu):
            gate, up = jnp.split(gu, 2, axis=-1)
            return jax.nn.silu(gate) * up
        key = jax.random.key(seed)
        ks = jax.random.split(key, 8)
        x = jax.random.normal(ks[0], (2, 64, DIM), dtype=jnp.float32)
        input_ids = jax.random.randint(ks[1], (2, 64), 0, VOCAB)
        s = 0.02
        gate_w = jax.random.normal(ks[2], (N_EXPERTS, DIM), dtype=jnp.float32) * s
        gate_b = jax.random.normal(ks[3], (N_EXPERTS,), dtype=jnp.float32) * s
        w13 = jax.random.normal(ks[4], (N_EXPERTS, 2 * INTER, DIM), dtype=jnp.float32) * s
        w2 = jax.random.normal(ks[5], (N_EXPERTS, DIM, INTER), dtype=jnp.float32) * s
        w13_s = jax.random.normal(ks[6], (2 * INTER, DIM), dtype=jnp.float32) * s
        w2_s = jax.random.normal(ks[7], (DIM, INTER), dtype=jnp.float32) * s
        return {'x': x, 'input_ids': input_ids, 'gate_w': gate_w, 'gate_b': gate_b, 'w13': w13, 'w2': w2, 'w13_s': w13_s, 'w2_s': w2_s}
    _L1_ffn_in = _L1_ffn_setup()
    _d = {'L0_attn_x': _L0_attn_in['x'], 'L0_attn_in_proj_w': _L0_attn_in['in_proj_w'], 'L0_attn_conv_w': _L0_attn_in['conv_w'], 'L0_attn_conv_b': _L0_attn_in['conv_b'], 'L0_attn_dt_bias': _L0_attn_in['dt_bias'], 'L0_attn_A_log': _L0_attn_in['A_log'], 'L0_attn_D': _L0_attn_in['D'], 'L0_attn_norm_w': _L0_attn_in['norm_w'], 'L0_attn_out_proj_w': _L0_attn_in['out_proj_w'], 'L0_attn_ln_w': _L0_attn_in['ln_w'], 'L0_attn_ln_b': _L0_attn_in['ln_b'], 'L0_ffn_wqkv': _L0_ffn_in['wqkv'], 'L0_ffn_q_scale': _L0_ffn_in['q_scale'], 'L0_ffn_k_scale': _L0_ffn_in['k_scale'], 'L0_ffn_wo': _L0_ffn_in['wo'], 'L0_ffn_ln_g': _L0_ffn_in['ln_g'], 'L0_ffn_ln_b': _L0_ffn_in['ln_b'], 'L0_ffn_w1': _L0_ffn_in['w1'], 'L0_ffn_b1': _L0_ffn_in['b1'], 'L0_ffn_w2': _L0_ffn_in['w2'], 'L0_ffn_b2': _L0_ffn_in['b2'], 'L1_attn_w_down_q': _L1_attn_in['w_down_q'], 'L1_attn_w_down_kv': _L1_attn_in['w_down_kv'], 'L1_attn_w_up_q': _L1_attn_in['w_up_q'], 'L1_attn_w_up_k': _L1_attn_in['w_up_k'], 'L1_attn_w_up_v': _L1_attn_in['w_up_v'], 'L1_attn_w_out': _L1_attn_in['w_out'], 'L1_attn_ln_scale': _L1_attn_in['ln_scale'], 'L1_attn_ln_bias': _L1_attn_in['ln_bias'], 'L1_ffn_input_ids': _L1_ffn_in['input_ids'], 'L1_ffn_gate_w': _L1_ffn_in['gate_w'], 'L1_ffn_gate_b': _L1_ffn_in['gate_b'], 'L1_ffn_w13': _L1_ffn_in['w13'], 'L1_ffn_w2': _L1_ffn_in['w2'], 'L1_ffn_w13_s': _L1_ffn_in['w13_s'], 'L1_ffn_w2_s': _L1_ffn_in['w2_s']}
    _x0 = _d['L0_attn_x']
    _d['L0_attn_x'] = jax.random.normal(jax.random.fold_in(jax.random.key(seed), 1), (1, 2048, 128), dtype=_x0.dtype)
    del _x0
    return _d

def reference(L0_attn_x, L0_attn_in_proj_w, L0_attn_conv_w, L0_attn_conv_b, L0_attn_dt_bias, L0_attn_A_log, L0_attn_D, L0_attn_norm_w, L0_attn_out_proj_w, L0_attn_ln_w, L0_attn_ln_b, L0_ffn_wqkv, L0_ffn_q_scale, L0_ffn_k_scale, L0_ffn_wo, L0_ffn_ln_g, L0_ffn_ln_b, L0_ffn_w1, L0_ffn_b1, L0_ffn_w2, L0_ffn_b2, L1_attn_w_down_q, L1_attn_w_down_kv, L1_attn_w_up_q, L1_attn_w_up_k, L1_attn_w_up_v, L1_attn_w_out, L1_attn_ln_scale, L1_attn_ln_bias, L1_ffn_input_ids, L1_ffn_gate_w, L1_ffn_gate_b, L1_ffn_w13, L1_ffn_w2, L1_ffn_w13_s, L1_ffn_w2_s):

    def _L0_attn_ref(x, in_proj_w, conv_w, conv_b, dt_bias, A_log, D, norm_w, out_proj_w, ln_w, ln_b):
        import jax, jax.numpy as jnp
        import numpy as np
        from jax import lax
        D_MODEL = 128
        D_STATE = 128
        D_CONV = 4
        EXPAND = 2
        HEADDIM = 64
        D_INNER = EXPAND * D_MODEL
        NHEADS = D_INNER // HEADDIM
        CONV_DIM = D_INNER + 2 * D_STATE
        D_IN_PROJ = 2 * D_INNER + 2 * D_STATE + NHEADS
        B_SZ, L_SEQ = (4, 256)
        EPS = 1e-05

        def _mamba_block(x, in_proj_w, conv_w, conv_b, dt_bias, A_log, D, norm_w, out_proj_w, ln_w, ln_b):
            b, l, _ = x.shape
            zxbcdt = jnp.einsum('bld,ed->ble', x, in_proj_w)
            z = zxbcdt[..., :D_INNER]
            xBC = zxbcdt[..., D_INNER:D_INNER + CONV_DIM]
            dt = jax.nn.softplus(zxbcdt[..., D_INNER + CONV_DIM:] + dt_bias)
            xBC_t = xBC.transpose(0, 2, 1)
            conv = lax.conv_general_dilated(xBC_t, conv_w[:, None, :], (1,), [(D_CONV - 1, 0)], feature_group_count=CONV_DIM, dimension_numbers=('NCW', 'OIW', 'NCW'))
            xBC = jax.nn.silu(conv + conv_b[:, None]).transpose(0, 2, 1)
            x_ssm = xBC[..., :D_INNER].reshape(b, l, NHEADS, HEADDIM)
            Bm = xBC[..., D_INNER:D_INNER + D_STATE]
            Cm = xBC[..., D_INNER + D_STATE:]
            A = -jnp.exp(A_log)
            dA = jnp.exp(dt * A)

            def step(h, inp):
                dA_t, x_t, B_t, C_t, dt_t = inp
                dBx = dt_t[:, :, None, None] * x_t[..., None] * B_t[:, None, None, :]
                h = h * dA_t[:, :, None, None] + dBx
                y = jnp.einsum('bhpn,bn->bhp', h, C_t)
                return (h, y)
            h0 = jnp.zeros((b, NHEADS, HEADDIM, D_STATE), dtype=x.dtype)
            inputs = (dA.transpose(1, 0, 2), x_ssm.transpose(1, 0, 2, 3), Bm.transpose(1, 0, 2), Cm.transpose(1, 0, 2), dt.transpose(1, 0, 2))
            _, ys = lax.scan(step, h0, inputs)
            y = ys.transpose(1, 0, 2, 3) + D[None, None, :, None] * x_ssm
            y = y.reshape(b, l, D_INNER)
            y = y * jax.nn.silu(z)
            y = y * lax.rsqrt(jnp.mean(y * y, axis=-1, keepdims=True) + EPS) * norm_w
            y = jnp.einsum('bld,ed->ble', y, out_proj_w) + x
            mu = jnp.mean(y, axis=-1, keepdims=True)
            var = jnp.mean((y - mu) ** 2, axis=-1, keepdims=True)
            return (y - mu) * lax.rsqrt(var + EPS) * ln_w + ln_b
        return _mamba_block(x, in_proj_w, conv_w, conv_b, dt_bias, A_log, D, norm_w, out_proj_w, ln_w, ln_b)

    def _L0_ffn_ref(x, wqkv, q_scale, k_scale, wo, ln_g, ln_b, w1, b1, w2, b2):
        import jax, jax.numpy as jnp
        import numpy as np
        DIM = 128
        DEPTH = 2
        HEADS = 8
        DIM_HEAD = 64
        WINDOW = 64
        INNER = HEADS * DIM_HEAD
        HID = int(DIM * 4 * 2 / 3)
        B, N = (2, 1024)
        QK_SCALE = 8.0

        def shift_token(t):
            t1, t2 = jnp.split(t, 2, axis=-1)
            t2 = jnp.pad(t2, ((0, 0), (1, 0), (0, 0)))[:, :-1]
            return jnp.concatenate([t1, t2], axis=-1)

        def l2norm(t):
            return t / jnp.clip(jnp.linalg.norm(t, axis=-1, keepdims=True), 1e-12)

        def rotate_half(x):
            x1, x2 = jnp.split(x, 2, axis=-1)
            return jnp.concatenate([-x2, x1], axis=-1)

        def rotary_xpos(q, k):
            n = q.shape[-2]
            half_idx = jnp.arange(0, DIM_HEAD, 2, dtype=jnp.float32)
            inv_freq = 1.0 / 10000.0 ** (half_idx / DIM_HEAD)
            t = jnp.arange(n, dtype=jnp.float32)
            freqs = t[:, None] * inv_freq[None, :]
            freqs = jnp.concatenate([freqs, freqs], axis=-1)
            base = (half_idx + 0.4 * DIM_HEAD) / (1.4 * DIM_HEAD)
            power = (t - n // 2) / float(WINDOW // 2)
            scale = base[None, :] ** power[:, None]
            scale = jnp.concatenate([scale, scale], axis=-1)
            cos, sin = (jnp.cos(freqs), jnp.sin(freqs))
            q = q * cos * scale + rotate_half(q) * sin * scale
            k = k * cos / scale + rotate_half(k) * sin / scale
            return (q, k)

        def local_attention(q, k, v):
            b, h, n, d = q.shape
            w = n // WINDOW
            bq = q.reshape(b, h, w, WINDOW, d) * QK_SCALE
            bk = k.reshape(b, h, w, WINDOW, d)
            bv = v.reshape(b, h, w, WINDOW, d)

            def look_around(t):
                p = jnp.pad(t, ((0, 0), (0, 0), (1, 0), (0, 0), (0, 0)))
                return jnp.concatenate([p[:, :, :w], p[:, :, 1:]], axis=3)
            bk, bv = (look_around(bk), look_around(bv))
            bt = jnp.arange(n).reshape(w, WINDOW)
            btp = jnp.pad(bt, ((1, 0), (0, 0)), constant_values=-1)
            btk = jnp.concatenate([btp[:w], btp[1:]], axis=1)
            sim = jnp.einsum('bhwid,bhwjd->bhwij', bq, bk)
            i = bt[:, :, None]
            j = btk[:, None, :]
            mask = (i < j) | (i > j + WINDOW) | (j == -1)
            sim = jnp.where(mask, -jnp.finfo(sim.dtype).max, sim)
            attn = jax.nn.softmax(sim, axis=-1)
            out = jnp.einsum('bhwij,bhwjd->bhwid', attn, bv)
            return out.reshape(b, h, n, d)

        def _layer(x, wqkv, qs, ksc, wo, lg, lb, w1, b1, w2, b2):
            b, n, _ = x.shape
            h = shift_token(x)
            qkv = h @ wqkv
            q, k, v = jnp.split(qkv, 3, axis=-1)
            to_heads = lambda t: t.reshape(b, n, HEADS, DIM_HEAD).transpose(0, 2, 1, 3)
            q, k, v = (to_heads(q), to_heads(k), to_heads(v))
            q = l2norm(q) * qs
            k = l2norm(k) * ksc
            q, k = rotary_xpos(q, k)
            o = local_attention(q, k, v)
            o = o.transpose(0, 2, 1, 3).reshape(b, n, INNER)
            x = x + o @ wo
            h = shift_token(x)
            mu = h.mean(-1, keepdims=True)
            var = h.var(-1, keepdims=True)
            h = (h - mu) / jnp.sqrt(var + 1e-05) * lg + lb
            h = h @ w1 + b1
            a, g = jnp.split(h, 2, axis=-1)
            h = a * jax.nn.gelu(g, approximate=False)
            x = x + h @ w2 + b2
            return x
        for l in range(DEPTH):
            x = _layer(x, wqkv[l], q_scale[l], k_scale[l], wo[l], ln_g[l], ln_b[l], w1[l], b1[l], w2[l], b2[l])
        return x

    def _L1_attn_ref(x, w_down_q, w_down_kv, w_up_q, w_up_k, w_up_v, w_out, ln_scale, ln_bias):
        import jax, jax.numpy as jnp
        import numpy as np
        B, S, D = (2, 256, 128)
        H, DH = (16, 64)
        DQL, DKVL = (64, 64)
        DR = 64
        TOPK = 64
        LN_EPS = 1e-05
        ROPE_BASE = 10000.0

        def _rope_tables(seq_len, dim):
            inv_freq = 1.0 / ROPE_BASE ** (np.arange(0, dim, 2, dtype=np.float32) / dim)
            t = np.arange(seq_len, dtype=np.float32)
            freqs = np.outer(t, inv_freq)
            cos = np.concatenate([np.cos(freqs), np.cos(freqs)], -1)[:, ::2]
            sin = np.concatenate([np.sin(freqs), np.sin(freqs)], -1)[:, ::2]
            return (jnp.asarray(cos), jnp.asarray(sin))

        def _apply_rope_subspace(x, d_rope):
            s = x.shape[-2]
            cos, sin = _rope_tables(s, d_rope)
            xr, xp = (x[..., :d_rope], x[..., d_rope:])
            e, o = (xr[..., 0::2], xr[..., 1::2])
            rot = jnp.stack([e * cos - o * sin, e * sin + o * cos], axis=-1).reshape(xr.shape)
            return jnp.concatenate([rot, xp], axis=-1)

        def _reference_tuple_inner(x, w_down_q, w_down_kv, w_up_q, w_up_k, w_up_v, w_out, ln_scale, ln_bias):
            b, s, d = x.shape
            residual = x
            mu = jnp.mean(x, axis=-1, keepdims=True)
            var = jnp.mean((x - mu) ** 2, axis=-1, keepdims=True)
            h = (x - mu) * jax.lax.rsqrt(var + LN_EPS) * ln_scale + ln_bias
            c_q = h @ w_down_q.T
            c_kv = h @ w_down_kv.T
            q = (c_q @ w_up_q.T).reshape(b, s, H, DH).transpose(0, 2, 1, 3)
            k = (c_kv @ w_up_k.T).reshape(b, s, H, DH).transpose(0, 2, 1, 3)
            v = (c_kv @ w_up_v.T).reshape(b, s, H, DH).transpose(0, 2, 1, 3)
            q = _apply_rope_subspace(q, DR)
            k = _apply_rope_subspace(k, DR)
            scale = 1.0 / np.sqrt(DH).astype(np.float32)
            scores = jnp.einsum('bhqd,bhkd->bhqk', q, k) * scale
            _, indices = jax.lax.top_k(scores, min(TOPK, s))
            attn = jax.nn.softmax(scores, axis=-1)
            out = jnp.einsum('bhqk,bhkd->bhqd', attn, v)
            out = out.transpose(0, 2, 1, 3).reshape(b, s, H * DH)
            out = out @ w_out.T + residual
            return (out, indices.astype(jnp.int64))
        return _reference_tuple_inner(x, w_down_q, w_down_kv, w_up_q, w_up_k, w_up_v, w_out, ln_scale, ln_bias)[0]

    def _L1_ffn_ref(x, input_ids, gate_w, gate_b, w13, w2, w13_s, w2_s):
        import jax, jax.numpy as jnp
        import numpy as np
        from jax import lax
        DIM = 128
        INTER = 64
        N_EXPERTS = 16
        TOPK = 4
        ROUTE_SCALE = 2.5
        VOCAB = 4000

        def _silu_and_mul(gu):
            gate, up = jnp.split(gu, 2, axis=-1)
            return jax.nn.silu(gate) * up
        B, S, D = x.shape
        xt = x.reshape(-1, D)
        T = xt.shape[0]
        scores = jax.nn.sigmoid(xt.astype(jnp.float32) @ gate_w.T)
        biased = scores + gate_b
        _, idx = lax.top_k(biased, TOPK)
        w = jnp.take_along_axis(scores, idx, axis=-1)
        w = w / jnp.sum(w, axis=-1, keepdims=True)
        w = w * ROUTE_SCALE
        comb = jnp.zeros((T, N_EXPERTS), jnp.float32)
        comb = comb.at[jnp.arange(T)[:, None], idx].add(w)
        comb = comb.astype(x.dtype)

        def expert_body(y, args):
            w13_e, w2_e, c_e = args
            h = _silu_and_mul(xt @ w13_e.T)
            return (y + c_e[:, None] * (h @ w2_e.T), None)
        y, _ = lax.scan(expert_body, jnp.zeros_like(xt), (w13, w2, comb.T))
        y = y + _silu_and_mul(xt @ w13_s.T) @ w2_s.T
        return y.astype(x.dtype).reshape(B, S, D)
    x = L0_attn_x
    x = _layernorm(x + _L0_attn_ref(x, L0_attn_in_proj_w, L0_attn_conv_w, L0_attn_conv_b, L0_attn_dt_bias, L0_attn_A_log, L0_attn_D, L0_attn_norm_w, L0_attn_out_proj_w, L0_attn_ln_w, L0_attn_ln_b), axis=-1)
    x = _layernorm(x + _L0_ffn_ref(x, L0_ffn_wqkv, L0_ffn_q_scale, L0_ffn_k_scale, L0_ffn_wo, L0_ffn_ln_g, L0_ffn_ln_b, L0_ffn_w1, L0_ffn_b1, L0_ffn_w2, L0_ffn_b2), axis=-1)
    x = _layernorm(x + _L1_attn_ref(x, L1_attn_w_down_q, L1_attn_w_down_kv, L1_attn_w_up_q, L1_attn_w_up_k, L1_attn_w_up_v, L1_attn_w_out, L1_attn_ln_scale, L1_attn_ln_bias), axis=-1)
    x = _layernorm(x + _L1_ffn_ref(x, L1_ffn_input_ids, L1_ffn_gate_w, L1_ffn_gate_b, L1_ffn_w13, L1_ffn_w2, L1_ffn_w13_s, L1_ffn_w2_s), axis=-1)
    return x

_drawn_inputs = setup_inputs


def setup_inputs(seed=0):
    import zlib

    import numpy as np

    out = dict(_drawn_inputs(seed))
    spreads = {'L0_attn_norm_w': (1.0, 0.585),
     'L0_attn_ln_w': (1.0, 0.2),
     'L0_attn_ln_b': (0.0, 0.1),
     'L0_ffn_q_scale': (1.0, 0.6),
     'L0_ffn_k_scale': (1.0, 0.6),
     'L0_ffn_ln_g': (1.0, 0.6),
     'L0_ffn_ln_b': (0.0, 0.8),
     'L0_ffn_b1': (0.0, 0.8),
     'L0_ffn_b2': (0.0, 0.1),
     'L1_attn_ln_scale': (1.0, 0.6),
     'L1_attn_ln_bias': (0.0, 0.8)}
    factors = {'L0_attn_dt_bias': 8.0,
     'L0_attn_A_log': 8.0,
     'L0_attn_D': 4.779,
     'L0_ffn_wqkv': 3.967,
     'L0_ffn_wo': 4.011,
     'L0_ffn_w1': 6.215,
     'L0_ffn_w2': 6.123,
     'L1_attn_w_down_q': 8.0,
     'L1_attn_w_down_kv': 8.0,
     'L1_attn_w_up_q': 8.0,
     'L1_attn_w_up_k': 8.0,
     'L1_attn_w_up_v': 8.0,
     'L1_attn_w_out': 8.0,
     'L1_ffn_gate_w': 8.0,
     'L1_ffn_gate_b': 8.0,
     'L1_ffn_w13': 8.0,
     'L1_ffn_w2': 8.0,
     'L1_ffn_w13_s': 8.0,
     'L1_ffn_w2_s': 8.0}
    for name, (base, spread) in spreads.items():
        noise = np.random.default_rng([zlib.crc32(name.encode()), seed]).standard_normal(out[name].shape)
        drawn = base * np.exp(spread * noise) if base else spread * noise
        out[name] = jnp.asarray(drawn.astype(out[name].dtype))
    for name, factor in factors.items():
        out[name] = (out[name] * factor).astype(out[name].dtype)
    return out
```

```python
import concourse.bass as bass
from concourse import mybir
from concourse.alu_op_type import AluOpType as ALU
from contextlib import ExitStack
import numpy as np

F32 = mybir.dt.float32
F32R = mybir.dt.float32r
BF16 = mybir.dt.bfloat16
ACT = mybir.ActivationFunctionType
AX = mybir.AxisListType

P = 128
D = 128
S = 2048
T = S // P
CH = 512
NC = S // CH
EPS = 1e-5


class Chain:

    def __init__(self, eng, sem):
        self.eng, self.sem, self.n = eng, sem, 0

    def __call__(self, ins):
        self.n += 1
        ins.then_inc(self.sem, 1)
        self.eng.wait_ge(self.sem, self.n)


class Space:

    used = []

    def __init__(self, nc, name):
        self.nc, self.name, self.stack = nc, name, ExitStack()

    def __enter__(self):
        self.stack.__enter__()
        return self

    def __exit__(self, *e):
        return self.stack.__exit__(*e)

    def sb(self, name, shape, dt=F32):
        return self.stack.enter_context(self.nc.sbuf_tensor(f"{self.name}.{name}", shape, dt))

    def ps(self, name, shape, dt=F32):
        return self.stack.enter_context(self.nc.psum_tensor(f"{self.name}_{name}", shape, dt))

    def sem(self, name):
        holder = self.nc.semaphore(f"{self.name}_{name}")
        sem = holder.__enter__()
        Space.used.append((holder, sem))
        return sem


def clear_semaphores(nc):
    with nc.Block() as block:

        @block.gpsimd
        def _(pool):
            for _, sem in Space.used:
                pool.sem_clear(sem)

    while Space.used:
        Space.used.pop()[0].__exit__(None, None, None)


def normalise(nc, name, src, dst, scale=None, shift=None, residual=None):
    with Space(nc, name) as sp:
        stats = sp.sb("stats", [P, T, 6])
        moments = sp.sb("moments", [P, T, 2])
        spread = sp.sb("spread", [P, T])
        eps = sp.sb("eps", [P, 1])
        order, var_ready, std_ready = sp.sem("order"), sp.sem("var"), sp.sem("std")
        scaled, eps_ready = sp.sem("scaled"), sp.sem("eps_ready")
        with nc.Block() as block:

            @block.vector
            def _(dve):
                nc.vector.memset(eps[:], EPS).then_inc(eps_ready, 1)
                for t in range(T):
                    nc.vector.bn_stats(stats[:, t], src[:, t]).then_inc(order, 1)
                for t in range(T):
                    dve.wait_ge(order, t + 1)
                    ins = nc.vector.bn_aggr(moments[:, t], stats[:, t])
                ins.then_inc(var_ready, 1)
                dve.wait_ge(std_ready, 1)
                link = Chain(dve, order)
                link.n = T
                link(nc.vector.reciprocal(spread[:], spread[:]))
                dve.wait_ge(var_ready, 1)
                for t in range(T):
                    nc.vector.tensor_scalar(dst[:, t], src[:, t], moments[:, t, 0:1], spread[:, t:t + 1],
                                            ALU.subtract, ALU.mult).then_inc(scaled, 1)
                if scale is not None:
                    dve.wait_ge(scaled, T)
                    link(nc.vector.tensor_tensor(dst[:], dst[:], scale.unsqueeze(1).broadcast_to([P, T, D]),
                                                 ALU.mult))
                    link(nc.vector.tensor_tensor(dst[:], dst[:], shift.unsqueeze(1).broadcast_to([P, T, D]),
                                                 ALU.add))
                if residual is not None:
                    dve.wait_ge(scaled, T)
                    nc.vector.tensor_tensor(dst[:], dst[:], residual[:], ALU.add)

            @block.scalar
            def _(act):
                act.wait_ge(eps_ready, 1)
                act.wait_ge(var_ready, 1)
                nc.scalar.activation(spread[:], moments[:, :, 1], ACT.Sqrt,
                                     bias=eps[:, 0:1]).then_inc(std_ready, 1)



HEADS_S, HEAD_S, STATE = 4, 64, 128
INNER = HEADS_S * HEAD_S
TAPS = 4


def state_space(nc, dram, const, x_tok, out_tok):
    ident, upto, after, ones = const["ident"], const["upto"], const["after"], const["ones"]
    HP = HEADS_S * P
    with Space(nc, "ss") as sp:
        w_xbc = sp.sb("w_xbc", [P, 4 * P])
        w_zdt = sp.sb("w_zdt", [P, INNER + HEADS_S])
        conv_w = sp.sb("conv_w", [P, 4, TAPS])
        conv_b = sp.sb("conv_b", [P, 4])
        rows = sp.sb("rows", [P, 3 * HEADS_S + 2 * D])
        norm_w = sp.sb("norm_w", [P, 2])
        w_out = sp.sb("w_out", [P, 2, D])
        xbc = sp.sb("xbc", [P, 4, S])
        gate = sp.sb("gate", [P, T, INNER])
        dt = sp.sb("dt", [P, T, HEADS_S])
        decay = sp.sb("decay", [P, T, HEADS_S])
        w_loaded = sp.sem("w_loaded")
        dt_bias, a_log, skip = rows[:, 0:4], rows[:, 4:8], rows[:, 8:12]
        ln_w, ln_b = rows[:, 12:12 + D], rows[:, 12 + D:12 + 2 * D]

        with Space(nc, "ssa") as sa:
            xT = sa.sb("xT", [P, S])
            raw = sa.sb("raw", [P, 2, TAPS - 1 + S])
            turned = sa.ps("turned", [P, 2, CH])
            proj = sa.ps("proj", [P, 4, CH])
            zdt = sa.ps("zdt", [P, 2, CH])
            turn_done, xT_ready, pads = sa.sem("turn_done"), sa.sem("xT_ready"), sa.sem("pads")
            proj_done, raw_ready, conv_done = sa.sem("proj_done"), sa.sem("raw_ready"), sa.sem("conv_done")
            zdt_done, z_read, order = sa.sem("zdt_done"), sa.sem("z_read"), sa.sem("order")
            with nc.Block() as block:

                @block.sync
                def _(sync):
                    for dst, src in ((w_xbc, "w_xbc"), (w_zdt, "w_zdt"), (conv_w, "conv_w"), (conv_b, "conv_b"),
                                     (rows, "ss_rows"), (norm_w, "norm_w"), (w_out, "w_out_s")):
                        sync.dma_start(dst[:], dram[src]).then_inc(w_loaded, 16)

                @block.gpsimd
                def _(pool):
                    nc.gpsimd.memset(raw[:, :, 0:TAPS - 1], 0.0).then_inc(pads, 1)

                @block.tensor
                def _(pe):
                    pe.wait_ge(const["x_loaded"], 16)
                    pe.wait_ge(const["loaded"], const["count"])
                    for g in range(NC):
                        if g >= 2:
                            pe.wait_ge(xT_ready, g - 1)
                        for k in range(4):
                            ins = nc.tensor.transpose(turned[:, g % 2, k * P:(k + 1) * P], x_tok[:, 4 * g + k],
                                                      ident[:])
                        ins.then_inc(turn_done, 1)
                    pe.wait_ge(w_loaded, 7 * 16)
                    for ct in range(4):
                        for c in range(NC):
                            n = ct * NC + c
                            pe.wait_ge(xT_ready, c + 1)
                            if n >= 4:
                                pe.wait_ge(raw_ready, n - 3)
                            nc.tensor.matmul(proj[:, n % 4], w_xbc[:, ct * P:(ct + 1) * P],
                                             xT[:, c * CH:(c + 1) * CH], start=True, stop=True).then_inc(proj_done, 1)
                    for t in range(T):
                        if t >= 2:
                            pe.wait_ge(z_read, t - 1)
                        nc.tensor.matmul(zdt[:, t % 2, 0:INNER + HEADS_S], xT[:, t * P:(t + 1) * P], w_zdt[:],
                                         start=True, stop=True).then_inc(zdt_done, 1)

                @block.scalar
                def _(act):
                    for g in range(NC):
                        act.wait_ge(turn_done, g + 1)
                        nc.scalar.activation(xT[:, g * CH:(g + 1) * CH], turned[:, g % 2], ACT.Copy)\
                            .then_inc(xT_ready, 1)

                    def silu(ct):
                        act.wait_ge(conv_done, ct + 1)
                        nc.scalar.activation(xbc[:, ct], xbc[:, ct], ACT.Silu, bias=conv_b[:, ct:ct + 1])

                    for ct in range(4):
                        if ct >= 2:
                            act.wait_ge(conv_done, ct - 1)
                        for c in range(NC):
                            n = ct * NC + c
                            act.wait_ge(proj_done, n + 1)
                            nc.scalar.activation(raw[:, ct % 2, TAPS - 1 + c * CH:TAPS - 1 + (c + 1) * CH],
                                                 proj[:, n % 4], ACT.Copy).then_inc(raw_ready, 1)
                        if ct:
                            silu(ct - 1)
                    silu(3)
                    for t in range(T):
                        act.wait_ge(zdt_done, t + 1)
                        nc.scalar.activation(dt[:, t], zdt[:, t % 2, INNER:INNER + HEADS_S], ACT.Copy)
                        nc.scalar.activation(gate[:, t], zdt[:, t % 2, 0:INNER], ACT.Silu).then_inc(z_read, 1)

                @block.vector
                def _(dve):
                    link = Chain(dve, order)
                    dve.wait_ge(pads, 1)
                    dve.wait_ge(w_loaded, 7 * 16)
                    for ct in range(4):
                        dve.wait_ge(raw_ready, NC * (ct + 1))
                        link(nc.vector.tensor_scalar(xbc[:, ct], raw[:, ct % 2, 0:S], conv_w[:, ct, 0:1], None,
                                                     ALU.mult))
                        for k in range(1, TAPS):
                            ins = nc.vector.scalar_tensor_tensor(out=xbc[:, ct], in0=raw[:, ct % 2, k:k + S],
                                                                 scalar=conv_w[:, ct, k:k + 1], in1=xbc[:, ct],
                                                                 op0=ALU.mult, op1=ALU.add)
                            if k < TAPS - 1:
                                link(ins)
                        ins.then_inc(conv_done, 1)

        DECAY_MIN = -200.0
        HT = T * HEADS_S
        grow = sp.sb("grow", [P, 3, HT])
        dt_after = sp.sb("dt_after", [P, T, HEADS_S])
        with Space(nc, "ssb") as sb_:
            size = sb_.sb("size", [P, T, HEADS_S])
            top = sb_.sb("top", [P, T, HEADS_S])
            a_exp = sb_.sb("a_exp", [P, HEADS_S])
            e = sb_.sb("e", [P, T, HEADS_S])
            u = sb_.sb("u", [P, T, HEADS_S])
            lu = sb_.sb("lu", [P, T, HEADS_S])
            sums = sb_.ps("sums", [P, CH])
            d_v, d_a, order, sums_done, grown = (sb_.sem("d_v"), sb_.sem("d_a"), sb_.sem("order"),
                                                 sb_.sem("sums_done"), sb_.sem("grown"))
            with nc.Block() as block:

                @block.vector
                def _(dve):
                    link = Chain(dve, order)
                    link(nc.vector.tensor_tensor(dt[:], dt[:], dt_bias.unsqueeze(1).broadcast_to([P, T, HEADS_S]),
                                                 ALU.add))
                    link(nc.vector.scalar_tensor_tensor(out=size[:], in0=dt[:], scalar=-1.0, in1=dt[:], op0=ALU.mult,
                                                        op1=ALU.max))
                    nc.vector.tensor_scalar(top[:], dt[:], 0.0, None, ALU.max).then_inc(d_v, 1)
                    dve.wait_ge(d_a, 2)
                    link(nc.vector.tensor_scalar(u[:], e[:], 1.0, None, ALU.add))
                    nc.vector.scalar_tensor_tensor(out=e[:], in0=u[:], scalar=-1.0, in1=e[:], op0=ALU.add,
                                                   op1=ALU.subtract).then_inc(d_v, 1)
                    dve.wait_ge(d_a, 3)
                    dve.wait_ge(d_v, 2)
                    link(nc.vector.tensor_tensor(lu[:], lu[:], e[:], ALU.subtract))
                    link(nc.vector.tensor_tensor(dt[:], top[:], lu[:], ALU.add))
                    link(nc.vector.tensor_tensor(decay[:], dt[:],
                                                 a_exp[:].unsqueeze(1).broadcast_to([P, T, HEADS_S]), ALU.mult))
                    nc.vector.tensor_scalar(decay[:], decay[:], -1.0, DECAY_MIN, ALU.mult, ALU.max).then_inc(d_v, 1)
                    dve.wait_ge(grown, 1)
                    nc.vector.tensor_tensor(dt_after[:], dt[:], grow[:, 1].rearrange("p (t h) -> p t h", h=HEADS_S),
                                            ALU.mult)
                    for k in range(2):
                        nc.vector.tensor_scalar(w_out[:, k], w_out[:, k], norm_w[:, k:k + 1], None, ALU.mult)

                @block.scalar
                def _(act):
                    nc.scalar.activation(a_exp[:], a_log, ACT.Exp).then_inc(d_a, 1)
                    act.wait_ge(d_v, 1)
                    nc.scalar.activation(e[:], size[:], ACT.Exp, scale=-1.0).then_inc(d_a, 1)
                    act.wait_ge(d_v, 2)
                    nc.scalar.activation(lu[:], u[:], ACT.Ln).then_inc(d_a, 1)
                    act.wait_ge(sums_done, 1)
                    nc.scalar.activation(grow[:], sums[:, 0:3 * HT].rearrange("p (k n) -> p k n", k=3), ACT.Exp)\
                        .then_inc(grown, 1)

                @block.tensor
                def _(pe):
                    pe.wait_ge(d_v, 3)
                    flat = decay[:].rearrange("p t h -> p (t h)")
                    for k, mask in enumerate((upto, after, ones)):
                        ins = nc.tensor.matmul(sums[:, k * HT:(k + 1) * HT], mask[:], flat, start=True, stop=True)
                    ins.then_inc(sums_done, 1)

        grow_upto = grow[:, 0].rearrange("p (t h) -> p t h", h=HEADS_S)
        grow_all = grow[:, 2].rearrange("p (t h) -> p t h", h=HEADS_S)

        def per_head(ap, width=HEAD_S):
            return ap.unsqueeze(2).broadcast_to([P, HEADS_S, width])

        with Space(nc, "ssc") as sc:
            xb = sc.sb("xb", [P, 2, 3 * P])
            steps = sc.sb("steps", [P, 2, HP])
            fade = sc.sb("fade", [P, 2, HP])
            gram = sc.sb("gram", [P, 2, P])
            mix = sc.sb("mix", [P, 2, HP])
            x_dt = sc.sb("x_dt", [P, 2, INNER])
            x_st = sc.sb("x_st", [P, 2, INNER])
            x_sk = sc.sb("x_sk", [P, 2, INNER])
            state = sc.sb("state", [P, 2, INNER])
            y = sc.sb("y", [P, INNER])
            turned = sc.ps("turned", [P, 2, CH])
            between = sc.ps("between", [P, 2, CH])
            y_ps = sc.ps("y_ps", [P, 2, CH])
            gs_ps = sc.ps("gs_ps", [P, CH])
            st_ps = sc.ps("st_ps", [P, CH])
            names = ["steps_ready", "front", "xb_ready", "fade_ready", "gram_ready", "mix_ready", "x_ready",
                     "y_done", "st_done", "state_ready", "y_read", "dve", "gated"]
            m = {n: sc.sem(n) for n in names}
            h4 = "p (h q) -> p h q"

            with nc.Block() as block:

                @block.tensor
                def _(pe):
                    def front(c):
                        cols = slice(c * P, (c + 1) * P)
                        if c >= 2:
                            pe.wait_ge(m["xb_ready"], c - 1)
                            pe.wait_ge(m["fade_ready"], c - 1)
                        for k in range(3):
                            nc.tensor.transpose(turned[:, c % 2, k * P:(k + 1) * P], xbc[:, k, cols], ident[:])
                        if c >= 1:
                            pe.wait_ge(m["gram_ready"], c)
                        nc.tensor.matmul(gs_ps[:, 0:P], xbc[:, 2, cols], xbc[:, 3, cols], start=True, stop=True)
                        pe.wait_ge(m["steps_ready"], c + 1)
                        nc.tensor.matmul(between[:, c % 2], after[:], steps[:, c % 2], start=True, stop=True)\
                            .then_inc(m["front"], 1)

                    front(0)
                    for c in range(T):
                        if c + 1 < T:
                            front(c + 1)
                        pe.wait_ge(m["mix_ready"], c + 1)
                        pe.wait_ge(m["x_ready"], c + 1)
                        if c >= 2:
                            pe.wait_ge(m["y_read"], c - 1)
                        for h in range(HEADS_S):
                            nc.tensor.matmul(y_ps[:, c % 2, h * HEAD_S:(h + 1) * HEAD_S],
                                             mix[:, c % 2, h * P:(h + 1) * P],
                                             x_dt[:, c % 2, h * HEAD_S:(h + 1) * HEAD_S], start=True, stop=True)
                        pe.wait_ge(m["state_ready"], c + 1)
                        nc.tensor.matmul(y_ps[:, c % 2, INNER:], xbc[:, 3, c * P:(c + 1) * P], state[:, c % 2],
                                         start=True, stop=True).then_inc(m["y_done"], 1)
                        nc.tensor.matmul(st_ps[:, 0:INNER], xb[:, c % 2, INNER:], x_st[:, c % 2],
                                         start=True, stop=True).then_inc(m["st_done"], 1)

                @block.gpsimd
                def _(pool):
                    def steps_of(c):
                        if c >= 2:
                            pool.wait_ge(m["front"], c - 1)
                        nc.gpsimd.tensor_tensor(steps[:, c % 2].rearrange(h4, h=HEADS_S),
                                                upto[:].unsqueeze(1).broadcast_to([P, HEADS_S, P]),
                                                per_head(decay[:, c], P), ALU.mult).then_inc(m["steps_ready"], 1)

                    nc.gpsimd.memset(state[:, 0], 0.0).then_inc(m["state_ready"], 1)
                    steps_of(0)
                    for c in range(T):
                        if c + 1 < T:
                            steps_of(c + 1)
                        pool.wait_ge(m["xb_ready"], c + 1)
                        if c >= 2:
                            pool.wait_ge(m["st_done"], c - 1)
                            pool.wait_ge(m["gated"], c - 1)
                        x = xb[:, c % 2, 0:INNER].rearrange(h4, h=HEADS_S)
                        for dst, by in ((x_dt, dt[:, c]), (x_sk, skip), (x_st, dt_after[:, c])):
                            ins = nc.gpsimd.tensor_tensor(dst[:, c % 2].rearrange(h4, h=HEADS_S), x, per_head(by),
                                                          ALU.mult)
                        ins.then_inc(m["x_ready"], 1)

                @block.scalar
                def _(act):
                    for c in range(T):
                        act.wait_ge(m["front"], c + 1)
                        if c >= 2:
                            act.wait_ge(m["st_done"], c - 1)
                            act.wait_ge(m["x_ready"], c - 1)
                        nc.scalar.activation(xb[:, c % 2], turned[:, c % 2, 0:3 * P], ACT.Copy)\
                            .then_inc(m["xb_ready"], 1)
                        if c >= 2:
                            act.wait_ge(m["mix_ready"], c - 1)
                        nc.scalar.activation(fade[:, c % 2], between[:, c % 2], ACT.Exp).then_inc(m["fade_ready"], 1)

                @block.vector
                def _(dve):
                    link = Chain(dve, m["dve"])
                    for c in range(T):
                        dve.wait_ge(m["front"], c + 1)
                        nc.vector.tensor_tensor(gram[:, c % 2], gs_ps[:, 0:P], upto[:], ALU.mult)\
                            .then_inc(m["gram_ready"], 1)
                        dve.wait_ge(m["gram_ready"], c + 1)
                        dve.wait_ge(m["fade_ready"], c + 1)
                        if c >= 2:
                            dve.wait_ge(m["y_done"], c - 1)
                        nc.vector.tensor_tensor(mix[:, c % 2].rearrange(h4, h=HEADS_S),
                                                fade[:, c % 2].rearrange(h4, h=HEADS_S),
                                                gram[:, c % 2].unsqueeze(1).broadcast_to([P, HEADS_S, P]), ALU.mult)\
                            .then_inc(m["mix_ready"], 1)
                        dve.wait_ge(m["state_ready"], c + 1)
                        nxt = state[:, (c + 1) % 2]
                        if c >= 1:
                            dve.wait_ge(m["y_done"], c)
                        link(nc.vector.tensor_tensor(nxt.rearrange(h4, h=HEADS_S),
                                                     state[:, c % 2].rearrange(h4, h=HEADS_S),
                                                     per_head(grow_all[:, c]), ALU.mult))
                        dve.wait_ge(m["st_done"], c + 1)
                        nc.vector.tensor_tensor(nxt, nxt, st_ps[:, 0:INNER], ALU.add).then_inc(m["state_ready"], 1)
                        dve.wait_ge(m["y_done"], c + 1)
                        dve.wait_ge(m["x_ready"], c + 1)
                        link(nc.vector.tensor_tensor(y[:].rearrange(h4, h=HEADS_S),
                                                     y_ps[:, c % 2, INNER:].rearrange(h4, h=HEADS_S),
                                                     per_head(grow_upto[:, c]), ALU.mult))
                        nc.vector.tensor_tensor(y[:], y[:], y_ps[:, c % 2, 0:INNER], ALU.add).then_inc(m["y_read"], 1)
                        dve.wait_ge(m["y_read"], c + 1)
                        link(nc.vector.tensor_tensor(y[:], y[:], x_sk[:, c % 2], ALU.add))
                        nc.vector.tensor_tensor(gate[:, c], gate[:, c], y[:], ALU.mult).then_inc(m["gated"], 1)

        with Space(nc, "ssd") as sd:
            square = sd.sb("square", [P, INNER])
            total = sd.sb("total", [P, T])
            rms = sd.sb("rms", [P, T])
            yT = sd.sb("yT", [P, 2, INNER])
            eps = sd.sb("eps", [P, 1])
            turned = sd.ps("turned", [P, 2, CH])
            prod = sd.ps("prod", [P, 2, CH])
            m = {n: sd.sem(n) for n in ("turn_done", "yT_ready", "prod_done", "out_ready", "total_ready", "rms_ready",
                                        "order", "eps_ready", "sq")}
            with nc.Block() as block:

                @block.tensor
                def _(pe):
                    def turn(t):
                        if t >= 2:
                            pe.wait_ge(m["yT_ready"], t - 1)
                        for k in range(2):
                            ins = nc.tensor.transpose(turned[:, t % 2, k * P:(k + 1) * P], gate[:, t, k * P:(k + 1) * P],
                                                      ident[:])
                        ins.then_inc(m["turn_done"], 1)

                    turn(0)
                    for t in range(T):
                        if t + 1 < T:
                            turn(t + 1)
                        pe.wait_ge(m["yT_ready"], t + 1)
                        if t >= 2:
                            pe.wait_ge(m["out_ready"], t - 1)
                        for k in range(2):
                            ins = nc.tensor.matmul(prod[:, t % 2, 0:D], yT[:, t % 2, k * P:(k + 1) * P], w_out[:, k],
                                                   start=(k == 0), stop=(k == 1))
                        ins.then_inc(m["prod_done"], 1)

                @block.scalar
                def _(act):
                    for t in range(T):
                        if t:
                            act.wait_ge(m["sq"], t)
                        nc.scalar.activation(square[:], gate[:, t], ACT.Square, accum_out=total[:, t:t + 1])\
                            .then_inc(m["sq"], 1)
                    act.wait_ge(m["sq"], T)
                    act.wait_ge(m["eps_ready"], 1)
                    nc.scalar.activation(rms[:], total[:], ACT.Sqrt, bias=eps[:, 0:1], scale=1.0 / INNER)\
                        .then_inc(m["total_ready"], 1)
                    for t in range(T):
                        act.wait_ge(m["turn_done"], t + 1)
                        if t >= 2:
                            act.wait_ge(m["prod_done"], t - 1)
                        nc.scalar.activation(yT[:, t % 2], turned[:, t % 2, 0:INNER], ACT.Copy)\
                            .then_inc(m["yT_ready"], 1)

                @block.vector
                def _(dve):
                    nc.vector.memset(eps[:], EPS).then_inc(m["eps_ready"], 1)
                    dve.wait_ge(m["total_ready"], 1)
                    nc.vector.reciprocal(rms[:], rms[:]).then_inc(m["rms_ready"], 1)
                    dve.wait_ge(m["rms_ready"], 1)
                    for t in range(T):
                        dve.wait_ge(m["prod_done"], t + 1)
                        nc.vector.scalar_tensor_tensor(out=out_tok[:, t], in0=prod[:, t % 2, 0:D],
                                                       scalar=rms[:, t:t + 1], in1=x_tok[:, t], op0=ALU.mult,
                                                       op1=ALU.add).then_inc(m["out_ready"], 1)

        normalise(nc, "ssn", out_tok, out_tok, ln_w, ln_b, x_tok)
    normalise(nc, "n0", out_tok, out_tok)
    clear_semaphores(nc)



DEPTH = 2
HEADS_L, HEAD_L, WINDOW = 8, 64, 64
INNER_L = HEADS_L * HEAD_L
PAIRS = HEADS_L // 2
KEYS = WINDOW + P
HIDDEN = 341
HID_T = 3
NORM_MIN = 1e-12
MASKED = -1e30


def attention_layer(nc, dram, const, tables, layer, src, dst):
    ident = const["ident"]
    with Space(nc, f"la{layer}") as sp:
        wqkv = sp.sb("wqkv", [P, 3 * INNER_L])
        wrot = sp.sb("wrot", [P, 2 * INNER_L])
        scales = sp.sb("scales", [P, 4])
        wo = sp.sb("wo", [P, PAIRS, D])
        qkT = sp.sb("qkT", [P, 2 * PAIRS, S])
        loaded = sp.sem("loaded")
        with Space(nc, f"lv{layer}") as sv:
            v = sv.sb("v", [P, T, HEADS_L, HEAD_L + 1])
            project_qkv(nc, dram, const, tables, layer, sp, src, wqkv, wrot, scales, wo, qkT, v, loaded)
            attend_local(nc, const, layer, tables["band"], qkT, v)
        with Space(nc, f"lo{layer}") as so:
            prod = so.ps("prod", [P, 2, CH])
            prod_done, added = so.sem("prod_done"), so.sem("added")
            with nc.Block() as block:

                @block.tensor
                def _(pe):
                    for t in range(T):
                        if t >= 2:
                            pe.wait_ge(added, t - 1)
                        for k in range(PAIRS):
                            ins = nc.tensor.matmul(prod[:, t % 2, 0:D], qkT[:, k, t * P:(t + 1) * P], wo[:, k],
                                                   start=(k == 0), stop=(k == PAIRS - 1))
                        ins.then_inc(prod_done, 1)

                @block.vector
                def _(dve):
                    for t in range(T):
                        dve.wait_ge(prod_done, t + 1)
                        nc.vector.tensor_tensor(dst[:, t], prod[:, t % 2, 0:D], src[:, t], ALU.add).then_inc(added, 1)
    feed_forward(nc, dram, const, layer, dst)


def project_qkv(nc, dram, const, tables, layer, sp, src, wqkv, wrot, scales, wo, qkT, v, loaded):
    ident, head_sum, head_copy = const["ident"], tables["head_sum"], tables["head_copy"]
    F = 2 * PAIRS
    N = F * NC
    with Space(nc, f"lp{layer}") as sq_:
        hT = sq_.sb("hT", [P, S + 1])
        square = sq_.sb("square", [P, 2, CH])
        rotated = sq_.sb("rotated", [P, 2, CH])
        turned_by = sq_.sb("turned_by", [P, 2, CH])
        norms = sq_.sb("norms", [64, S])
        parts = sq_.sb("parts", [64, S], F32R)
        unit = sq_.sb("unit", [64, 1])
        with Space(nc, f"lq{layer}") as s:
            turned = s.ps("turned", [P, 1, CH])
            plain = s.ps("plain", [P, 2, CH])
            swapped = s.ps("swapped", [P, 2, CH])
            sums = s.ps("sums", [P, 1, CH])
            v_ps = s.ps("v_ps", [P, 2, CH])
            m = {n: s.sem(n) for n in ("turn_done", "low_ready", "high_ready", "zeroed", "proj_done", "square_ready",
                                       "cos_done", "sin_done", "rot_ready", "sums_done", "norms_ready", "v_done",
                                       "v_read", "ones_set")}
            with nc.Block() as block:

                @block.sync
                def _(sync):
                    for d, n in ((wqkv, f"wqkv{layer}"), (wrot, f"wrot{layer}"), (scales, f"scales{layer}"),
                                 (wo, f"wo{layer}")):
                        sync.dma_start(d[:], dram[n]).then_inc(loaded, 16)

                @block.tensor
                def _(pe):
                    for g in range(NC):
                        if g >= 1:
                            pe.wait_ge(m["low_ready"], g)
                            pe.wait_ge(m["high_ready"], g)
                        for k in range(4):
                            ins = nc.tensor.transpose(turned[:, 0, k * P:(k + 1) * P], src[:, 4 * g + k], ident[:])
                        ins.then_inc(m["turn_done"], 1)
                    pe.wait_ge(loaded, 4 * 16)
                    pe.wait_ge(tables["loaded"], tables["count"])
                    pe.wait_ge(m["low_ready"], NC)
                    pe.wait_ge(m["high_ready"], NC)
                    pe.wait_ge(m["zeroed"], 1)

                    def sum_squares(n):
                        c, f = divmod(n, F)
                        pe.wait_ge(m["square_ready"], n + 1)
                        if f == 0 and c >= 1:
                            pe.wait_ge(m["norms_ready"], c)
                        nc.tensor.matmul(sums[0:64, 0], head_sum[:, f], square[:, n % 2], start=(f == 0),
                                         stop=(f == F - 1)).then_inc(m["sums_done"], 1)

                    for n in range(N):
                        c, f = divmod(n, F)
                        h = hT[:, c * CH:(c + 1) * CH]
                        if n >= 2:
                            pe.wait_ge(m["cos_done"], n - 1)
                            pe.wait_ge(m["sin_done"], n - 1)
                        nc.tensor.matmul(plain[:, n % 2], wqkv[:, f * P:(f + 1) * P], h, start=True, stop=True)
                        nc.tensor.matmul(swapped[:, n % 2], wrot[:, f * P:(f + 1) * P], h, start=True, stop=True)\
                            .then_inc(m["proj_done"], 1)
                        if n:
                            sum_squares(n - 1)
                    sum_squares(N - 1)
                    for t in range(T):
                        if t >= 2:
                            pe.wait_ge(m["v_read"], t - 1)
                        nc.tensor.matmul(v_ps[:, t % 2], hT[:, t * P:(t + 1) * P], wqkv[:, 2 * INNER_L:],
                                         start=True, stop=True).then_inc(m["v_done"], 1)

                @block.scalar
                def _(act):
                    for g in range(NC):
                        act.wait_ge(m["turn_done"], g + 1)
                        nc.scalar.activation(hT[0:64, g * CH:(g + 1) * CH], turned[0:64, 0], ACT.Copy)\
                            .then_inc(m["low_ready"], 1)
                    for n in range(N):
                        act.wait_ge(m["proj_done"], n + 1)
                        if n >= 2:
                            act.wait_ge(m["sums_done"], n - 1)
                        nc.scalar.activation(square[:, n % 2], plain[:, n % 2], ACT.Square)\
                            .then_inc(m["square_ready"], 1)
                    for t in range(T):
                        act.wait_ge(m["v_done"], t + 1)
                        nc.scalar.activation(v[:, t, :, 0:HEAD_L],
                                             v_ps[:, t % 2].rearrange("p (h d) -> p h d", d=HEAD_L), ACT.Copy)\
                            .then_inc(m["v_read"], 1)

                @block.vector
                def _(dve):
                    nc.vector.memset(hT[64:P, 0:1], 0.0).then_inc(m["zeroed"], 1)
                    for g in range(NC):
                        dve.wait_ge(m["turn_done"], g + 1)
                        nc.vector.tensor_copy(hT[64:P, g * CH + 1:(g + 1) * CH + 1], turned[64:P, 0])\
                            .then_inc(m["high_ready"], 1)
                    for n in range(N):
                        c, f = divmod(n, F)
                        k = f // PAIRS
                        cols = slice(c * CH, (c + 1) * CH)
                        dve.wait_ge(m["square_ready"], n + 1)
                        if n >= 2:
                            dve.wait_ge(m["rot_ready"], n - 1)
                        nc.vector.scalar_tensor_tensor(out=rotated[:, n % 2], in0=plain[:, n % 2],
                                                       scalar=scales[:, 2 * k:2 * k + 1],
                                                       in1=tables["cos"][:, k, cols], op0=ALU.mult, op1=ALU.mult)\
                            .then_inc(m["cos_done"], 1)
                        nc.vector.scalar_tensor_tensor(out=turned_by[:, n % 2], in0=swapped[:, n % 2],
                                                       scalar=scales[:, 2 * k + 1:2 * k + 2],
                                                       in1=tables["sin"][:, k, cols], op0=ALU.mult, op1=ALU.mult)\
                            .then_inc(m["sin_done"], 1)
                        if f == F - 1:
                            dve.wait_ge(m["sums_done"], n + 1)
                            nc.vector.tensor_scalar(norms[:, cols], sums[0:64, 0], NORM_MIN ** 2, None, ALU.max)\
                                .then_inc(m["norms_ready"], 1)

                @block.gpsimd
                def _(pool):
                    nc.gpsimd.memset(v[:, :, :, HEAD_L:], 1.0)
                    for n in range(N):
                        c, f = divmod(n, F)
                        pool.wait_ge(m["cos_done"], n + 1)
                        pool.wait_ge(m["sin_done"], n + 1)
                        nc.gpsimd.tensor_tensor(qkT[:, f, c * CH:(c + 1) * CH], rotated[:, n % 2],
                                                turned_by[:, n % 2], ALU.add).then_inc(m["rot_ready"], 1)

        LIFT = 2.0 ** 20
        with Space(nc, f"lr{layer}") as s:
            spread = s.ps("spread", [P, 4, CH])
            m = {n: s.sem(n) for n in ("unit_set", "ln_ready", "inv_ready", "high_ready", "parts_ready", "spread_done",
                                       "scaled")}
            with nc.Block() as block:

                @block.scalar
                def _(act):
                    act.wait_ge(m["unit_set"], 1)
                    nc.scalar.activation(norms[:], norms[:], ACT.Ln, scale=LIFT).then_inc(m["ln_ready"], 1)
                    act.wait_ge(m["ln_ready"], 1)
                    nc.scalar.activation(norms[:], norms[:], ACT.Exp, scale=-0.5, bias=unit[:, 0:1])\
                        .then_inc(m["inv_ready"], 1)

                @block.vector
                def _(dve):
                    nc.vector.memset(unit[:], float(0.5 * np.log(LIFT))).then_inc(m["unit_set"], 1)
                    dve.wait_ge(m["inv_ready"], 1)
                    nc.vector.tensor_copy(parts[:], norms[:]).then_inc(m["high_ready"], 1)
                    dve.wait_ge(m["high_ready"], 1)
                    nc.vector.tensor_tensor(parts[32:64], norms[32:64], parts[32:64].bitcast(F32), ALU.subtract)\
                        .then_inc(m["parts_ready"], 1)
                    for n in range(N):
                        f, c = divmod(n, NC)
                        dve.wait_ge(m["spread_done"], n + 1)
                        q = qkT[:, f, c * CH:(c + 1) * CH]
                        nc.vector.tensor_tensor(q, q, spread[:, n % 4], ALU.mult).then_inc(m["scaled"], 1)

                @block.tensor
                def _(pe):
                    pe.wait_ge(m["parts_ready"], 1)
                    for n in range(N):
                        f, c = divmod(n, NC)
                        if n >= 4:
                            pe.wait_ge(m["scaled"], n - 3)
                        nc.tensor.matmul(spread[:, n % 4], head_copy[:, f], parts[:, c * CH:(c + 1) * CH],
                                         start=True, stop=True).then_inc(m["spread_done"], 1)


def attend_local(nc, const, layer, band, qkT, v):
    ident = const["ident"]
    HH = HEADS_L // 2
    U = 2 * T
    W = 2 * P
    SCALE = 8.0
    with Space(nc, f"lt{layer}") as s:
        probs = s.sb("probs", [P, 2, HH, W])
        before = s.sb("before", [P, 2, HH * P])
        own = s.sb("own", [P, 2, HH * P])
        most = s.sb("most", [P, 2, HH])
        denom = s.sb("denom", [P, 2, HH])
        o_tok = s.sb("o_tok", [P, 2, INNER_L // 2])
        sim = s.ps("sim", [P, 2, 2, CH])
        own_ps = s.ps("own_ps", [P, CH])
        before_ps = s.ps("before_ps", [P, CH])
        o_ps = s.ps("o_ps", [P, CH])
        oT_ps = s.ps("oT_ps", [P, CH])
        names = ["zeroed", "sim_done", "less_ready", "probs_ready", "turn_done", "own_ready", "before_ready",
                 "o_done", "o_ready", "oT_done", "oT_ready", "max_ready", "rec"]
        m = {n: s.sem(n) for n in names}

        def sims(ap):
            return ap[:, :, 0:2 * KEYS].rearrange("p b (h k) -> p b h k", h=2)

        with nc.Block() as block:

            @block.tensor
            def _(pe):
                def front(u):
                    t, half = divmod(u, 2)
                    if u >= 2:
                        pe.wait_ge(m["less_ready"], u - 1)
                    for b in range(2):
                        bank = sim[:, u % 2, b]
                        nc.tensor.matmul(bank[:, 0:2 * KEYS], const["ident16"][:], band[:], start=True, stop=False)
                        for h in range(2):
                            head = half * HH + 2 * h + b
                            rows = slice((head % 2) * 64, (head % 2) * 64 + 64)
                            lo = WINDOW if t == 0 else 0
                            ins = nc.tensor.matmul(bank[:, h * KEYS + lo:(h + 1) * KEYS],
                                                   qkT[rows, head // 2, t * P:(t + 1) * P],
                                                   qkT[rows, PAIRS + head // 2, t * P - WINDOW + lo:(t + 1) * P],
                                                   start=False, stop=(h == 1))
                    ins.then_inc(m["sim_done"], 1)

                def turn(u):
                    pe.wait_ge(m["probs_ready"], u + 1)
                    if u >= 1:
                        pe.wait_ge(m["own_ready"], u)
                        pe.wait_ge(m["before_ready"], u)
                    for h in range(HH):
                        nc.tensor.transpose(before_ps[:, h * P:(h + 1) * P], probs[:, u % 2, h, 0:P], ident[:])
                        ins = nc.tensor.transpose(own_ps[:, h * P:(h + 1) * P], probs[:, u % 2, h, P:], ident[:])
                    ins.then_inc(m["turn_done"], 1)

                def values(u):
                    t, half = divmod(u, 2)
                    pe.wait_ge(m["own_ready"], u + 1)
                    pe.wait_ge(m["before_ready"], u + 1)
                    if u >= 1:
                        pe.wait_ge(m["o_ready"], u)
                    for h in range(HH):
                        at = 2 * (h % 2) + h // 2
                        out = o_ps[:, at * (HEAD_L + 1):(at + 1) * (HEAD_L + 1)]
                        head = half * HH + at
                        ins = nc.tensor.matmul(out, own[:, u % 2, h * P:(h + 1) * P], v[:, t, head], start=True,
                                               stop=(t == 0))
                        if t:
                            ins = nc.tensor.matmul(out, before[:, u % 2, h * P:(h + 1) * P], v[:, t - 1, head],
                                                   start=False, stop=True)
                    ins.then_inc(m["o_done"], 1)

                def result(u):
                    pe.wait_ge(m["o_ready"], u + 1)
                    if u >= 1:
                        pe.wait_ge(m["oT_ready"], u)
                    for k in range(2):
                        ins = nc.tensor.transpose(oT_ps[:, k * P:(k + 1) * P], o_tok[:, u % 2, k * P:(k + 1) * P],
                                                  ident[:])
                    ins.then_inc(m["oT_done"], 1)

                front(0)
                for u in range(U + 2):
                    if u + 1 < U:
                        front(u + 1)
                    if u < U:
                        turn(u)
                    if 1 <= u <= U:
                        values(u - 1)
                    if u >= 2:
                        result(u - 2)

            @block.scalar
            def _(act):
                act.wait_ge(m["zeroed"], 1)

                def exps(u):
                    act.wait_ge(m["less_ready"], u + 1)
                    nc.scalar.activation(probs[:, u % 2, :, WINDOW:], probs[:, u % 2, :, WINDOW:], ACT.Exp,
                                         scale=SCALE).then_inc(m["probs_ready"], 1)

                exps(0)
                for u in range(U + 2):
                    if u < U:
                        act.wait_ge(m["turn_done"], u + 1)
                        if u >= 2:
                            act.wait_ge(m["o_done"], u - 1)
                        nc.scalar.activation(own[:, u % 2], own_ps[:], ACT.Copy).then_inc(m["own_ready"], 1)
                    if u + 1 < U:
                        exps(u + 1)
                    if u >= 2:
                        t, half = divmod(u - 2, 2)
                        act.wait_ge(m["oT_done"], u - 1)
                        nc.scalar.activation(qkT[:, 2 * half:2 * half + 2, t * P:(t + 1) * P],
                                             oT_ps[:, 0:2 * P].rearrange("p (k n) -> p k n", k=2), ACT.Copy)\
                            .then_inc(m["oT_ready"], 1)

            @block.vector
            def _(dve):
                nc.vector.memset(probs[:], 0.0).then_inc(m["zeroed"], 1)
                dve.wait_ge(m["zeroed"], 1)

                def less(u):
                    dve.wait_ge(m["sim_done"], u + 1)
                    nc.vector.tensor_reduce(most[:, u % 2].rearrange("p (b h) -> p b h", h=2), sims(sim[:, u % 2]),
                                            AX.X, ALU.max).then_inc(m["max_ready"], 1)
                    dve.wait_ge(m["max_ready"], u + 1)
                    if u >= 2:
                        dve.wait_ge(m["turn_done"], u - 1)
                    for b in range(2):
                        ins = nc.vector.tensor_tensor(
                            probs[:, u % 2, 2 * b:2 * b + 2, WINDOW:],
                            sim[:, u % 2, b, 0:2 * KEYS].rearrange("p (h k) -> p h k", h=2),
                            most[:, u % 2, 2 * b:2 * b + 2].unsqueeze(2).broadcast_to([P, 2, KEYS]), ALU.subtract)
                    ins.then_inc(m["less_ready"], 1)

                less(0)
                for u in range(U + 1):
                    if u + 1 < U:
                        less(u + 1)
                    if u < U:
                        dve.wait_ge(m["turn_done"], u + 1)
                        if u >= 2:
                            dve.wait_ge(m["o_done"], u - 1)
                        nc.vector.tensor_copy(before[:, u % 2], before_ps[:]).then_inc(m["before_ready"], 1)
                    if u >= 1:
                        w = u - 1
                        o4 = o_ps[:, 0:HH * (HEAD_L + 1)].rearrange("p (h d) -> p h d", h=HH)
                        dve.wait_ge(m["o_done"], w + 1)
                        nc.vector.reciprocal(denom[:, w % 2], o4[:, :, HEAD_L]).then_inc(m["rec"], 1)
                        dve.wait_ge(m["rec"], w + 1)
                        if w >= 2:
                            dve.wait_ge(m["oT_done"], w - 1)
                        nc.vector.tensor_tensor(o_tok[:, w % 2].rearrange("p (h d) -> p h d", h=HH),
                                                o4[:, :, 0:HEAD_L],
                                                denom[:, w % 2].unsqueeze(2).broadcast_to([P, HH, HEAD_L]), ALU.mult)\
                            .then_inc(m["o_ready"], 1)


def feed_forward(nc, dram, const, layer, x):
    ident = const["ident"]
    with Space(nc, f"ff{layer}") as sp:
        h = sp.sb("h", [P, T, D])
        w1 = sp.sb("w1", [P, 2, HID_T * P])
        b1 = sp.sb("b1", [P, 2, HID_T])
        w2 = sp.sb("w2", [P, HID_T, D])
        b2 = sp.sb("b2", [P, D])
        norm = sp.sb("norm", [P, 2])
        hT = sp.sb("hT", [P, S])
        hidden = sp.sb("hidden", [P, HID_T, S])
        gelu = sp.sb("gelu", [P, 2, CH])
        loaded, shifted, zeroed = sp.sem("loaded"), sp.sem("shifted"), sp.sem("zeroed")
        with nc.Block() as block:

            @block.sync
            def _(sync):
                half = slice(D // 2, D)
                sync.dma_start(h[1:P, :, half], x[0:P - 1, :, half]).then_inc(shifted, 16)
                sync.dma_start(h[0:1, 1:T, half], x[P - 1:P, 0:T - 1, half]).then_inc(shifted, 16)
                for d, n in ((w1, "w1"), (b1, "b1"), (w2, "w2"), (b2, "b2"), (norm, "ffn_norm")):
                    sync.dma_start(d[:], dram[f"{n}{layer}"]).then_inc(loaded, 16)
                sync.wait_ge(shifted, 32)

            @block.vector
            def _(dve):
                nc.vector.memset(h[0:1, 0, D // 2:D], 0.0)
                nc.vector.tensor_copy(h[:, :, 0:D // 2], x[:, :, 0:D // 2])
        normalise(nc, f"fn{layer}", h, h)
        with Space(nc, f"fp{layer}") as s:
            turned = s.ps("turned", [P, 2, CH])
            a_ps = s.ps("a_ps", [P, 2, CH])
            g_ps = s.ps("g_ps", [P, 2, CH])
            prod = s.ps("prod", [P, 2, CH])
            m = {n: s.sem(n) for n in ("turn_done", "hT_ready", "a_done", "g_done", "gelu_ready", "hidden_ready",
                                       "prod_done", "added", "biased")}
            with nc.Block() as block:

                @block.gpsimd
                def _(pool):
                    pool.wait_ge(loaded, 5 * 16)
                    nc.gpsimd.tensor_tensor(x[:], x[:], b2[:].unsqueeze(1).broadcast_to([P, T, D]), ALU.add)\
                        .then_inc(m["biased"], 1)

                @block.tensor
                def _(pe):
                    for g in range(NC):
                        if g >= 2:
                            pe.wait_ge(m["hT_ready"], g - 1)
                        for k in range(4):
                            ins = nc.tensor.transpose(turned[:, g % 2, k * P:(k + 1) * P], h[:, 4 * g + k], ident[:])
                        ins.then_inc(m["turn_done"], 1)
                    pe.wait_ge(loaded, 5 * 16)

                    def up(n):
                        c, f = divmod(n, HID_T)
                        pe.wait_ge(m["hT_ready"], c + 1)
                        if n >= 2:
                            pe.wait_ge(m["hidden_ready"], n - 1)
                        hc = hT[:, c * CH:(c + 1) * CH]
                        nc.tensor.matmul(g_ps[:, n % 2], w1[:, 1, f * P:(f + 1) * P], hc, start=True, stop=True)\
                            .then_inc(m["g_done"], 1)
                        nc.tensor.matmul(a_ps[:, n % 2], w1[:, 0, f * P:(f + 1) * P], hc, start=True, stop=True)\
                            .then_inc(m["a_done"], 1)

                    def down(t):
                        pe.wait_ge(m["hidden_ready"], HID_T * (t // 4 + 1))
                        if t >= 2:
                            pe.wait_ge(m["added"], t - 1)
                        for f in range(HID_T):
                            ins = nc.tensor.matmul(prod[:, t % 2, 0:D], hidden[:, f, t * P:(t + 1) * P], w2[:, f],
                                                   start=(f == 0), stop=(f == HID_T - 1))
                        ins.then_inc(m["prod_done"], 1)

                    for c in range(NC + 1):
                        if c < NC:
                            for f in range(HID_T):
                                up(c * HID_T + f)
                        if c:
                            for t in range(4 * (c - 1), 4 * c):
                                down(t)

                @block.scalar
                def _(act):
                    for n in range(NC * HID_T):
                        act.wait_ge(m["g_done"], n + 1)
                        if n >= 2:
                            act.wait_ge(m["hidden_ready"], n - 1)
                        f = n % HID_T
                        nc.scalar.activation(gelu[:, n % 2], g_ps[:, n % 2], ACT.Gelu, bias=b1[:, 1, f:f + 1])\
                            .then_inc(m["gelu_ready"], 1)

                @block.vector
                def _(dve):
                    dve.wait_ge(loaded, 5 * 16)
                    for g in range(NC):
                        dve.wait_ge(m["turn_done"], g + 1)
                        nc.vector.tensor_scalar(hT[:, g * CH:(g + 1) * CH], turned[:, g % 2], norm[:, 0:1],
                                                norm[:, 1:2], ALU.mult, ALU.add).then_inc(m["hT_ready"], 1)

                    def add(t):
                        dve.wait_ge(m["prod_done"], t + 1)
                        dve.wait_ge(m["biased"], 1)
                        nc.vector.tensor_tensor(x[:, t], x[:, t], prod[:, t % 2, 0:D], ALU.add).then_inc(m["added"], 1)

                    for c in range(NC + 1):
                        if c < NC:
                            for f in range(HID_T):
                                n = c * HID_T + f
                                dve.wait_ge(m["gelu_ready"], n + 1)
                                dve.wait_ge(m["a_done"], n + 1)
                                nc.vector.scalar_tensor_tensor(out=hidden[:, f, c * CH:(c + 1) * CH],
                                                               in0=a_ps[:, n % 2], scalar=b1[:, 0, f:f + 1],
                                                               in1=gelu[:, n % 2], op0=ALU.add, op1=ALU.mult)\
                                    .then_inc(m["hidden_ready"], 1)
                        if c:
                            for t in range(4 * (c - 1), 4 * c):
                                add(t)


def local_transformer(nc, dram, const, x, cur):
    with Space(nc, "lt") as sp:
        tables = {"cos": sp.sb("cos", [P, 2, S]), "sin": sp.sb("sin", [P, 2, S]),
                  "band": sp.sb("band", [P, 2 * KEYS], BF16),
                  "head_sum": sp.sb("head_sum", [P, 2 * PAIRS, 64]),
                  "head_copy": sp.sb("head_copy", [64, 2 * PAIRS, P], F32R),
                  "loaded": nc.alloc_semaphore("tables_loaded"), "count": 3 * 16}
        with Space(nc, "lc") as s:
            band32 = s.sb("band32", [P, 2 * KEYS])
            copy32 = s.sb("copy32", [64, 2 * PAIRS, P])
            got = s.sem("got")
            with nc.Block() as block:

                @block.sync
                def _(sync):
                    for n in ("cos", "sin", "head_sum"):
                        sync.dma_start(tables[n][:], dram[n]).then_inc(tables["loaded"], 16)
                    sync.dma_start(band32[:], dram["band"]).then_inc(got, 16)
                    sync.dma_start(copy32[:], dram["head_copy"]).then_inc(got, 16)

                @block.vector
                def _(dve):
                    dve.wait_ge(got, 32)
                    nc.vector.tensor_copy(tables["band"][:], band32[:])
                    nc.vector.tensor_copy(tables["head_copy"][:], copy32[:])
        for layer in range(DEPTH):
            attention_layer(nc, dram, const, tables, layer, x if layer == 0 else cur, cur)
            clear_semaphores(nc)
        with nc.Block() as block:

            @block.vector
            def _(dve):
                nc.vector.tensor_tensor(x[:], x[:], cur[:], ALU.add)
    normalise(nc, "n1", x, x)



HEADS_G, HEAD_G, LATENT = 16, 64, 64
PAIRS_G = HEADS_G // 2
IW = 2 * P
UNITS = S // IW
RT = 4
MERGED = 4


def latent_attention(nc, dram, const, x, acc):
    ident = const["ident"]
    spare = x[:].rearrange("p t d -> p (t d)")
    values = spare[:, 0:T * LATENT].rearrange("p (t c) -> p t c", c=LATENT)
    mixers = spare[:, T * LATENT:2 * T * LATENT].rearrange("p (g n) -> p g n", n=D)
    with Space(nc, "g") as sp:
        c_q = sp.sb("c_q", [P, S], F32R)
        c_k = sp.sb("c_k", [P, S], F32R)
        cos = sp.sb("cos", [P, S])
        sin = sp.sb("sin", [P, S])
        cos_loaded, stacked = sp.sem("cos_loaded"), sp.sem("stacked")
        normalise(nc, "gn", x, acc)
        with Space(nc, "ga") as s:
            norm = s.sb("norm", [P, 2])
            w_down = s.sb("w_down", [P, 2 * LATENT])
            w_v = s.sb("w_v", [P, PAIRS_G, LATENT])
            w_o = s.sb("w_o", [P, PAIRS_G, D])
            hT = s.sb("hT", [P, S])
            c = s.sb("c", [P, S])
            high = s.sb("high", [P, S], F32R)
            low = s.sb("low", [P, S], F32R)
            turned = s.ps("turned", [P, 2, CH])
            down = s.ps("down", [P, 2, CH])
            v_ps = s.ps("v_ps", [P, 2, CH])
            m_ps = s.ps("m_ps", [P, 2, CH])
            m = {n: s.sem(n) for n in ("loaded", "turn_done", "hT_ready", "down_done", "c_ready", "high_ready",
                                       "low_ready", "v_done", "m_done", "copied")}
            with nc.Block() as block:

                @block.sync
                def _(sync):
                    for d, n in ((norm, "g_norm"), (w_down, "w_down"), (w_v, "w_v"), (w_o, "w_o")):
                        sync.dma_start(d[:], dram[n]).then_inc(m["loaded"], 16)
                    sync.dma_start(cos[:], dram["g_cos"]).then_inc(cos_loaded, 16)
                    sync.dma_start(sin[:], dram["g_sin"]).then_inc(cos_loaded, 16)
                    sync.wait_ge(m["high_ready"], NC)
                    sync.wait_ge(m["low_ready"], NC)
                    for stack, rows in ((c_q, slice(0, 64)), (c_k, slice(64, P))):
                        for half, part in ((slice(0, 64), high), (slice(64, P), low)):
                            sync.dma_start(stack[half].bitcast(F32), part[rows].bitcast(F32)).then_inc(stacked, 16)
                    sync.wait_ge(stacked, 4 * 16)

                @block.tensor
                def _(pe):
                    for g in range(NC):
                        if g >= 2:
                            pe.wait_ge(m["hT_ready"], g - 1)
                        for k in range(4):
                            ins = nc.tensor.transpose(turned[:, g % 2, k * P:(k + 1) * P], acc[:, 4 * g + k], ident[:])
                        ins.then_inc(m["turn_done"], 1)
                    pe.wait_ge(m["loaded"], 4 * 16)
                    for c_ in range(NC):
                        pe.wait_ge(m["hT_ready"], c_ + 1)
                        if c_ >= 2:
                            pe.wait_ge(m["c_ready"], c_ - 1)
                        nc.tensor.matmul(down[:, c_ % 2], w_down[:], hT[:, c_ * CH:(c_ + 1) * CH], start=True,
                                         stop=True).then_inc(m["down_done"], 1)
                    for t in range(T):
                        ins = nc.tensor.matmul(v_ps[:, t // 8, (t % 8) * LATENT:(t % 8 + 1) * LATENT],
                                               hT[:, t * P:(t + 1) * P], w_down[:, LATENT:], start=True, stop=True)
                    ins.then_inc(m["v_done"], 1)
                    for g in range(PAIRS_G):
                        for h in range(2):
                            rows = slice(h * 64, h * 64 + 64)
                            ins = nc.tensor.matmul(m_ps[rows, h, (g % 4) * P:(g % 4 + 1) * P], w_v[rows, g],
                                                   w_o[rows, g], start=True, stop=True)
                        if g % 4 == 3:
                            ins.then_inc(m["m_done"], 1)
                            if g == 3:
                                pe.wait_ge(m["copied"], 2)

                @block.vector
                def _(dve):
                    dve.wait_ge(m["loaded"], 4 * 16)
                    for g in range(NC):
                        dve.wait_ge(m["turn_done"], g + 1)
                        nc.vector.tensor_scalar(hT[:, g * CH:(g + 1) * CH], turned[:, g % 2], norm[:, 0:1],
                                                norm[:, 1:2], ALU.mult, ALU.add).then_inc(m["hT_ready"], 1)
                    dve.wait_ge(m["turn_done"], NC)
                    nc.vector.tensor_scalar(acc[:, 2:T], x[:, 0:T - 2], 2.0, None, ALU.mult)
                    nc.vector.tensor_scalar(acc[:, 0:2], x[:, T - 2:T], 2.0, None, ALU.mult).then_inc(m["copied"], 1)
                    for c_ in range(NC):
                        cols = slice(c_ * CH, (c_ + 1) * CH)
                        dve.wait_ge(m["down_done"], c_ + 1)
                        nc.vector.tensor_scalar(c[0:64, cols], down[0:64, c_ % 2], 0.125, None, ALU.mult)
                        nc.vector.tensor_copy(c[64:P, cols], down[64:P, c_ % 2]).then_inc(m["c_ready"], 1)
                    dve.wait_ge(m["v_done"], 1)
                    dve.wait_ge(m["copied"], 1)
                    nc.vector.tensor_copy(values.rearrange("p (b t) c -> p b (t c)", b=2), v_ps[:])
                    for k in range(2):
                        dve.wait_ge(m["m_done"], k + 1)
                        for h in range(2):
                            rows = slice(h * 64, h * 64 + 64)
                            ins = nc.vector.tensor_copy(mixers[rows, 4 * k:4 * k + 4],
                                                        m_ps[rows, h].rearrange("p (g n) -> p g n", n=D))
                        ins.then_inc(m["copied"], 1)

                @block.scalar
                def _(act):
                    for c_ in range(NC):
                        cols = slice(c_ * CH, (c_ + 1) * CH)
                        act.wait_ge(m["c_ready"], c_ + 1)
                        nc.scalar.activation(high[:, cols], c[:, cols], ACT.Copy).then_inc(m["high_ready"], 1)

                @block.gpsimd
                def _(pool):
                    for c_ in range(NC):
                        cols = slice(c_ * CH, (c_ + 1) * CH)
                        pool.wait_ge(m["high_ready"], c_ + 1)
                        nc.gpsimd.tensor_tensor(low[:, cols], c[:, cols], high[:, cols].bitcast(F32), ALU.subtract)\
                            .then_inc(m["low_ready"], 1)

        keys = sp.sb("keys", [P, 2, 2, S], F32R)
        q_pair = sp.sb("q_pair", [P, 2, S], F32R)
        q_unit = sp.sb("q_unit", [P, 2, 2, 2, IW], F32R)
        w_raw = sp.sb("w_raw", [P, 4 * P])
        w_up = sp.sb("w_up", [P, 2, 2, 4 * P], F32R)
        by_cos = sp.sb("by_cos", [P, CH])
        by_sin = sp.sb("by_sin", [P, CH])
        k_part = sp.sb("k_part", [P, 2, CH], F32R)
        probs = sp.sb("probs", [P, 2, S])
        probsT = sp.sb("probsT", [P, 2, 2, T, IW])
        most = sp.sb("most", [P, 2, 3])
        bias = sp.sb("bias", [P, 2])
        sums = sp.sb("sums", [P, 2, RT, 2])
        recip = sp.sb("recip", [P, RT])
        mixed = sp.sb("mixed", [P, 2, IW])
        mixer = sp.sb("mixer", [P, D])
        zero = sp.sb("zero", [P, 1])
        score = sp.ps("score", [P, 4, CH])
        turned = sp.ps("turned", [P, 2, CH])
        mix_ps = sp.ps("mix_ps", [P, CH])
        side = sp.ps("side", [P, CH])
        m = {n: sp.sem("m_" + n) for n in
             ("w_loaded", "w_ready", "side_full", "side_free", "roped", "high_ready", "low_ready", "k_loaded",
              "q_loaded0", "q_loaded1", "zeroed", "score_done", "bias_ready", "exp_done", "turn_done", "even_copied",
              "odd_copied", "mix_done", "mixed_ready", "mixer_ready", "maxes", "sums_added", "added")}
        q_loaded = [m["q_loaded0"], m["q_loaded1"]]
        PIECES = 2 * NC
        SIDE0 = 2 * PIECES

        def piece_pe(pe, pair, kind, chunk, swap, use):
            pe.wait_ge(m["side_free"], use) if not isinstance(use, int) or use else None
            src = (c_k, c_q)[kind]
            at = ((2, 3), (0, 1))[kind][swap]
            for part in range(2):
                ins = nc.tensor.matmul(side[:], w_up[:, pair, part, at * P:(at + 1) * P],
                                       src[:, bass.ds(chunk * CH, CH)], start=(part == 0), stop=(part == 1))
            ins.then_inc(m["side_full"], 1)

        def piece_dve(dve, chunk, swap, use, n):
            dve.wait_ge(m["side_full"], use + 1)
            if not swap and not (isinstance(n, int) and n == 0):
                dve.wait_ge(m["low_ready"], n)
            dst, table = ((by_cos, cos), (by_sin, sin))[swap]
            nc.vector.tensor_tensor(dst[:], side[:], table[:, bass.ds(chunk * CH, CH)], ALU.mult)\
                .then_inc(m["side_free"], 1)

        def part_of(kind, chunk, part, rows=slice(0, P)):
            return k_part[rows, part] if kind == 0 else q_pair[rows, part, bass.ds(chunk * CH, CH)]

        def piece_pool_add(pool, use, n):
            pool.wait_ge(m["side_free"], use + 2)
            nc.gpsimd.tensor_tensor(by_cos[:], by_cos[:], by_sin[:], ALU.add).then_inc(m["roped"], 1)

        def piece_act(act, kind, chunk, n, k_sent):
            act.wait_ge(m["roped"], n + 1)
            if kind == 0 and k_sent is not None:
                act.wait_ge(m["k_loaded"], k_sent)
            nc.scalar.activation(part_of(kind, chunk, 0), by_cos[:], ACT.Copy).then_inc(m["high_ready"], 1)

        def piece_pool_low(pool, kind, chunk, n):
            pool.wait_ge(m["high_ready"], n + 1)
            nc.gpsimd.tensor_tensor(part_of(kind, chunk, 1), by_cos[:], part_of(kind, chunk, 0).bitcast(F32),
                                    ALU.subtract).then_inc(m["low_ready"], 1)

        def send_k(sync, turn, chunk, n):
            sync.wait_ge(m["low_ready"], n + 1)
            for head in range(2):
                for part in range(2):
                    sync.dma_start(keys[part * 64:(part + 1) * 64, turn, head, bass.ds(chunk * CH, CH)].bitcast(F32),
                                   k_part[head * 64:(head + 1) * 64, part].bitcast(F32)).then_inc(m["k_loaded"], 16)

        def send_q(sync, w, chunk):
            for head in range(2):
                for half in range(2):
                    sync.dma_start(q_unit[half * 64:(half + 1) * 64, w, head].bitcast(F32),
                                   q_pair[head * 64:(head + 1) * 64, :, bass.ds(chunk * IW, IW)].bitcast(F32))\
                        .then_inc(q_loaded[w], 16)

        def load_w(sync, pair):
            sync.dma_start(w_raw[:], dram["w_up"][bass.ds(pair, 1), :, :].rearrange("a p n -> (a p) n"))\
                .then_inc(m["w_loaded"], 16)

        def split_w(pool, turn, count):
            pool.wait_ge(m["w_loaded"], 16 * count)
            nc.gpsimd.tensor_tensor(w_up[:, turn, 0], w_raw[:], zero[:].broadcast_to([P, 4 * P]), ALU.add)\
                .then_inc(m["w_ready"], 1)
            pool.wait_ge(m["w_ready"], 2 * count - 1)
            nc.gpsimd.tensor_tensor(w_up[:, turn, 1], w_raw[:], w_up[:, turn, 0].bitcast(F32), ALU.subtract)\
                .then_inc(m["w_ready"], 1)

        with nc.Block() as block:

            @block.sync
            def _(sync):
                load_w(sync, 0)
                sync.wait_ge(m["w_ready"], 2)
                load_w(sync, 1)
                for c_ in range(NC):
                    send_k(sync, 0, c_, 2 * c_)
                sync.wait_ge(m["low_ready"], PIECES)
                for w in range(2):
                    send_q(sync, w, w)

            @block.gpsimd
            def _(pool):
                nc.gpsimd.memset(zero[:], 0.0).then_inc(m["zeroed"], 1)
                pool.wait_ge(m["zeroed"], 1)
                split_w(pool, 0, 1)
                for n in range(PIECES):
                    kind, c_ = n % 2, n // 2
                    piece_pool_add(pool, 2 * n, n)
                    piece_pool_low(pool, kind, c_, n)
                split_w(pool, 1, 2)
                nc.gpsimd.memset(mixed[:], 0.0)
                nc.gpsimd.memset(mixer[:], 0.0)
                nc.gpsimd.memset(probsT[:, 1], 0.0)
                nc.gpsimd.memset(sums[:], 1.0)

            @block.tensor
            def _(pe):
                pe.wait_ge(m["w_ready"], 2)
                for n in range(PIECES):
                    for swap in range(2):
                        piece_pe(pe, 0, n % 2, n // 2, swap, 2 * n + swap)

            @block.vector
            def _(dve):
                dve.wait_ge(cos_loaded, 32)
                for n in range(PIECES):
                    for swap in range(2):
                        piece_dve(dve, n // 2, swap, 2 * n + swap, n)

            @block.scalar
            def _(act):
                for n in range(PIECES):
                    kind, c_ = n % 2, n // 2
                    piece_act(act, kind, c_, n, 64 * c_ if kind == 0 and c_ else None)

        def rows_of(r):
            return r // 2, r % 2

        def scores(pe, q, k_of, first, rest):
            if first is not None:
                pe.wait_ge(m["exp_done"], first)
            for b in range(4):
                if b == 2 and rest is not None:
                    pe.wait_ge(m["exp_done"], rest)
                for part in range(2):
                    ins = nc.tensor.matmul(score[:, b], q[:, part], k_of(b), start=(part == 0), stop=(part == 1))
                if b:
                    ins.then_inc(m["score_done"], 1)

        def row_max(dve, slot, before):
            for k, banks in enumerate((slice(0, 2), slice(2, 3), slice(3, 4))):
                dve.wait_ge(m["score_done"], before + k + 1)
                nc.vector.tensor_reduce(most[:, slot, k:k + 1], score[:, banks], AX.XY, ALU.max, negate=True)\
                    .then_inc(m["maxes"], 1)
            dve.wait_ge(m["maxes"], before + 3)
            nc.vector.scalar_tensor_tensor(out=bias[:, slot:slot + 1], in0=most[:, slot, 0:1],
                                           scalar=most[:, slot, 1:2], in1=most[:, slot, 2:3], op0=ALU.min,
                                           op1=ALU.min).then_inc(m["bias_ready"], 1)

        def exps(act, slot, w, r, count):
            act.wait_ge(m["bias_ready"], count)
            for k in range(2):
                nc.scalar.activation(probs[:, slot, k * 2 * CH:(k + 1) * 2 * CH],
                                     score[:, 2 * k:2 * k + 2].rearrange("p b n -> p (b n)"), ACT.Exp,
                                     bias=bias[:, slot:slot + 1],
                                     accum_out=sums[:, w, r, k:k + 1]).then_inc(m["exp_done"], 1)

        def copied(w, r, q):
            head, tile = rows_of(r)
            return (probsT[:, w, head, MERGED * q:MERGED * (q + 1), tile * P:(tile + 1) * P],
                    turned[:, q % 2].rearrange("p (t n) -> p t n", n=P))

        def mix(pe, w, tiles):
            for t in tiles:
                for head in range(2):
                    ins = nc.tensor.matmul(mix_ps[head * 64:(head + 1) * 64, 0:IW], values[:, t],
                                           probsT[:, w, head, t], start=(t == 0), stop=(t == T - 1))
            if T - 1 in tiles:
                ins.then_inc(m["mix_done"], 1)

        def take_mixed(act, count):
            act.wait_ge(m["mix_done"], count)
            for head in range(2):
                rows = slice(head * 64, (head + 1) * 64)
                ins = nc.scalar.activation(mixed[rows, head], mix_ps[rows, 0:IW], ACT.Copy)
            ins.then_inc(m["mixed_ready"], 1)

        def output(pe):
            for r in range(RT):
                head, tile = rows_of(r)
                ins = nc.tensor.matmul(side[:, r * D:(r + 1) * D], mixed[:, head, tile * P:(tile + 1) * P], mixer[:],
                                       start=True, stop=True)
            ins.then_inc(m["side_full"], 1)

        def reciprocals(dve, w, U):
            nc.vector.tensor_tensor(recip[:], sums[:, w, :, 0], sums[:, w, :, 1], ALU.add)\
                .then_inc(m["sums_added"], 1)
            dve.wait_ge(m["sums_added"], 2 * U + 1)
            nc.vector.reciprocal(recip[:], recip[:]).then_inc(m["sums_added"], 1)
            dve.wait_ge(m["sums_added"], 2 * U + 2)

        def add_output(dve, U, slot):
            dve.wait_ge(m["side_full"], SIDE0 + 3 * U + 3)
            for r in range(RT):
                _, tile = rows_of(r)
                if r == 2:
                    dve.wait_ge(m["added"], 3 * U + 2)
                a = acc[:, bass.ds(2 * slot + tile, 1)].rearrange("p a d -> p (a d)")
                nc.vector.scalar_tensor_tensor(out=a, in0=side[:, r * D:(r + 1) * D], scalar=recip[:, r:r + 1], in1=a,
                                               op0=ALU.mult, op1=ALU.add)\
                    .then_inc(m["side_free"] if r == RT - 1 else m["added"], 1)

        KTURN = 2 * S
        kflat = keys[:].rearrange("p a h n -> p (a h n)")

        with nc.Block() as block:

            @block.sync
            def _(sync):
                with sync.Fori(0, PAIRS_G // 2) as i:
                    for turn in range(2):
                        g = 2 * i + turn
                        sync.wait_ge(m["w_ready"], 2 * g + 4)
                        load_w(sync, g + 2)
                        with sync.Fori(0, NC) as j:
                            for w in range(2):
                                U = 8 * g + 2 * j + w
                                if w == 0:
                                    send_k(sync, 1 - turn, j, PIECES + U)
                                sync.wait_ge(m["score_done"], 12 * U + 12)
                                send_q(sync, w, (2 * j + w + 2) % UNITS)
                sync.wait_ge(q_loaded[0], 64 * (4 * PAIRS_G + 1))
                sync.wait_ge(q_loaded[1], 64 * (4 * PAIRS_G + 1))

            @block.gpsimd
            def _(pool):
                with pool.Fori(0, PAIRS_G // 2) as i:
                    for turn in range(2):
                        g = 2 * i + turn
                        pool.wait_ge(m["side_full"], SIDE0 + 24 * g)
                        split_w(pool, turn, g + 3)
                        with pool.Fori(0, NC) as j:
                            for w in range(2):
                                U = 8 * g + 2 * j + w
                                piece_pool_add(pool, SIDE0 + 3 * U, PIECES + U)
                                piece_pool_low(pool, w, j, PIECES + U)
                                if w == 0:
                                    pool.wait_ge(m["side_full"], SIDE0 + 3 * U + 3)
                                    pool.wait_ge(m["side_full"], SIDE0)
                                    nc.gpsimd.tensor_copy(mixer[:], mixers[:, bass.ds(g, 1)]
                                                          .rearrange("p a n -> p (a n)")).then_inc(m["mixer_ready"], 1)

            @block.tensor
            def _(pe):
                pe.wait_ge(q_loaded[0], 64)
                pe.wait_ge(m["k_loaded"], 256)
                scores(pe, q_unit[:, 0, 0, :, 0:P], lambda b: keys[:, 0, 0, b * CH:(b + 1) * CH], None, None)
                with pe.Fori(0, PAIRS_G // 2) as i:
                    for turn in range(2):
                        g = 2 * i + turn
                        with pe.Fori(0, NC) as j:
                            for w in range(2):
                                U = 8 * g + 2 * j + w
                                for r in range(RT):
                                    G = 4 * U + r
                                    if r < RT - 1:
                                        head, tile = rows_of(r + 1)
                                        q = q_unit[:, w, head, :, tile * P:(tile + 1) * P]
                                        k_of = lambda b, head=head: keys[:, turn, head, b * CH:(b + 1) * CH]
                                    else:
                                        q = q_unit[:, 1 - w, 0, :, 0:P]
                                        if w == 0:
                                            pe.wait_ge(q_loaded[1], 64 * (4 * g + j + 1))
                                            k_of = lambda b: keys[:, turn, 0, b * CH:(b + 1) * CH]
                                        else:
                                            last = (j + 1) // NC
                                            pe.wait_ge(q_loaded[0], 64 * (4 * g + j + 2))
                                            pe.wait_ge(m["k_loaded"], 256 * (g + 1 + last))
                                            base = last * KTURN if turn == 0 else last * -KTURN + KTURN
                                            k_of = lambda b, base=base: kflat[:, bass.ds(base + b * CH, CH)]
                                    scores(pe, q, k_of, 2 * G + 1, 2 * G + 2)

                                    def turn_group(k):
                                        pe.wait_ge(m["odd_copied" if k % 2 else "even_copied"], 2 * G + k // 2 + 1)
                                        for t in range(MERGED):
                                            ins = nc.tensor.transpose(turned[:, k % 2, t * P:(t + 1) * P],
                                                                      probs[:, r % 2, (MERGED * k + t) * P:
                                                                            (MERGED * k + t + 1) * P], ident[:])
                                        ins.then_inc(m["turn_done"], 1)

                                    turn_group(0)
                                    turn_group(1)
                                    if r == 0:
                                        pe.wait_ge(m["mixed_ready"], U + 1)
                                        mix(pe, 1 - w, range(0, 6))
                                    elif r == 1:
                                        mix(pe, 1 - w, range(6, 11))
                                    elif r == 2:
                                        mix(pe, 1 - w, range(11, T))
                                    else:
                                        pe.wait_ge(m["side_free"], SIDE0 + 3 * U + 2)
                                        pe.wait_ge(m["mixed_ready"], U + 2)
                                        if w:
                                            pe.wait_ge(m["mixer_ready"], 4 * g + j + 1)
                                        output(pe)
                                    if r < 2:
                                        pe.wait_ge(m["w_ready"], 2 * g + 4)
                                        piece_pe(pe, 1 - turn, w, j, r, SIDE0 + 3 * U + r)
                                    turn_group(2)
                                    turn_group(3)
                UL = PAIRS_G * UNITS
                pe.wait_ge(m["mixed_ready"], UL + 1)
                pe.wait_ge(m["even_copied"], 8 * UL + 1)
                pe.wait_ge(m["odd_copied"], 8 * UL + 1)
                mix(pe, 1, range(T))
                pe.wait_ge(m["mixed_ready"], UL + 2)
                pe.wait_ge(m["side_free"], SIDE0 + 3 * UL)
                output(pe)

            @block.vector
            def _(dve):
                dve.sem_inc(m["even_copied"], 1)
                row_max(dve, 0, 0)
                with dve.Fori(0, PAIRS_G // 2) as i:
                    for turn in range(2):
                        g = 2 * i + turn
                        with dve.Fori(0, NC) as j:
                            for w in range(2):
                                U = 8 * g + 2 * j + w
                                for r in range(RT):
                                    G = 4 * U + r
                                    row_max(dve, (r + 1) % 2, 3 * G + 3)
                                    dve.wait_ge(m["turn_done"], 4 * G + 1)
                                    nc.vector.tensor_copy(*copied(w, r, 0)).then_inc(m["even_copied"], 1)
                                    if r < 2:
                                        piece_dve(dve, j, r, SIDE0 + 3 * U + r, PIECES + U)
                                    if r == 2:
                                        reciprocals(dve, 1 - w, U)
                                    if r == 3:
                                        add_output(dve, U, 2 * j + w)
                                    dve.wait_ge(m["turn_done"], 4 * G + 3)
                                    nc.vector.tensor_copy(*copied(w, r, 2)).then_inc(m["even_copied"], 1)
                UL = PAIRS_G * UNITS
                dve.wait_ge(m["side_free"], SIDE0 + 3 * UL)
                reciprocals(dve, 1, UL)
                dve.wait_ge(m["side_full"], SIDE0 + 3 * UL + 1)
                for r in range(RT):
                    _, tile = rows_of(r)
                    if r == 2:
                        dve.wait_ge(m["added"], 3 * UL + 2)
                    nc.vector.scalar_tensor_tensor(out=acc[:, tile], in0=side[:, r * D:(r + 1) * D],
                                                   scalar=recip[:, r:r + 1], in1=acc[:, tile], op0=ALU.mult,
                                                   op1=ALU.add).then_inc(m["added"], 1)

            @block.scalar
            def _(act):
                act.sem_inc(m["odd_copied"], 1)
                act.sem_inc(m["mixed_ready"], 1)
                exps(act, 0, 0, 0, 1)
                with act.Fori(0, PAIRS_G // 2) as i:
                    for turn in range(2):
                        g = 2 * i + turn
                        with act.Fori(0, NC) as j:
                            for w in range(2):
                                U = 8 * g + 2 * j + w
                                for r in range(RT):
                                    G = 4 * U + r
                                    act.wait_ge(m["turn_done"], 4 * G + 2)
                                    nc.scalar.activation(*copied(w, r, 1), ACT.Copy).then_inc(m["odd_copied"], 1)
                                    exps(act, (r + 1) % 2, w if r < RT - 1 else 1 - w, (r + 1) % RT, G + 2)
                                    act.wait_ge(m["turn_done"], 4 * G + 4)
                                    nc.scalar.activation(*copied(w, r, 3), ACT.Copy).then_inc(m["odd_copied"], 1)
                                    if r == 2:
                                        piece_act(act, w, j, PIECES + U, 64 * (4 * (g + 1) + j) if w == 0 else None)
                                        take_mixed(act, U + 1)
                take_mixed(act, PAIRS_G * UNITS + 1)

    with nc.Block() as block:

        @block.vector
        def _(dve):
            nc.vector.tensor_copy(x[:, 0:T - 2], acc[:, 2:T])
            nc.vector.tensor_copy(x[:, T - 2:T], acc[:, 0:2])
    normalise(nc, "n2", x, x)
    clear_semaphores(nc)



EXPERTS, TOP, HID_E = 16, 4, 64
ROUTE = 2.5
GROUPS = EXPERTS // 2 + 1


def experts(nc, dram, const, x):
    ident = const["ident"]
    E = EXPERTS
    with Space(nc, "e") as sp:
        xT = sp.sb("xT", [P, S])
        w_gate = sp.sb("w_gate", [P, GROUPS, P])
        w_up = sp.sb("w_up", [P, GROUPS, P])
        w_down = sp.sb("w_down", [P, GROUPS, D])
        combT = sp.sb("combT", [64, S])
        parts = sp.sb("parts", [64, S], F32R)
        copy = sp.sb("copy", [64, EXPERTS // 2, P], F32R)
        w_loaded = sp.sem("w_loaded")
        with Space(nc, "ea") as s:
            router = s.sb("router", [P, E])
            rows = s.sb("rows", [P, E])
            lower = s.sb("lower", [P, E, E])
            lower16 = s.sb("lower16", [P, E, E], BF16)
            copy32 = s.sb("copy32", [64, EXPERTS // 2, P])
            score = s.sb("score", [P, T, E])
            biased = s.sb("biased", [P, T, E])
            above = s.sb("above", [P, T, E, E], BF16)
            ties = s.sb("ties", [P, T, E, E], BF16)
            rank = s.sb("rank", [P, T, E])
            total = s.sb("total", [P, T])
            comb = s.sb("comb", [P, T, 64])
            turned = s.ps("turned", [P, 2, CH])
            score_ps = s.ps("score_ps", [P, CH])
            comb_ps = s.ps("comb_ps", [P, 4, CH])
            m = {n: s.sem(n) for n in ("loaded", "turn_done", "xT_ready", "score_done", "score_ready", "zeroed",
                                       "comb_ready", "comb_done", "order", "combT_ready", "high_ready")}
            with nc.Block() as block:

                @block.sync
                def _(sync):
                    for d, n in ((router, "router"), (rows, "router_bias"), (lower, "lower"), (copy32, "head_copy")):
                        sync.dma_start(d[:], dram[n]).then_inc(m["loaded"], 16)
                    for d, n in ((w_gate, "w_gate"), (w_up, "w_up_e"), (w_down, "w_down_e")):
                        sync.dma_start(d[:], dram[n]).then_inc(w_loaded, 16)

                @block.tensor
                def _(pe):
                    for g in range(NC):
                        if g >= 2:
                            pe.wait_ge(m["xT_ready"], g - 1)
                        for k in range(4):
                            ins = nc.tensor.transpose(turned[:, g % 2, k * P:(k + 1) * P], x[:, 4 * g + k], ident[:])
                        ins.then_inc(m["turn_done"], 1)
                    pe.wait_ge(m["loaded"], 4 * 16)
                    pe.wait_ge(m["xT_ready"], NC)
                    for t in range(T):
                        ins = nc.tensor.matmul(score_ps[:, t * E:(t + 1) * E], xT[:, t * P:(t + 1) * P], router[:],
                                               start=True, stop=True)
                    ins.then_inc(m["score_done"], 1)
                    pe.wait_ge(m["comb_ready"], 1)
                    for t in range(T):
                        ins = nc.tensor.transpose(comb_ps[0:64, t // 4, (t % 4) * P:(t % 4 + 1) * P], comb[:, t],
                                                  ident[:])
                    ins.then_inc(m["comb_done"], 1)

                @block.scalar
                def _(act):
                    for g in range(NC):
                        act.wait_ge(m["turn_done"], g + 1)
                        nc.scalar.activation(xT[:, g * CH:(g + 1) * CH], turned[:, g % 2], ACT.Copy)\
                            .then_inc(m["xT_ready"], 1)
                    act.wait_ge(m["score_done"], 1)
                    nc.scalar.activation(score[:].rearrange("p t e -> p (t e)"), score_ps[:, 0:T * E], ACT.Sigmoid)\
                        .then_inc(m["score_ready"], 1)

                @block.gpsimd
                def _(pool):
                    nc.gpsimd.memset(comb[:], 0.0).then_inc(m["zeroed"], 1)

                @block.vector
                def _(dve):
                    link = Chain(dve, m["order"])
                    dve.wait_ge(m["loaded"], 4 * 16)
                    nc.vector.tensor_copy(lower16[:], lower[:])
                    nc.vector.tensor_copy(copy[:], copy32[:])
                    dve.wait_ge(m["score_ready"], 1)
                    link(nc.vector.tensor_tensor(biased[:], score[:], rows[:].unsqueeze(1).broadcast_to([P, T, E]),
                                                 ALU.add))
                    other = biased[:].unsqueeze(2).broadcast_to([P, T, E, E])
                    mine = biased[:].unsqueeze(3).broadcast_to([P, T, E, E])
                    nc.vector.tensor_tensor(above[:], other, mine, ALU.is_gt)
                    link(nc.vector.tensor_tensor(ties[:], other, mine, ALU.is_equal))
                    link(nc.vector.tensor_tensor(ties[:], ties[:], lower16[:].unsqueeze(1).broadcast_to([P, T, E, E]),
                                                 ALU.mult))
                    link(nc.vector.tensor_tensor(above[:], above[:], ties[:], ALU.add))
                    link(nc.vector.tensor_reduce(rank[:], above[:], AX.X, ALU.add))
                    link(nc.vector.scalar_tensor_tensor(out=score[:], in0=rank[:], scalar=float(TOP), in1=score[:],
                                                        op0=ALU.is_lt, op1=ALU.mult))
                    link(nc.vector.tensor_reduce(total[:], score[:], AX.X, ALU.add))
                    link(nc.vector.reciprocal(total[:], total[:]))
                    link(nc.vector.tensor_tensor(score[:], score[:], total[:].unsqueeze(2).broadcast_to([P, T, E]),
                                                 ALU.mult))
                    dve.wait_ge(m["zeroed"], 1)
                    for k in (0, 32):
                        ins = nc.vector.tensor_scalar(comb[:, :, k:k + E], score[:], ROUTE, None, ALU.mult)
                    ins.then_inc(m["comb_ready"], 1)
                    dve.wait_ge(m["comb_done"], 1)
                    nc.vector.tensor_copy(combT[:].rearrange("p (b n) -> p b n", b=4), comb_ps[0:64])\
                        .then_inc(m["combT_ready"], 1)
                    dve.wait_ge(m["combT_ready"], 1)
                    nc.vector.tensor_copy(parts[:], combT[:]).then_inc(m["high_ready"], 1)
                    dve.wait_ge(m["high_ready"], 1)
                    nc.vector.tensor_tensor(parts[32:64], combT[32:64], parts[32:64].bitcast(F32), ALU.subtract)

        with Space(nc, "eb") as s:
            hidden = s.sb("hidden", [P, GROUPS, S])
            gated = s.sb("gated", [P, 2, CH])
            g_ps = s.ps("g_ps", [P, 2, CH])
            u_ps = s.ps("u_ps", [P, 2, CH])
            c_ps = s.ps("c_ps", [P, 2, CH])
            prod = s.ps("prod", [P, 2, CH])
            m = {n: s.sem(n) for n in ("g_done", "u_done", "silu_ready", "mult_done", "hidden_ready", "prod_done",
                                       "added")}
            with nc.Block() as block:

                @block.tensor
                def _(pe):
                    pe.wait_ge(w_loaded, 3 * 16)

                    def up(n):
                        c, g = divmod(n, GROUPS)
                        cols = slice(c * CH, (c + 1) * CH)
                        if n >= 2:
                            pe.wait_ge(m["hidden_ready"], n - 1)
                        nc.tensor.matmul(g_ps[:, n % 2], w_gate[:, g], xT[:, cols], start=True, stop=True)\
                            .then_inc(m["g_done"], 1)
                        if g < GROUPS - 1:
                            nc.tensor.matmul(c_ps[:, n % 2], copy[:, g], parts[:, cols], start=True, stop=True)
                        nc.tensor.matmul(u_ps[:, n % 2], w_up[:, g], xT[:, cols], start=True, stop=True)\
                            .then_inc(m["u_done"], 1)

                    def down(t):
                        pe.wait_ge(m["hidden_ready"], GROUPS * (t // 4 + 1))
                        if t >= 2:
                            pe.wait_ge(m["added"], t - 1)
                        for g in range(GROUPS):
                            ins = nc.tensor.matmul(prod[:, t % 2, 0:D], hidden[:, g, t * P:(t + 1) * P], w_down[:, g],
                                                   start=(g == 0), stop=(g == GROUPS - 1))
                        ins.then_inc(m["prod_done"], 1)

                    for c in range(NC + 1):
                        for g in range(GROUPS):
                            if c < NC:
                                up(c * GROUPS + g)
                            if c and g >= 2 and g % 2 == 0:
                                down(4 * (c - 1) + g // 2 - 1)

                @block.scalar
                def _(act):
                    for n in range(NC * GROUPS):
                        act.wait_ge(m["g_done"], n + 1)
                        if n >= 2:
                            act.wait_ge(m["mult_done"], n - 1)
                        nc.scalar.activation(gated[:, n % 2], g_ps[:, n % 2], ACT.Silu).then_inc(m["silu_ready"], 1)

                @block.vector
                def _(dve):
                    def multiply(n):
                        c, g = divmod(n, GROUPS)
                        out = hidden[:, g, c * CH:(c + 1) * CH]
                        dve.wait_ge(m["silu_ready"], n + 1)
                        dve.wait_ge(m["u_done"], n + 1)
                        nc.vector.tensor_tensor(out, gated[:, n % 2], u_ps[:, n % 2], ALU.mult)\
                            .then_inc(m["mult_done"], 1)

                    def weigh(n):
                        c, g = divmod(n, GROUPS)
                        out = hidden[:, g, c * CH:(c + 1) * CH]
                        dve.wait_ge(m["mult_done"], n + 1)
                        if g < GROUPS - 1:
                            nc.vector.tensor_tensor(out, out, c_ps[:, n % 2], ALU.mult)\
                                .then_inc(m["hidden_ready"], 1)
                        else:
                            dve.sem_inc(m["hidden_ready"], 1)

                    def add(t):
                        dve.wait_ge(m["prod_done"], t + 1)
                        nc.vector.tensor_tensor(x[:, t], x[:, t], prod[:, t % 2, 0:D], ALU.add).then_inc(m["added"], 1)

                    for c in range(NC + 1):
                        for g in range(GROUPS):
                            if c < NC:
                                multiply(c * GROUPS + g)
                                weigh(c * GROUPS + g)
                            if c and g >= 2 and g % 2 == 0:
                                add(4 * (c - 1) + g // 2 - 1)
    normalise(nc, "n3", x, x)


def build(nc, dram, out, stages=4):
    with Space(nc, "top") as top:
        x_tok = top.sb("x_tok", [P, T, D])
        const = {n: top.sb(n, [P, P]) for n in ("ident", "upto", "after", "ones")}
        const["ident16"] = top.sb("ident16", [P, P], BF16)
        const["x_loaded"], const["loaded"] = nc.alloc_semaphore("x_loaded"), nc.alloc_semaphore("consts_loaded")
        const["count"] = 3 * 16
        stored = nc.alloc_semaphore("stored")
        Space.used = []
        with nc.Block() as block:

            @block.sync
            def _(sync):
                sync.dma_start(x_tok[:], dram["x"].rearrange("(t p) d -> p t d", p=P)).then_inc(const["x_loaded"], 16)
                for n in ("ident", "upto", "after"):
                    sync.dma_start(const[n][:], dram[n]).then_inc(const["loaded"], 16)

            @block.vector
            def _(dve):
                nc.vector.memset(const["ones"][:], 1.0)
                dve.wait_ge(const["loaded"], const["count"])
                nc.vector.tensor_copy(const["ident16"][:], const["ident"][:])

        with Space(nc, "mid") as mid:
            y_tok = mid.sb("y_tok", [P, T, D])
            state_space(nc, dram, const, x_tok, y_tok)
            if stages >= 2:
                local_transformer(nc, dram, const, y_tok, x_tok)
            if stages >= 3:
                latent_attention(nc, dram, const, y_tok, x_tok)
            if stages >= 4:
                experts(nc, dram, const, y_tok)
            last = y_tok
            with nc.Block() as block:

                @block.sync
                def _(sync):
                    sync.dma_start(out.rearrange("(t p) d -> p t d", p=P), last[:]).then_inc(stored, 16)
                    sync.wait_ge(stored, 16)


def _layout(i):
    f = {k: np.asarray(v) for k, v in i.items()}
    a = {}

    def rows(*vs):
        return np.ascontiguousarray(np.broadcast_to(np.concatenate([v.reshape(-1) for v in vs])[None],
                                                    (P, sum(v.size for v in vs))))

    k = np.arange(P)
    a["ident"] = np.eye(P, dtype=np.float32)
    a["upto"] = (k[:, None] <= k[None]).astype(np.float32)
    a["after"] = (k[:, None] > k[None]).astype(np.float32)
    a["x"] = f["L0_attn_x"].reshape(S, D)
    w = f["L0_attn_in_proj_w"]
    a["w_xbc"] = w[INNER:3 * INNER].T
    a["w_zdt"] = np.concatenate([w[:INNER], w[3 * INNER:]]).T
    a["conv_w"] = f["L0_attn_conv_w"].reshape(4, P, TAPS).transpose(1, 0, 2)
    a["conv_b"] = f["L0_attn_conv_b"].reshape(4, P).T
    a["ss_rows"] = rows(f["L0_attn_dt_bias"], f["L0_attn_A_log"], f["L0_attn_D"], f["L0_attn_ln_w"], f["L0_attn_ln_b"])
    a["norm_w"] = f["L0_attn_norm_w"].reshape(2, P).T
    a["w_out_s"] = f["L0_attn_out_proj_w"].T.reshape(2, P, D).transpose(1, 0, 2)
    F = 2 * PAIRS
    half = np.arange(0, HEAD_L, 2, dtype=np.float32)
    freqs = np.arange(S, dtype=np.float32)[:, None] * (1.0 / 10000.0 ** (half / HEAD_L)).astype(np.float32)[None]
    base = (half + 0.4 * HEAD_L) / (1.4 * HEAD_L)
    power = (np.arange(S, dtype=np.float32) - S // 2) / (WINDOW // 2)
    scale = base[None].astype(np.float64) ** power[:, None]
    cos, sin = np.cos(freqs.astype(np.float64)), np.sin(freqs.astype(np.float64))

    def by_channel(first, second):
        return np.concatenate([first.T, second.T, first.T, second.T]).astype(np.float32)

    a["cos"] = np.stack([by_channel(cos * scale, cos * scale), by_channel(cos / scale, cos / scale)], 1)
    a["sin"] = np.stack([by_channel(-sin * scale, sin * scale), by_channel(-sin / scale, sin / scale)], 1)
    i, j = np.arange(P)[:, None], np.arange(KEYS)[None] - WINDOW
    band = np.where((i < j) | (i > j + WINDOW), np.float32(MASKED), np.float32(0))
    a["band"] = np.concatenate([band, band], 1)
    head_sum = np.zeros((P, F, 64), np.float32)
    for g in range(F):
        for h in range(2):
            for r in (0, 32):
                head_sum[h * 64:(h + 1) * 64, g, r + 2 * g + h] = 1.0
    a["head_sum"], a["head_copy"] = head_sum, head_sum.transpose(2, 1, 0)
    swap = np.r_[HEAD_L // 2:HEAD_L, 0:HEAD_L // 2]
    for n in range(DEPTH):
        w = f["L0_ffn_wqkv"][n]
        a[f"wqkv{n}"] = w
        a[f"wrot{n}"] = w[:, :2 * INNER_L].reshape(D, 2 * HEADS_L, HEAD_L)[:, :, swap].reshape(D, 2 * INNER_L)
        q, k = f["L0_ffn_q_scale"][n], f["L0_ffn_k_scale"][n]
        a[f"scales{n}"] = np.stack([np.tile(q, 2), np.tile(q[swap], 2), np.tile(k, 2), np.tile(k[swap], 2)], 1)
        a[f"wo{n}"] = f["L0_ffn_wo"][n].reshape(PAIRS, P, D).transpose(1, 0, 2)
        pad = HID_T * P - HIDDEN
        a[f"w1{n}"] = np.pad(f["L0_ffn_w1"][n].reshape(D, 2, HIDDEN), ((0, 0), (0, 0), (0, pad)))
        a[f"b1{n}"] = np.pad(f["L0_ffn_b1"][n].reshape(2, HIDDEN), ((0, 0), (0, pad)))\
            .reshape(2, HID_T, P).transpose(2, 0, 1)
        a[f"w2{n}"] = np.pad(f["L0_ffn_w2"][n], ((0, pad), (0, 0))).reshape(HID_T, P, D).transpose(1, 0, 2)
        a[f"b2{n}"] = rows(f["L0_ffn_b2"][n])
        a[f"ffn_norm{n}"] = np.stack([f["L0_ffn_ln_g"][n], f["L0_ffn_ln_b"][n]], 1)
    a["g_norm"] = np.stack([f["L1_attn_ln_scale"], f["L1_attn_ln_bias"]], 1)
    a["w_down"] = np.concatenate([f["L1_attn_w_down_q"], f["L1_attn_w_down_kv"]]).T
    a["w_v"] = f["L1_attn_w_up_v"].reshape(PAIRS_G, P, LATENT).transpose(1, 0, 2)
    a["w_o"] = f["L1_attn_w_out"].T.reshape(PAIRS_G, P, D).transpose(1, 0, 2)
    order = np.r_[0:HEAD_G:2, 1:HEAD_G:2]
    turned = np.r_[1:HEAD_G:2, 0:HEAD_G:2]
    ups = []
    for name in ("L1_attn_w_up_q", "L1_attn_w_up_k"):
        w = f[name].reshape(PAIRS_G, 2, HEAD_G, LATENT)
        for o in (order, turned):
            ups.append(w[:, :, o].reshape(PAIRS_G, P, LATENT).transpose(0, 2, 1))
    up = np.concatenate(ups, 2)
    up = np.concatenate([up, up], 1)
    a["w_up"] = np.concatenate([up, up[:2]])
    inv = 1.0 / 10000.0 ** (np.arange(0, HEAD_G, 2, dtype=np.float32) / HEAD_G)
    freqs = np.outer(np.arange(S, dtype=np.float32), inv)
    cos, sin = (np.concatenate([t(freqs), t(freqs)], 1)[:, ::2] for t in (np.cos, np.sin))
    a["g_cos"] = np.concatenate([cos.T] * 4).astype(np.float32)
    a["g_sin"] = np.concatenate([-sin.T, sin.T] * 2).astype(np.float32)
    a["router"] = f["L1_ffn_gate_w"].T
    a["router_bias"] = rows(f["L1_ffn_gate_b"])
    e = np.arange(EXPERTS)
    a["lower"] = rows((e[None] < e[:, None]).astype(np.float32)).reshape(P, EXPERTS, EXPERTS)
    w13 = np.concatenate([f["L1_ffn_w13"], f["L1_ffn_w13_s"][None], np.zeros((1, P, D), np.float32)])
    w13 = w13.reshape(GROUPS, 2, 2, HID_E, D)
    a["w_gate"] = w13[:, :, 0].reshape(GROUPS, P, D).transpose(2, 0, 1)
    a["w_up_e"] = w13[:, :, 1].reshape(GROUPS, P, D).transpose(2, 0, 1)
    w2 = np.concatenate([f["L1_ffn_w2"], f["L1_ffn_w2_s"][None], np.zeros((1, D, HID_E), np.float32)])
    a["w_down_e"] = w2.transpose(0, 2, 1).reshape(GROUPS, P, D).transpose(1, 0, 2)
    return {n: np.ascontiguousarray(v) for n, v in a.items()}


def kernel(**inputs):
    import numpy as _np
    import concourse.bacc as _bacc
    from concourse import mybir as _mybir
    from concourse.bass_utils import run_bass_kernel_spmd as _run

    nc = _bacc.Bacc("TRN2", target_bir_lowering=False, num_devices=1)
    arrays = _layout(inputs)
    dram = {n: nc.dram_tensor(n, a.shape, _mybir.dt.from_np(a.dtype), kind="ExternalInput").ap()
            for n, a in arrays.items()}
    out = nc.dram_tensor("out", (S, D), _mybir.dt.from_np(_np.dtype("float32")), kind="ExternalOutput").ap()
    build(nc, dram, out)
    result = _run(nc, [arrays], core_ids=[0])
    return result.results[0]["out"].reshape(1, S, D)
```

```python
import concourse.bass as bass
from concourse import mybir
from concourse.alu_op_type import AluOpType as ALU
from contextlib import ExitStack
import numpy as np

F32 = mybir.dt.float32
F32R = mybir.dt.float32r
BF16 = mybir.dt.bfloat16
ACT = mybir.ActivationFunctionType
AX = mybir.AxisListType

P = 128
D = 128
S = 2048
T = S // P
CH = 512
NC = S // CH
EPS = 1e-5


class Chain:

    def __init__(self, eng, sem):
        self.eng, self.sem, self.n = eng, sem, 0

    def __call__(self, ins):
        self.n += 1
        ins.then_inc(self.sem, 1)
        self.eng.wait_ge(self.sem, self.n)


class Space:

    used = []

    def __init__(self, nc, name):
        self.nc, self.name, self.stack = nc, name, ExitStack()

    def __enter__(self):
        self.stack.__enter__()
        return self

    def __exit__(self, *e):
        return self.stack.__exit__(*e)

    def sb(self, name, shape, dt=F32):
        return self.stack.enter_context(self.nc.sbuf_tensor(f"{self.name}.{name}", shape, dt))

    def ps(self, name, shape, dt=F32):
        return self.stack.enter_context(self.nc.psum_tensor(f"{self.name}_{name}", shape, dt))

    def sem(self, name):
        holder = self.nc.semaphore(f"{self.name}_{name}")
        sem = holder.__enter__()
        Space.used.append((holder, sem))
        return sem


def clear_semaphores(nc):
    with nc.Block() as block:

        @block.gpsimd
        def _(pool):
            for _, sem in Space.used:
                pool.sem_clear(sem)

    while Space.used:
        Space.used.pop()[0].__exit__(None, None, None)


def normalise(nc, name, src, dst, scale=None, shift=None, residual=None):
    with Space(nc, name) as sp:
        stats = sp.sb("stats", [P, T, 6])
        moments = sp.sb("moments", [P, T, 2])
        spread = sp.sb("spread", [P, T])
        eps = sp.sb("eps", [P, 1])
        order, var_ready, std_ready = sp.sem("order"), sp.sem("var"), sp.sem("std")
        scaled, eps_ready, shifted = sp.sem("scaled"), sp.sem("eps_ready"), sp.sem("shifted")
        with nc.Block() as block:

            @block.vector
            def _(dve):
                nc.vector.memset(eps[:], EPS).then_inc(eps_ready, 1)
                for t in range(T):
                    nc.vector.bn_stats(stats[:, t], src[:, t]).then_inc(order, 1)
                for t in range(T):
                    dve.wait_ge(order, t + 1)
                    ins = nc.vector.bn_aggr(moments[:, t], stats[:, t])
                ins.then_inc(var_ready, 1)
                dve.wait_ge(std_ready, 1)
                link = Chain(dve, order)
                link.n = T
                link(nc.vector.reciprocal(spread[:], spread[:]))
                dve.wait_ge(var_ready, 1)
                if scale is None:
                    for t in range(T):
                        nc.vector.tensor_scalar(dst[:, t], src[:, t], moments[:, t, 0:1], spread[:, t:t + 1],
                                                ALU.subtract, ALU.mult)
                else:
                    for t in range(T):
                        nc.vector.scalar_tensor_tensor(out=dst[:, t], in0=src[:, t], scalar=moments[:, t, 0:1],
                                                       in1=scale, op0=ALU.subtract, op1=ALU.mult).then_inc(scaled, 1)
                    dve.wait_ge(shifted, 1)
                    for t in range(T):
                        dve.wait_ge(scaled, t + 1)
                        nc.vector.scalar_tensor_tensor(out=dst[:, t], in0=dst[:, t], scalar=spread[:, t:t + 1],
                                                       in1=residual[:, t], op0=ALU.mult, op1=ALU.add)

            if scale is not None:

                @block.gpsimd
                def _(pool):
                    nc.gpsimd.tensor_tensor(residual[:], residual[:], shift.unsqueeze(1).broadcast_to([P, T, D]),
                                            ALU.add).then_inc(shifted, 1)

            @block.scalar
            def _(act):
                act.wait_ge(eps_ready, 1)
                act.wait_ge(var_ready, 1)
                nc.scalar.activation(spread[:], moments[:, :, 1], ACT.Sqrt,
                                     bias=eps[:, 0:1]).then_inc(std_ready, 1)



HEADS_S, HEAD_S, STATE = 4, 64, 128
INNER = HEADS_S * HEAD_S
TAPS = 4


def state_space(nc, dram, const, x_tok, out_tok):
    ident, upto, after, ones = const["ident"], const["upto"], const["after"], const["ones"]
    HP = HEADS_S * P
    with Space(nc, "ss") as sp:
        w_xbc = sp.sb("w_xbc", [P, 4 * P])
        w_zdt = sp.sb("w_zdt", [P, INNER + HEADS_S])
        conv_w = sp.sb("conv_w", [P, 4, TAPS])
        conv_b = sp.sb("conv_b", [P, 4])
        rows = sp.sb("rows", [P, 3 * HEADS_S + 2 * D])
        norm_w = sp.sb("norm_w", [P, 2])
        w_out = sp.sb("w_out", [P, 2, D])
        xbc = sp.sb("xbc", [P, 4, S])
        gate = sp.sb("gate", [P, T, INNER])
        dt = sp.sb("dt", [P, T, HEADS_S])
        decay = sp.sb("decay", [P, T, HEADS_S])
        w_loaded = sp.sem("w_loaded")
        dt_bias, a_log, skip = rows[:, 0:4], rows[:, 4:8], rows[:, 8:12]
        ln_w, ln_b = rows[:, 12:12 + D], rows[:, 12 + D:12 + 2 * D]

        with Space(nc, "ssa") as sa:
            xT = sa.sb("xT", [P, S])
            raw = sa.sb("raw", [P, 2, TAPS - 1 + S])
            turned = sa.ps("turned", [P, 2, CH])
            proj = sa.ps("proj", [P, 4, CH])
            zdt = sa.ps("zdt", [P, 2, CH])
            turn_done, xT_ready, pads = sa.sem("turn_done"), sa.sem("xT_ready"), sa.sem("pads")
            proj_done, raw_ready, conv_done = sa.sem("proj_done"), sa.sem("raw_ready"), sa.sem("conv_done")
            zdt_done, z_read, order = sa.sem("zdt_done"), sa.sem("z_read"), sa.sem("order")
            with nc.Block() as block:

                @block.sync
                def _(sync):
                    for dst, src in ((w_xbc, "w_xbc"), (w_zdt, "w_zdt"), (conv_w, "conv_w"), (conv_b, "conv_b"),
                                     (rows, "ss_rows"), (norm_w, "norm_w"), (w_out, "w_out_s")):
                        sync.dma_start(dst[:], dram[src]).then_inc(w_loaded, 16)

                @block.gpsimd
                def _(pool):
                    nc.gpsimd.memset(raw[:, :, 0:TAPS - 1], 0.0).then_inc(pads, 1)

                @block.tensor
                def _(pe):
                    pe.wait_ge(const["x_loaded"], 16)
                    pe.wait_ge(const["loaded"], const["count"])
                    for g in range(NC):
                        if g >= 2:
                            pe.wait_ge(xT_ready, g - 1)
                        for k in range(4):
                            ins = nc.tensor.transpose(turned[:, g % 2, k * P:(k + 1) * P], x_tok[:, 4 * g + k],
                                                      ident[:])
                        ins.then_inc(turn_done, 1)
                    pe.wait_ge(w_loaded, 7 * 16)
                    for ct in range(4):
                        if ct == 2:
                            for t in range(T):
                                if t >= 2:
                                    pe.wait_ge(z_read, t - 1)
                                nc.tensor.matmul(zdt[:, t % 2, 0:INNER + HEADS_S], xT[:, t * P:(t + 1) * P], w_zdt[:],
                                                 start=True, stop=True).then_inc(zdt_done, 1)
                        for c in range(NC):
                            n = ct * NC + c
                            pe.wait_ge(xT_ready, c + 1)
                            if n >= 4:
                                pe.wait_ge(raw_ready, n - 3)
                            nc.tensor.matmul(proj[:, n % 4], w_xbc[:, ct * P:(ct + 1) * P],
                                             xT[:, c * CH:(c + 1) * CH], start=True, stop=True).then_inc(proj_done, 1)

                @block.scalar
                def _(act):
                    for g in range(NC):
                        act.wait_ge(turn_done, g + 1)
                        nc.scalar.activation(xT[:, g * CH:(g + 1) * CH], turned[:, g % 2], ACT.Copy)\
                            .then_inc(xT_ready, 1)

                    def silu(ct):
                        act.wait_ge(conv_done, ct + 1)
                        nc.scalar.activation(xbc[:, ct], xbc[:, ct], ACT.Silu, bias=conv_b[:, ct:ct + 1])

                    for ct in range(4):
                        if ct == 2:
                            for t in range(T):
                                act.wait_ge(zdt_done, t + 1)
                                nc.scalar.activation(dt[:, t], zdt[:, t % 2, INNER:INNER + HEADS_S], ACT.Copy)
                                nc.scalar.activation(gate[:, t], zdt[:, t % 2, 0:INNER], ACT.Silu).then_inc(z_read, 1)
                        if ct >= 2:
                            act.wait_ge(conv_done, ct - 1)
                        for c in range(NC):
                            n = ct * NC + c
                            act.wait_ge(proj_done, n + 1)
                            nc.scalar.activation(raw[:, ct % 2, TAPS - 1 + c * CH:TAPS - 1 + (c + 1) * CH],
                                                 proj[:, n % 4], ACT.Copy).then_inc(raw_ready, 1)
                        if ct:
                            silu(ct - 1)
                    silu(3)

                @block.vector
                def _(dve):
                    link = Chain(dve, order)
                    dve.wait_ge(pads, 1)
                    dve.wait_ge(w_loaded, 7 * 16)
                    for ct in range(4):
                        dve.wait_ge(raw_ready, NC * (ct + 1))
                        link(nc.vector.tensor_scalar(xbc[:, ct], raw[:, ct % 2, 0:S], conv_w[:, ct, 0:1], None,
                                                     ALU.mult))
                        for k in range(1, TAPS):
                            ins = nc.vector.scalar_tensor_tensor(out=xbc[:, ct], in0=raw[:, ct % 2, k:k + S],
                                                                 scalar=conv_w[:, ct, k:k + 1], in1=xbc[:, ct],
                                                                 op0=ALU.mult, op1=ALU.add)
                            if k < TAPS - 1:
                                link(ins)
                        ins.then_inc(conv_done, 1)

        DECAY_MIN = -200.0
        HT = T * HEADS_S
        grow = sp.sb("grow", [P, 3, HT])
        dt_after = sp.sb("dt_after", [P, T, HEADS_S])
        with Space(nc, "ssb") as sb_:
            size = sb_.sb("size", [P, T, HEADS_S])
            top = sb_.sb("top", [P, T, HEADS_S])
            a_exp = sb_.sb("a_exp", [P, HEADS_S])
            e = sb_.sb("e", [P, T, HEADS_S])
            u = sb_.sb("u", [P, T, HEADS_S])
            lu = sb_.sb("lu", [P, T, HEADS_S])
            sums = sb_.ps("sums", [P, CH])
            d_v, d_a, order, sums_done, grown = (sb_.sem("d_v"), sb_.sem("d_a"), sb_.sem("order"),
                                                 sb_.sem("sums_done"), sb_.sem("grown"))
            with nc.Block() as block:

                @block.vector
                def _(dve):
                    link = Chain(dve, order)
                    link(nc.vector.tensor_tensor(dt[:], dt[:], dt_bias.unsqueeze(1).broadcast_to([P, T, HEADS_S]),
                                                 ALU.add))
                    link(nc.vector.scalar_tensor_tensor(out=size[:], in0=dt[:], scalar=-1.0, in1=dt[:], op0=ALU.mult,
                                                        op1=ALU.max))
                    nc.vector.tensor_scalar(top[:], dt[:], 0.0, None, ALU.max).then_inc(d_v, 1)
                    dve.wait_ge(d_a, 2)
                    link(nc.vector.tensor_scalar(u[:], e[:], 1.0, None, ALU.add))
                    nc.vector.scalar_tensor_tensor(out=e[:], in0=u[:], scalar=-1.0, in1=e[:], op0=ALU.add,
                                                   op1=ALU.subtract).then_inc(d_v, 1)
                    dve.wait_ge(d_a, 3)
                    dve.wait_ge(d_v, 2)
                    link(nc.vector.tensor_tensor(lu[:], lu[:], e[:], ALU.subtract))
                    link(nc.vector.tensor_tensor(dt[:], top[:], lu[:], ALU.add))
                    link(nc.vector.tensor_tensor(decay[:], dt[:],
                                                 a_exp[:].unsqueeze(1).broadcast_to([P, T, HEADS_S]), ALU.mult))
                    nc.vector.tensor_scalar(decay[:], decay[:], -1.0, DECAY_MIN, ALU.mult, ALU.max).then_inc(d_v, 1)
                    dve.wait_ge(grown, 1)
                    nc.vector.tensor_tensor(dt_after[:], dt[:], grow[:, 1].rearrange("p (t h) -> p t h", h=HEADS_S),
                                            ALU.mult)
                    for k in range(2):
                        nc.vector.tensor_scalar(w_out[:, k], w_out[:, k], norm_w[:, k:k + 1], None, ALU.mult)

                @block.scalar
                def _(act):
                    nc.scalar.activation(a_exp[:], a_log, ACT.Exp).then_inc(d_a, 1)
                    act.wait_ge(d_v, 1)
                    nc.scalar.activation(e[:], size[:], ACT.Exp, scale=-1.0).then_inc(d_a, 1)
                    act.wait_ge(d_v, 2)
                    nc.scalar.activation(lu[:], u[:], ACT.Ln).then_inc(d_a, 1)
                    act.wait_ge(sums_done, 1)
                    nc.scalar.activation(grow[:], sums[:, 0:3 * HT].rearrange("p (k n) -> p k n", k=3), ACT.Exp)\
                        .then_inc(grown, 1)

                @block.tensor
                def _(pe):
                    pe.wait_ge(d_v, 3)
                    flat = decay[:].rearrange("p t h -> p (t h)")
                    for k, mask in enumerate((upto, after, ones)):
                        ins = nc.tensor.matmul(sums[:, k * HT:(k + 1) * HT], mask[:], flat, start=True, stop=True)
                    ins.then_inc(sums_done, 1)

        grow_upto = grow[:, 0].rearrange("p (t h) -> p t h", h=HEADS_S)
        grow_all = grow[:, 2].rearrange("p (t h) -> p t h", h=HEADS_S)

        def per_head(ap, width=HEAD_S):
            return ap.unsqueeze(2).broadcast_to([P, HEADS_S, width])

        with Space(nc, "ssc") as sc:
            xb = sc.sb("xb", [P, 2, 3 * P])
            steps = sc.sb("steps", [P, 2, HP])
            fade = sc.sb("fade", [P, 2, HP])
            gram = sc.sb("gram", [P, 2, P])
            mix = sc.sb("mix", [P, 2, HP])
            x_dt = sc.sb("x_dt", [P, 2, INNER])
            x_st = sc.sb("x_st", [P, 2, INNER])
            x_sk = sc.sb("x_sk", [P, 2, INNER])
            state = sc.sb("state", [P, 2, INNER])
            y = sc.sb("y", [P, INNER])
            turned = sc.ps("turned", [P, 2, CH])
            between = sc.ps("between", [P, 2, CH])
            y_ps = sc.ps("y_ps", [P, 2, CH])
            gs_ps = sc.ps("gs_ps", [P, CH])
            st_ps = sc.ps("st_ps", [P, CH])
            names = ["steps_ready", "front", "xb_ready", "fade_ready", "gram_ready", "mix_ready", "x_ready",
                     "y_done", "st_done", "state_ready", "y_read", "dve", "gated"]
            m = {n: sc.sem(n) for n in names}
            h4 = "p (h q) -> p h q"

            with nc.Block() as block:

                @block.tensor
                def _(pe):
                    def front(c):
                        cols = slice(c * P, (c + 1) * P)
                        if c >= 2:
                            pe.wait_ge(m["xb_ready"], c - 1)
                            pe.wait_ge(m["fade_ready"], c - 1)
                        for k in range(3):
                            nc.tensor.transpose(turned[:, c % 2, k * P:(k + 1) * P], xbc[:, k, cols], ident[:])
                        if c >= 1:
                            pe.wait_ge(m["gram_ready"], c)
                        nc.tensor.matmul(gs_ps[:, 0:P], xbc[:, 2, cols], xbc[:, 3, cols], start=True, stop=True)
                        pe.wait_ge(m["steps_ready"], c + 1)
                        nc.tensor.matmul(between[:, c % 2], after[:], steps[:, c % 2], start=True, stop=True)\
                            .then_inc(m["front"], 1)

                    front(0)
                    for c in range(T):
                        if c + 1 < T:
                            front(c + 1)
                        pe.wait_ge(m["mix_ready"], c + 1)
                        pe.wait_ge(m["x_ready"], c + 1)
                        if c >= 2:
                            pe.wait_ge(m["y_read"], c - 1)
                        for h in range(HEADS_S):
                            nc.tensor.matmul(y_ps[:, c % 2, h * HEAD_S:(h + 1) * HEAD_S],
                                             mix[:, c % 2, h * P:(h + 1) * P],
                                             x_dt[:, c % 2, h * HEAD_S:(h + 1) * HEAD_S], start=True, stop=True)
                        pe.wait_ge(m["state_ready"], c + 1)
                        nc.tensor.matmul(y_ps[:, c % 2, INNER:], xbc[:, 3, c * P:(c + 1) * P], state[:, c % 2],
                                         start=True, stop=True).then_inc(m["y_done"], 1)
                        nc.tensor.matmul(st_ps[:, 0:INNER], xb[:, c % 2, INNER:], x_st[:, c % 2],
                                         start=True, stop=True).then_inc(m["st_done"], 1)

                @block.gpsimd
                def _(pool):
                    def steps_of(c):
                        if c >= 2:
                            pool.wait_ge(m["front"], c - 1)
                        nc.gpsimd.tensor_tensor(steps[:, c % 2].rearrange(h4, h=HEADS_S),
                                                upto[:].unsqueeze(1).broadcast_to([P, HEADS_S, P]),
                                                per_head(decay[:, c], P), ALU.mult).then_inc(m["steps_ready"], 1)

                    nc.gpsimd.memset(state[:, 0], 0.0).then_inc(m["state_ready"], 1)
                    steps_of(0)
                    for c in range(T):
                        if c + 1 < T:
                            steps_of(c + 1)
                        pool.wait_ge(m["xb_ready"], c + 1)
                        if c >= 2:
                            pool.wait_ge(m["st_done"], c - 1)
                            pool.wait_ge(m["gated"], c - 1)
                        x = xb[:, c % 2, 0:INNER].rearrange(h4, h=HEADS_S)
                        for dst, by in ((x_dt, dt[:, c]), (x_sk, skip), (x_st, dt_after[:, c])):
                            ins = nc.gpsimd.tensor_tensor(dst[:, c % 2].rearrange(h4, h=HEADS_S), x, per_head(by),
                                                          ALU.mult)
                        ins.then_inc(m["x_ready"], 1)

                @block.scalar
                def _(act):
                    for c in range(T):
                        act.wait_ge(m["front"], c + 1)
                        if c >= 2:
                            act.wait_ge(m["st_done"], c - 1)
                            act.wait_ge(m["x_ready"], c - 1)
                        nc.scalar.activation(xb[:, c % 2], turned[:, c % 2, 0:3 * P], ACT.Copy)\
                            .then_inc(m["xb_ready"], 1)
                        if c >= 2:
                            act.wait_ge(m["mix_ready"], c - 1)
                        nc.scalar.activation(fade[:, c % 2], between[:, c % 2], ACT.Exp).then_inc(m["fade_ready"], 1)

                @block.vector
                def _(dve):
                    link = Chain(dve, m["dve"])

                    def mixes(c):
                        dve.wait_ge(m["front"], c + 1)
                        nc.vector.tensor_tensor(gram[:, c % 2], gs_ps[:, 0:P], upto[:], ALU.mult)\
                            .then_inc(m["gram_ready"], 1)
                        dve.wait_ge(m["gram_ready"], c + 1)
                        dve.wait_ge(m["fade_ready"], c + 1)
                        if c >= 2:
                            dve.wait_ge(m["y_done"], c - 1)
                        nc.vector.tensor_tensor(mix[:, c % 2].rearrange(h4, h=HEADS_S),
                                                fade[:, c % 2].rearrange(h4, h=HEADS_S),
                                                gram[:, c % 2].unsqueeze(1).broadcast_to([P, HEADS_S, P]), ALU.mult)\
                            .then_inc(m["mix_ready"], 1)

                    mixes(0)
                    for c in range(T):
                        if c + 1 < T:
                            mixes(c + 1)
                        dve.wait_ge(m["state_ready"], c + 1)
                        nxt = state[:, (c + 1) % 2]
                        if c >= 1:
                            dve.wait_ge(m["y_done"], c)
                        link(nc.vector.tensor_tensor(nxt.rearrange(h4, h=HEADS_S),
                                                     state[:, c % 2].rearrange(h4, h=HEADS_S),
                                                     per_head(grow_all[:, c]), ALU.mult))
                        dve.wait_ge(m["st_done"], c + 1)
                        nc.vector.tensor_tensor(nxt, nxt, st_ps[:, 0:INNER], ALU.add).then_inc(m["state_ready"], 1)
                        dve.wait_ge(m["y_done"], c + 1)
                        dve.wait_ge(m["x_ready"], c + 1)
                        link(nc.vector.tensor_tensor(y[:].rearrange(h4, h=HEADS_S),
                                                     y_ps[:, c % 2, INNER:].rearrange(h4, h=HEADS_S),
                                                     per_head(grow_upto[:, c]), ALU.mult))
                        nc.vector.tensor_tensor(y[:], y[:], y_ps[:, c % 2, 0:INNER], ALU.add).then_inc(m["y_read"], 1)
                        dve.wait_ge(m["y_read"], c + 1)
                        link(nc.vector.tensor_tensor(y[:], y[:], x_sk[:, c % 2], ALU.add))
                        nc.vector.tensor_tensor(gate[:, c], gate[:, c], y[:], ALU.mult).then_inc(m["gated"], 1)

        with Space(nc, "ssd") as sd:
            square = sd.sb("square", [P, INNER])
            total = sd.sb("total", [P, T])
            rms = sd.sb("rms", [P, T])
            yT = sd.sb("yT", [P, 2, INNER])
            eps = sd.sb("eps", [P, 1])
            turned = sd.ps("turned", [P, 2, CH])
            prod = sd.ps("prod", [P, 2, CH])
            m = {n: sd.sem(n) for n in ("turn_done", "yT_ready", "prod_done", "out_ready", "total_ready", "rms_ready",
                                        "order", "eps_ready", "sq")}
            with nc.Block() as block:

                @block.tensor
                def _(pe):
                    def turn(t):
                        if t >= 2:
                            pe.wait_ge(m["yT_ready"], t - 1)
                        for k in range(2):
                            ins = nc.tensor.transpose(turned[:, t % 2, k * P:(k + 1) * P], gate[:, t, k * P:(k + 1) * P],
                                                      ident[:])
                        ins.then_inc(m["turn_done"], 1)

                    turn(0)
                    for t in range(T):
                        if t + 1 < T:
                            turn(t + 1)
                        pe.wait_ge(m["yT_ready"], t + 1)
                        if t >= 2:
                            pe.wait_ge(m["out_ready"], t - 1)
                        for k in range(2):
                            ins = nc.tensor.matmul(prod[:, t % 2, 0:D], yT[:, t % 2, k * P:(k + 1) * P], w_out[:, k],
                                                   start=(k == 0), stop=(k == 1))
                        ins.then_inc(m["prod_done"], 1)

                @block.scalar
                def _(act):
                    for t in range(T):
                        if t:
                            act.wait_ge(m["sq"], t)
                        nc.scalar.activation(square[:], gate[:, t], ACT.Square, accum_out=total[:, t:t + 1])\
                            .then_inc(m["sq"], 1)
                    act.wait_ge(m["sq"], T)
                    act.wait_ge(m["eps_ready"], 1)
                    nc.scalar.activation(rms[:], total[:], ACT.Sqrt, bias=eps[:, 0:1], scale=1.0 / INNER)\
                        .then_inc(m["total_ready"], 1)
                    for t in range(T):
                        act.wait_ge(m["turn_done"], t + 1)
                        if t >= 2:
                            act.wait_ge(m["prod_done"], t - 1)
                        nc.scalar.activation(yT[:, t % 2], turned[:, t % 2, 0:INNER], ACT.Copy)\
                            .then_inc(m["yT_ready"], 1)

                @block.vector
                def _(dve):
                    nc.vector.memset(eps[:], EPS).then_inc(m["eps_ready"], 1)
                    dve.wait_ge(m["total_ready"], 1)
                    nc.vector.reciprocal(rms[:], rms[:]).then_inc(m["rms_ready"], 1)
                    dve.wait_ge(m["rms_ready"], 1)
                    for t in range(T):
                        dve.wait_ge(m["prod_done"], t + 1)
                        nc.vector.scalar_tensor_tensor(out=out_tok[:, t], in0=prod[:, t % 2, 0:D],
                                                       scalar=rms[:, t:t + 1], in1=x_tok[:, t], op0=ALU.mult,
                                                       op1=ALU.add).then_inc(m["out_ready"], 1)

        normalise(nc, "ssn", out_tok, out_tok, ln_w, ln_b, x_tok)
    normalise(nc, "n0", out_tok, out_tok)
    clear_semaphores(nc)



DEPTH = 2
HEADS_L, HEAD_L, WINDOW = 8, 64, 64
INNER_L = HEADS_L * HEAD_L
PAIRS = HEADS_L // 2
KEYS = WINDOW + P
HIDDEN = 341
HID_T = 3
NORM_MIN = 1e-12
MASKED = -1e30


def attention_layer(nc, dram, const, tables, layer, src, dst):
    with Space(nc, f"la{layer}") as sp:
        wqkv = sp.sb("wqkv", [P, 3 * INNER_L])
        wrot = sp.sb("wrot", [P, 2 * INNER_L])
        scales = sp.sb("scales", [P, 4])
        wo = sp.sb("wo", [P, PAIRS, D])
        qkT = sp.sb("qkT", [P, 2 * PAIRS, S])
        loaded = sp.sem("loaded")
        v = sp.sb("v", [P, T, INNER_L])
        project_qkv(nc, dram, const, tables, layer, src, wqkv, wrot, scales, wo, qkT, v, loaded)
        attend_local(nc, const, layer, tables["band"], qkT, v, wo, src, dst)
    feed_forward(nc, dram, const, layer, dst)


def project_qkv(nc, dram, const, tables, layer, src, wqkv, wrot, scales, wo, qkT, v, loaded):
    ident, head_sum, head_copy = const["ident"], tables["head_sum"], tables["head_copy"]
    F = 2 * PAIRS
    N = F * NC
    LAG = F + 3
    LIFT = 2.0 ** 20
    with Space(nc, f"lp{layer}") as s:
        hT = s.sb("hT", [P, S + 1])
        square = s.sb("square", [P, 2, CH])
        rotated = s.sb("rotated", [P, 2, CH])
        turned_by = s.sb("turned_by", [P, 2, CH])
        norms = s.sb("norms", [64, S])
        parts = s.sb("parts", [64, S], F32R)
        unit = s.sb("unit", [64, 1])
        shared = s.ps("shared", [P, 2, CH])
        plain = s.ps("plain", [P, 2, CH])
        swapped = s.ps("swapped", [P, 2, CH])
        sums = s.ps("sums", [P, 1, CH])
        v_ps = s.ps("v_ps", [P, 1, CH])
        m = {n: s.sem(n) for n in ("turn_done", "low_ready", "high_ready", "zeroed", "proj_done", "square_ready",
                                   "cos_done", "sin_done", "rot_ready", "sums_done", "norms_ready", "v_done",
                                   "v_read", "unit_set", "ln_ready", "inv_ready", "coarse_ready", "parts_ready",
                                   "spread_done", "scaled")}

        def cols(c):
            return slice(c * CH, (c + 1) * CH)

        with nc.Block() as block:

            @block.sync
            def _(sync):
                for d, n in ((wqkv, f"wqkv{layer}"), (wrot, f"wrot{layer}"), (scales, f"scales{layer}"),
                             (wo, f"wo{layer}")):
                    sync.dma_start(d[:], dram[n]).then_inc(loaded, 16)

            @block.tensor
            def _(pe):
                for g in range(NC):
                    if g >= 2:
                        pe.wait_ge(m["low_ready"], g - 1)
                        pe.wait_ge(m["high_ready"], g - 1)
                    for k in range(4):
                        ins = nc.tensor.transpose(shared[:, g % 2, k * P:(k + 1) * P], src[:, 4 * g + k], ident[:])
                    ins.then_inc(m["turn_done"], 1)
                pe.wait_ge(loaded, 4 * 16)
                pe.wait_ge(tables["loaded"], tables["count"])
                pe.wait_ge(m["zeroed"], 1)

                def sum_squares(n):
                    c, f = divmod(n, F)
                    pe.wait_ge(m["square_ready"], n + 1)
                    if f == 0 and c >= 1:
                        pe.wait_ge(m["norms_ready"], c)
                    nc.tensor.matmul(sums[0:64, 0], head_sum[:, f], square[:, n % 2], start=(f == 0),
                                     stop=(f == F - 1)).then_inc(m["sums_done"], 1)

                def spread(n):
                    c, f = divmod(n, F)
                    pe.wait_ge(m["parts_ready"], c + 1)
                    if n >= 2:
                        pe.wait_ge(m["scaled"], n - 1)
                    nc.tensor.matmul(shared[:, n % 2], head_copy[:, f], parts[:, cols(c)], start=True, stop=True)\
                        .then_inc(m["spread_done"], 1)

                for n in range(N + LAG):
                    c, f = divmod(n, F)
                    if n < N:
                        if f == 0:
                            last = min(c + 2, NC)
                            pe.wait_ge(m["low_ready"], last)
                            pe.wait_ge(m["high_ready"], last)
                        if n >= 2:
                            pe.wait_ge(m["cos_done"], n - 1)
                            pe.wait_ge(m["sin_done"], n - 1)
                        nc.tensor.matmul(plain[:, n % 2], wqkv[:, f * P:(f + 1) * P], hT[:, cols(c)], start=True,
                                         stop=True)
                        nc.tensor.matmul(swapped[:, n % 2], wrot[:, f * P:(f + 1) * P], hT[:, cols(c)], start=True,
                                         stop=True).then_inc(m["proj_done"], 1)
                    if 1 <= n <= N:
                        sum_squares(n - 1)
                    if n < N and n % 2:
                        t = n // 2
                        if t >= 1:
                            pe.wait_ge(m["v_read"], t)
                        nc.tensor.matmul(v_ps[:, 0], hT[:, t * P:(t + 1) * P], wqkv[:, 2 * INNER_L:], start=True,
                                         stop=True).then_inc(m["v_done"], 1)
                    if n >= LAG:
                        spread(n - LAG)

            @block.scalar
            def _(act):
                for g in range(NC):
                    act.wait_ge(m["turn_done"], g + 1)
                    nc.scalar.activation(hT[0:64, cols(g)], shared[0:64, g % 2], ACT.Copy).then_inc(m["low_ready"], 1)

                def inverse(c):
                    act.wait_ge(m["norms_ready"], c + 1)
                    nc.scalar.activation(norms[:, cols(c)], norms[:, cols(c)], ACT.Ln, scale=LIFT)\
                        .then_inc(m["ln_ready"], 1)
                    act.wait_ge(m["unit_set"], 1)
                    act.wait_ge(m["ln_ready"], c + 1)
                    nc.scalar.activation(norms[:, cols(c)], norms[:, cols(c)], ACT.Exp, scale=-0.5,
                                         bias=unit[:, 0:1]).then_inc(m["inv_ready"], 1)

                for n in range(N + 1):
                    if n < N:
                        act.wait_ge(m["proj_done"], n + 1)
                        if n >= 2:
                            act.wait_ge(m["sums_done"], n - 1)
                        nc.scalar.activation(square[:, n % 2], plain[:, n % 2], ACT.Square)\
                            .then_inc(m["square_ready"], 1)
                        if n % 2:
                            t = n // 2
                            act.wait_ge(m["v_done"], t + 1)
                            nc.scalar.activation(v[:, t], v_ps[:, 0], ACT.Copy).then_inc(m["v_read"], 1)
                    if n and n % F == 0:
                        inverse(n // F - 1)

            @block.vector
            def _(dve):
                nc.vector.memset(unit[:], float(0.5 * np.log(LIFT))).then_inc(m["unit_set"], 1)
                nc.vector.memset(hT[64:P, 0:1], 0.0).then_inc(m["zeroed"], 1)
                for g in range(NC):
                    dve.wait_ge(m["turn_done"], g + 1)
                    nc.vector.tensor_copy(hT[64:P, g * CH + 1:(g + 1) * CH + 1], shared[64:P, g % 2])\
                        .then_inc(m["high_ready"], 1)

                def split(c):
                    dve.wait_ge(m["inv_ready"], c + 1)
                    nc.vector.tensor_copy(parts[:, cols(c)], norms[:, cols(c)]).then_inc(m["coarse_ready"], 1)
                    dve.wait_ge(m["coarse_ready"], c + 1)
                    nc.vector.tensor_tensor(parts[32:64, cols(c)], norms[32:64, cols(c)],
                                            parts[32:64, cols(c)].bitcast(F32), ALU.subtract)\
                        .then_inc(m["parts_ready"], 1)

                for n in range(N + LAG):
                    c, f = divmod(n, F)
                    k = f // PAIRS
                    if n < N:
                        dve.wait_ge(m["square_ready"], n + 1)
                        if n >= 2:
                            dve.wait_ge(m["rot_ready"], n - 1)
                        nc.vector.scalar_tensor_tensor(out=rotated[:, n % 2], in0=plain[:, n % 2],
                                                       scalar=scales[:, 2 * k:2 * k + 1],
                                                       in1=tables["cos"][:, k, cols(c)], op0=ALU.mult, op1=ALU.mult)\
                            .then_inc(m["cos_done"], 1)
                        nc.vector.scalar_tensor_tensor(out=turned_by[:, n % 2], in0=swapped[:, n % 2],
                                                       scalar=scales[:, 2 * k + 1:2 * k + 2],
                                                       in1=tables["sin"][:, k, cols(c)], op0=ALU.mult, op1=ALU.mult)\
                            .then_inc(m["sin_done"], 1)
                        if f == F - 1:
                            dve.wait_ge(m["sums_done"], n + 1)
                            nc.vector.tensor_scalar(norms[:, cols(c)], sums[0:64, 0], NORM_MIN ** 2, None, ALU.max)\
                                .then_inc(m["norms_ready"], 1)
                    if F < n < N + F and n % F == 1:
                        split(n // F - 1)
                    if n >= LAG:
                        w = n - LAG
                        cw, fw = divmod(w, F)
                        dve.wait_ge(m["spread_done"], w + 1)
                        dve.wait_ge(m["rot_ready"], w + 1)
                        q = qkT[:, fw, cols(cw)]
                        nc.vector.tensor_tensor(q, q, shared[:, w % 2], ALU.mult).then_inc(m["scaled"], 1)

            @block.gpsimd
            def _(pool):
                for n in range(N):
                    c, f = divmod(n, F)
                    pool.wait_ge(m["cos_done"], n + 1)
                    pool.wait_ge(m["sin_done"], n + 1)
                    nc.gpsimd.tensor_tensor(qkT[:, f, cols(c)], rotated[:, n % 2], turned_by[:, n % 2], ALU.add)\
                        .then_inc(m["rot_ready"], 1)


def attend_local(nc, const, layer, band, qkT, v, wo, src, dst):
    ident = const["ident"]
    HH = HEADS_L // 2
    U = 2 * T
    W = 2 * P
    SCALE = 8.0
    with Space(nc, f"lt{layer}") as s:
        probs = s.sb("probs", [P, 2, HH, W])
        before = s.sb("before", [P, 2, HH * P])
        own = s.sb("own", [P, 2, HH * P])
        most = s.sb("most", [P, 2, HH])
        bias = s.sb("bias", [P, 2, HH])
        total = s.sb("total", [P, 2, HH])
        sim = s.ps("sim", [P, 2, 2, CH])
        own_ps = s.ps("own_ps", [P, CH])
        before_ps = s.ps("before_ps", [P, CH])
        oT_ps = s.ps("oT_ps", [P, CH])
        prod = s.ps("prod", [P, CH])
        names = ["zeroed", "sim_done", "max_ready", "bias_ready", "exp_done", "recip_ready", "probs_ready",
                 "turn_done", "own_ready", "before_ready", "o_done", "oT_ready", "prod_done", "added"]
        m = {n: s.sem(n) for n in names}

        def first_key(u):
            return WINDOW if u < 2 else 0

        with nc.Block() as block:

            @block.tensor
            def _(pe):
                def front(u):
                    t, half = divmod(u, 2)
                    lo = first_key(u)
                    if u >= 2:
                        pe.wait_ge(m["exp_done"], u - 1)
                    for b in range(2):
                        bank = sim[:, u % 2, b]
                        rows = slice(b * 64, b * 64 + 64)
                        nc.tensor.matmul(bank[:, 0:2 * KEYS], const["ident16"][:], band[:], start=True, stop=False)
                        for k in range(2):
                            pair = 2 * half + k
                            ins = nc.tensor.matmul(bank[:, k * KEYS + lo:(k + 1) * KEYS],
                                                   qkT[rows, pair, t * P:(t + 1) * P],
                                                   qkT[rows, PAIRS + pair, t * P - WINDOW + lo:(t + 1) * P],
                                                   start=False, stop=(k == 1))
                    ins.then_inc(m["sim_done"], 1)

                def turn(u):
                    pe.wait_ge(m["probs_ready"], u + 1)
                    if u >= 1:
                        pe.wait_ge(m["own_ready"], u)
                        pe.wait_ge(m["before_ready"], u)
                    for h in range(HH):
                        nc.tensor.transpose(before_ps[:, h * P:(h + 1) * P], probs[:, u % 2, h, 0:P], ident[:])
                        ins = nc.tensor.transpose(own_ps[:, h * P:(h + 1) * P], probs[:, u % 2, h, P:], ident[:])
                    ins.then_inc(m["turn_done"], 1)

                def values(u):
                    t, half = divmod(u, 2)
                    pe.wait_ge(m["own_ready"], u + 1)
                    pe.wait_ge(m["before_ready"], u + 1)
                    if u >= 1:
                        pe.wait_ge(m["oT_ready"], u)
                    for k in range(2):
                        for b in range(2):
                            slot = slice((2 * b + k) * P, (2 * b + k + 1) * P)
                            head = half * HH + 2 * k + b
                            channels = slice(head * HEAD_L, (head + 1) * HEAD_L)
                            out = oT_ps[b * 64:b * 64 + 64, k * P:(k + 1) * P]
                            ins = nc.tensor.matmul(out, v[:, t, channels], own[:, u % 2, slot], start=True,
                                                   stop=(t == 0))
                            if t:
                                ins = nc.tensor.matmul(out, v[:, t - 1, channels], before[:, u % 2, slot],
                                                       start=False, stop=True)
                    ins.then_inc(m["o_done"], 1)

                def output(t):
                    pe.wait_ge(m["oT_ready"], 2 * t + 2)
                    if t >= 1:
                        pe.wait_ge(m["added"], t)
                    for k in range(PAIRS):
                        ins = nc.tensor.matmul(prod[:, 0:D], qkT[:, k, t * P:(t + 1) * P], wo[:, k], start=(k == 0),
                                               stop=(k == PAIRS - 1))
                    ins.then_inc(m["prod_done"], 1)

                front(0)
                for u in range(U + 3):
                    if u + 1 < U:
                        front(u + 1)
                    if 1 <= u <= U:
                        values(u - 1)
                    if u >= 3 and u % 2:
                        output((u - 3) // 2)
                    if u < U:
                        turn(u)

            @block.scalar
            def _(act):
                act.wait_ge(m["zeroed"], 1)

                def exps(u):
                    lo = first_key(u)
                    act.wait_ge(m["bias_ready"], u + 1)
                    for b in range(2):
                        for k in range(2):
                            slot = 2 * b + k
                            ins = nc.scalar.activation(probs[:, u % 2, slot, WINDOW + lo:],
                                                       sim[:, u % 2, b, k * KEYS + lo:(k + 1) * KEYS], ACT.Exp,
                                                       scale=SCALE, bias=bias[:, u % 2, slot:slot + 1],
                                                       accum_out=total[:, u % 2, slot:slot + 1])
                    ins.then_inc(m["exp_done"], 1)

                exps(0)
                for u in range(U + 1):
                    if u >= 1:
                        act.wait_ge(m["turn_done"], u)
                        if u >= 3:
                            act.wait_ge(m["o_done"], u - 2)
                        nc.scalar.activation(own[:, (u - 1) % 2], own_ps[:], ACT.Copy).then_inc(m["own_ready"], 1)
                    if u + 1 < U:
                        exps(u + 1)
                    if u >= 1:
                        t, half = divmod(u - 1, 2)
                        act.wait_ge(m["o_done"], u)
                        nc.scalar.activation(qkT[:, 2 * half:2 * half + 2, t * P:(t + 1) * P],
                                             oT_ps[:, 0:2 * P].rearrange("p (k n) -> p k n", k=2), ACT.Copy)\
                            .then_inc(m["oT_ready"], 1)

            @block.vector
            def _(dve):
                nc.vector.memset(probs[:], 0.0).then_inc(m["zeroed"], 1)

                def biases(u):
                    dve.wait_ge(m["sim_done"], u + 1)
                    lo = first_key(u)
                    scores = sim[:, u % 2, :, 0:2 * KEYS].rearrange("p b (k n) -> p b k n", k=2)[:, :, :, lo:]
                    nc.vector.tensor_reduce(most[:, u % 2].rearrange("p (b k) -> p b k", b=2), scores, AX.X,
                                            ALU.max).then_inc(m["max_ready"], 1)
                    dve.wait_ge(m["max_ready"], u + 1)
                    nc.vector.tensor_scalar(bias[:, u % 2], most[:, u % 2], -SCALE, None, ALU.mult)\
                        .then_inc(m["bias_ready"], 1)

                def divide(u):
                    dve.wait_ge(m["exp_done"], u + 1)
                    nc.vector.reciprocal(total[:, u % 2], total[:, u % 2]).then_inc(m["recip_ready"], 1)
                    dve.wait_ge(m["recip_ready"], u + 1)
                    p = probs[:, u % 2, :, WINDOW:]
                    nc.vector.tensor_tensor(p, p, total[:, u % 2].unsqueeze(2).broadcast_to([P, HH, KEYS]),
                                            ALU.mult).then_inc(m["probs_ready"], 1)

                biases(0)
                for u in range(U + 3):
                    if 1 <= u <= U:
                        dve.wait_ge(m["turn_done"], u)
                        if u >= 3:
                            dve.wait_ge(m["o_done"], u - 2)
                        nc.vector.tensor_copy(before[:, (u - 1) % 2], before_ps[:]).then_inc(m["before_ready"], 1)
                    if u < U:
                        divide(u)
                    if u + 1 < U:
                        biases(u + 1)
                    if u >= 3 and u % 2:
                        t = (u - 3) // 2
                        dve.wait_ge(m["prod_done"], t + 1)
                        nc.vector.tensor_tensor(dst[:, t], prod[:, 0:D], src[:, t], ALU.add).then_inc(m["added"], 1)


def feed_forward(nc, dram, const, layer, x):
    ident = const["ident"]
    with Space(nc, f"ff{layer}") as sp:
        h = sp.sb("h", [P, T, D])
        w1 = sp.sb("w1", [P, 2, HID_T * P])
        b1 = sp.sb("b1", [P, 2, HID_T])
        w2 = sp.sb("w2", [P, HID_T, D])
        b2 = sp.sb("b2", [P, D])
        norm = sp.sb("norm", [P, 2])
        hT = sp.sb("hT", [P, S])
        hidden = sp.sb("hidden", [P, HID_T, S])
        gelu = sp.sb("gelu", [P, 2, CH])
        stats = sp.sb("stats", [P, T, 6])
        moments = sp.sb("moments", [P, T, 2])
        spread = sp.sb("spread", [P, T])
        eps = sp.sb("eps", [P, 1])
        loaded = sp.sem("loaded")
        with Space(nc, f"fp{layer}") as s:
            turned = s.ps("turned", [P, 2, CH])
            a_ps = s.ps("a_ps", [P, 2, CH])
            g_ps = s.ps("g_ps", [P, 2, CH])
            prod = s.ps("prod", [P, 2, CH])
            m = {n: s.sem(n) for n in ("turn_done", "hT_ready", "a_done", "g_done", "gelu_ready", "hidden_ready",
                                       "prod_done", "added", "biased", "half_ready", "eps_set", "stats_ready",
                                       "var_ready", "std_ready", "recip_ready", "h_ready")}
            shifted = [s.sem(f"shifted{g}") for g in range(NC)]
            with nc.Block() as block:

                @block.sync
                def _(sync):
                    half = slice(D // 2, D)
                    for g in range(NC):
                        lo, hi = 4 * g, 4 * g + 4
                        sync.dma_start(h[1:P, lo:hi, half], x[0:P - 1, lo:hi, half]).then_inc(shifted[g], 16)
                        first = max(lo, 1)
                        sync.dma_start(h[0:1, first:hi, half], x[P - 1:P, first - 1:hi - 1, half])\
                            .then_inc(shifted[g], 16)
                    for d, n in ((w1, "w1"), (b1, "b1"), (w2, "w2"), (b2, "b2"), (norm, "ffn_norm")):
                        sync.dma_start(d[:], dram[f"{n}{layer}"]).then_inc(loaded, 16)

                @block.gpsimd
                def _(pool):
                    nc.gpsimd.memset(h[0:1, 0, D // 2:D], 0.0)
                    nc.gpsimd.tensor_copy(h[:, :, 0:D // 2], x[:, :, 0:D // 2]).then_inc(m["half_ready"], 1)
                    pool.wait_ge(loaded, 5 * 16)
                    for g in range(NC):
                        pool.wait_ge(shifted[g], 32)
                    pool.wait_ge(m["half_ready"], 1)
                    nc.gpsimd.tensor_tensor(x[:], x[:], b2[:].unsqueeze(1).broadcast_to([P, T, D]), ALU.add)\
                        .then_inc(m["biased"], 1)

                @block.tensor
                def _(pe):
                    for g in range(NC):
                        pe.wait_ge(m["h_ready"], g + 1)
                        if g >= 2:
                            pe.wait_ge(m["hT_ready"], g - 1)
                        for k in range(4):
                            ins = nc.tensor.transpose(turned[:, g % 2, k * P:(k + 1) * P], h[:, 4 * g + k], ident[:])
                        ins.then_inc(m["turn_done"], 1)
                    pe.wait_ge(loaded, 5 * 16)

                    def up(n):
                        c, f = divmod(n, HID_T)
                        pe.wait_ge(m["hT_ready"], c + 1)
                        if n >= 2:
                            pe.wait_ge(m["hidden_ready"], n - 1)
                        hc = hT[:, c * CH:(c + 1) * CH]
                        nc.tensor.matmul(g_ps[:, n % 2], w1[:, 1, f * P:(f + 1) * P], hc, start=True, stop=True)\
                            .then_inc(m["g_done"], 1)
                        nc.tensor.matmul(a_ps[:, n % 2], w1[:, 0, f * P:(f + 1) * P], hc, start=True, stop=True)\
                            .then_inc(m["a_done"], 1)

                    def down(t):
                        pe.wait_ge(m["hidden_ready"], HID_T * (t // 4 + 1))
                        if t >= 2:
                            pe.wait_ge(m["added"], t - 1)
                        for f in range(HID_T):
                            ins = nc.tensor.matmul(prod[:, t % 2, 0:D], hidden[:, f, t * P:(t + 1) * P], w2[:, f],
                                                   start=(f == 0), stop=(f == HID_T - 1))
                        ins.then_inc(m["prod_done"], 1)

                    for c in range(NC + 1):
                        if c < NC:
                            for f in range(HID_T):
                                up(c * HID_T + f)
                        if c:
                            for t in range(4 * (c - 1), 4 * c):
                                down(t)

                @block.scalar
                def _(act):
                    act.wait_ge(m["eps_set"], 1)
                    for g in range(NC):
                        tiles = slice(4 * g, 4 * g + 4)
                        act.wait_ge(m["var_ready"], g + 1)
                        nc.scalar.activation(spread[:, tiles], moments[:, tiles, 1], ACT.Sqrt, bias=eps[:, 0:1])\
                            .then_inc(m["std_ready"], 1)
                    for n in range(NC * HID_T):
                        act.wait_ge(m["g_done"], n + 1)
                        if n >= 2:
                            act.wait_ge(m["hidden_ready"], n - 1)
                        f = n % HID_T
                        nc.scalar.activation(gelu[:, n % 2], g_ps[:, n % 2], ACT.Gelu, bias=b1[:, 1, f:f + 1])\
                            .then_inc(m["gelu_ready"], 1)

                @block.vector
                def _(dve):
                    nc.vector.memset(eps[:], EPS).then_inc(m["eps_set"], 1)
                    dve.wait_ge(m["half_ready"], 1)

                    def moments_of(g):
                        dve.wait_ge(shifted[g], 32)
                        for t in range(4 * g, 4 * g + 4):
                            ins = nc.vector.bn_stats(stats[:, t], h[:, t])
                        ins.then_inc(m["stats_ready"], 1)
                        dve.wait_ge(m["stats_ready"], g + 1)
                        for t in range(4 * g, 4 * g + 4):
                            ins = nc.vector.bn_aggr(moments[:, t], stats[:, t])
                        ins.then_inc(m["var_ready"], 1)

                    moments_of(0)
                    for g in range(NC):
                        if g + 1 < NC:
                            moments_of(g + 1)
                        tiles = slice(4 * g, 4 * g + 4)
                        dve.wait_ge(m["std_ready"], g + 1)
                        nc.vector.reciprocal(spread[:, tiles], spread[:, tiles]).then_inc(m["recip_ready"], 1)
                        dve.wait_ge(m["recip_ready"], g + 1)
                        dve.wait_ge(m["var_ready"], g + 1)
                        for t in range(4 * g, 4 * g + 4):
                            ins = nc.vector.tensor_scalar(h[:, t], h[:, t], moments[:, t, 0:1], spread[:, t:t + 1],
                                                          ALU.subtract, ALU.mult)
                        ins.then_inc(m["h_ready"], 1)
                    dve.wait_ge(loaded, 5 * 16)
                    for g in range(NC):
                        dve.wait_ge(m["turn_done"], g + 1)
                        nc.vector.tensor_scalar(hT[:, g * CH:(g + 1) * CH], turned[:, g % 2], norm[:, 0:1],
                                                norm[:, 1:2], ALU.mult, ALU.add).then_inc(m["hT_ready"], 1)

                    def add(t):
                        dve.wait_ge(m["prod_done"], t + 1)
                        dve.wait_ge(m["biased"], 1)
                        nc.vector.tensor_tensor(x[:, t], x[:, t], prod[:, t % 2, 0:D], ALU.add).then_inc(m["added"], 1)

                    for c in range(NC + 1):
                        if c < NC:
                            for f in range(HID_T):
                                n = c * HID_T + f
                                dve.wait_ge(m["gelu_ready"], n + 1)
                                dve.wait_ge(m["a_done"], n + 1)
                                nc.vector.scalar_tensor_tensor(out=hidden[:, f, c * CH:(c + 1) * CH],
                                                               in0=a_ps[:, n % 2], scalar=b1[:, 0, f:f + 1],
                                                               in1=gelu[:, n % 2], op0=ALU.add, op1=ALU.mult)\
                                    .then_inc(m["hidden_ready"], 1)
                        if c:
                            for t in range(4 * (c - 1), 4 * c):
                                add(t)


def local_transformer(nc, dram, const, x, cur):
    with Space(nc, "lt") as sp:
        tables = {"cos": sp.sb("cos", [P, 2, S]), "sin": sp.sb("sin", [P, 2, S]),
                  "band": sp.sb("band", [P, 2 * KEYS], BF16),
                  "head_sum": sp.sb("head_sum", [P, 2 * PAIRS, 64]),
                  "head_copy": sp.sb("head_copy", [64, 2 * PAIRS, P], F32R),
                  "loaded": nc.alloc_semaphore("tables_loaded"), "count": 3 * 16}
        with Space(nc, "lc") as s:
            band32 = s.sb("band32", [P, 2 * KEYS])
            copy32 = s.sb("copy32", [64, 2 * PAIRS, P])
            got = s.sem("got")
            with nc.Block() as block:

                @block.sync
                def _(sync):
                    for n in ("cos", "sin", "head_sum"):
                        sync.dma_start(tables[n][:], dram[n]).then_inc(tables["loaded"], 16)
                    sync.dma_start(band32[:], dram["band"]).then_inc(got, 16)
                    sync.dma_start(copy32[:], dram["head_copy"]).then_inc(got, 16)

                @block.vector
                def _(dve):
                    dve.wait_ge(got, 32)
                    nc.vector.tensor_copy(tables["band"][:], band32[:])
                    nc.vector.tensor_copy(tables["head_copy"][:], copy32[:])
        for layer in range(DEPTH):
            attention_layer(nc, dram, const, tables, layer, x if layer == 0 else cur, cur)
            clear_semaphores(nc)
        with nc.Block() as block:

            @block.vector
            def _(dve):
                nc.vector.tensor_tensor(x[:], x[:], cur[:], ALU.add)
    normalise(nc, "n1", x, x)



HEADS_G, HEAD_G, LATENT = 16, 64, 64
PAIRS_G = HEADS_G // 2
IW = 2 * P
UNITS = S // IW
RT = 4
LATE = 2 * (IW // P)
MERGED = 4


def latent_attention(nc, dram, const, x, acc):
    ident = const["ident"]
    spare = x[:].rearrange("p t d -> p (t d)")
    values = spare[:, 0:T * LATENT].rearrange("p (t c) -> p t c", c=LATENT)
    mixers = spare[:, T * LATENT:2 * T * LATENT].rearrange("p (g n) -> p g n", n=D)
    with Space(nc, "g") as sp:
        c_q = sp.sb("c_q", [P, S], F32R)
        c_k = sp.sb("c_k", [P, S], F32R)
        cos = sp.sb("cos", [P, S])
        sin = sp.sb("sin", [P, S])
        cos_loaded, stacked = sp.sem("cos_loaded"), sp.sem("stacked")
        normalise(nc, "gn", x, acc)
        with Space(nc, "ga") as s:
            norm = s.sb("norm", [P, 2])
            w_down = s.sb("w_down", [P, 2 * LATENT])
            w_v = s.sb("w_v", [P, PAIRS_G, LATENT])
            w_o = s.sb("w_o", [P, PAIRS_G, D])
            hT = s.sb("hT", [P, S])
            c = s.sb("c", [P, S])
            high = s.sb("high", [P, S], F32R)
            low = s.sb("low", [P, S], F32R)
            turned = s.ps("turned", [P, 2, CH])
            down = s.ps("down", [P, 2, CH])
            v_ps = s.ps("v_ps", [P, 2, CH])
            m_ps = s.ps("m_ps", [P, 2, CH])
            m = {n: s.sem(n) for n in ("loaded", "turn_done", "hT_ready", "down_done", "c_ready", "high_ready",
                                       "low_ready", "v_done", "m_done", "copied")}
            with nc.Block() as block:

                @block.sync
                def _(sync):
                    for d, n in ((norm, "g_norm"), (w_down, "w_down"), (w_v, "w_v"), (w_o, "w_o")):
                        sync.dma_start(d[:], dram[n]).then_inc(m["loaded"], 16)
                    sync.dma_start(cos[:], dram["g_cos"]).then_inc(cos_loaded, 16)
                    sync.dma_start(sin[:], dram["g_sin"]).then_inc(cos_loaded, 16)
                    sync.wait_ge(m["high_ready"], NC)
                    sync.wait_ge(m["low_ready"], NC)
                    for stack, rows in ((c_q, slice(0, 64)), (c_k, slice(64, P))):
                        for half, part in ((slice(0, 64), high), (slice(64, P), low)):
                            sync.dma_start(stack[half].bitcast(F32), part[rows].bitcast(F32)).then_inc(stacked, 16)
                    sync.wait_ge(stacked, 4 * 16)

                @block.tensor
                def _(pe):
                    for g in range(NC):
                        if g >= 2:
                            pe.wait_ge(m["hT_ready"], g - 1)
                        for k in range(4):
                            ins = nc.tensor.transpose(turned[:, g % 2, k * P:(k + 1) * P], acc[:, 4 * g + k], ident[:])
                        ins.then_inc(m["turn_done"], 1)
                    pe.wait_ge(m["loaded"], 4 * 16)
                    for c_ in range(NC):
                        pe.wait_ge(m["hT_ready"], c_ + 1)
                        if c_ >= 2:
                            pe.wait_ge(m["c_ready"], c_ - 1)
                        nc.tensor.matmul(down[:, c_ % 2], w_down[:], hT[:, c_ * CH:(c_ + 1) * CH], start=True,
                                         stop=True).then_inc(m["down_done"], 1)
                    for t in range(T):
                        ins = nc.tensor.matmul(v_ps[:, t // 8, (t % 8) * LATENT:(t % 8 + 1) * LATENT],
                                               hT[:, t * P:(t + 1) * P], w_down[:, LATENT:], start=True, stop=True)
                    ins.then_inc(m["v_done"], 1)
                    for g in range(PAIRS_G):
                        for h in range(2):
                            rows = slice(h * 64, h * 64 + 64)
                            ins = nc.tensor.matmul(m_ps[rows, h, (g % 4) * P:(g % 4 + 1) * P], w_v[rows, g],
                                                   w_o[rows, g], start=True, stop=True)
                        if g % 4 == 3:
                            ins.then_inc(m["m_done"], 1)
                            if g == 3:
                                pe.wait_ge(m["copied"], 2)

                @block.vector
                def _(dve):
                    dve.wait_ge(m["loaded"], 4 * 16)
                    for g in range(NC):
                        dve.wait_ge(m["turn_done"], g + 1)
                        nc.vector.tensor_scalar(hT[:, g * CH:(g + 1) * CH], turned[:, g % 2], norm[:, 0:1],
                                                norm[:, 1:2], ALU.mult, ALU.add).then_inc(m["hT_ready"], 1)
                    dve.wait_ge(m["turn_done"], NC)
                    nc.vector.tensor_scalar(acc[:, LATE:T], x[:, 0:T - LATE], 2.0, None, ALU.mult)
                    nc.vector.tensor_scalar(acc[:, 0:LATE], x[:, T - LATE:T], 2.0, None, ALU.mult).then_inc(m["copied"], 1)
                    for c_ in range(NC):
                        cols = slice(c_ * CH, (c_ + 1) * CH)
                        dve.wait_ge(m["down_done"], c_ + 1)
                        nc.vector.tensor_scalar(c[0:64, cols], down[0:64, c_ % 2], 0.125, None, ALU.mult)
                        nc.vector.tensor_copy(c[64:P, cols], down[64:P, c_ % 2]).then_inc(m["c_ready"], 1)
                    dve.wait_ge(m["v_done"], 1)
                    dve.wait_ge(m["copied"], 1)
                    nc.vector.tensor_copy(values.rearrange("p (b t) c -> p b (t c)", b=2), v_ps[:])
                    for k in range(2):
                        dve.wait_ge(m["m_done"], k + 1)
                        for h in range(2):
                            rows = slice(h * 64, h * 64 + 64)
                            ins = nc.vector.tensor_copy(mixers[rows, 4 * k:4 * k + 4],
                                                        m_ps[rows, h].rearrange("p (g n) -> p g n", n=D))
                        ins.then_inc(m["copied"], 1)

                @block.scalar
                def _(act):
                    for c_ in range(NC):
                        cols = slice(c_ * CH, (c_ + 1) * CH)
                        act.wait_ge(m["c_ready"], c_ + 1)
                        nc.scalar.activation(high[:, cols], c[:, cols], ACT.Copy).then_inc(m["high_ready"], 1)

                @block.gpsimd
                def _(pool):
                    for c_ in range(NC):
                        cols = slice(c_ * CH, (c_ + 1) * CH)
                        pool.wait_ge(m["high_ready"], c_ + 1)
                        nc.gpsimd.tensor_tensor(low[:, cols], c[:, cols], high[:, cols].bitcast(F32), ALU.subtract)\
                            .then_inc(m["low_ready"], 1)

        keys = sp.sb("keys", [P, 2, 2, S], F32R)
        q_pair = sp.sb("q_pair", [P, 2, S], F32R)
        q_unit = sp.sb("q_unit", [P, 2, 2, 2, IW], F32R)
        w_raw = sp.sb("w_raw", [P, 4 * P])
        w_up = sp.sb("w_up", [P, 2, 2, 4 * P], F32R)
        by_cos = sp.sb("by_cos", [P, CH])
        by_sin = sp.sb("by_sin", [P, CH])
        k_part = sp.sb("k_part", [P, 2, CH], F32R)
        probs = sp.sb("probs", [P, 2, S])
        probsT = sp.sb("probsT", [P, 2, 2, T, IW])
        most = sp.sb("most", [P, 2, 3])
        bias = sp.sb("bias", [P, 2])
        sums = sp.sb("sums", [P, 2, RT, 2])
        recip = sp.sb("recip", [P, RT])
        mixed = sp.sb("mixed", [P, 2, IW])
        mixer = sp.sb("mixer", [P, D])
        zero = sp.sb("zero", [P, 1])
        score = sp.ps("score", [P, 4, CH])
        turned = sp.ps("turned", [P, 2, CH])
        mix_ps = sp.ps("mix_ps", [P, CH])
        side = sp.ps("side", [P, CH])
        m = {n: sp.sem("m_" + n) for n in
             ("w_loaded", "w_ready", "side_full", "side_free", "roped", "high_ready", "low_ready", "k_loaded",
              "q_loaded0", "q_loaded1", "zeroed", "score_done", "bias_ready", "exp_done", "turn_done", "even_copied",
              "odd_copied", "mix_done", "mixed_ready", "mixer_ready", "maxes", "sums_added", "added")}
        q_loaded = [m["q_loaded0"], m["q_loaded1"]]
        PIECES = 2 * NC
        SIDE0 = 2 * PIECES

        def piece_pe(pe, pair, kind, chunk, swap, use):
            pe.wait_ge(m["side_free"], use)
            src = (c_k, c_q)[kind]
            at = ((2, 3), (0, 1))[kind][swap]
            for part in range(2):
                ins = nc.tensor.matmul(side[:], w_up[:, pair, part, at * P:(at + 1) * P],
                                       src[:, bass.ds(chunk * CH, CH)], start=(part == 0), stop=(part == 1))
            ins.then_inc(m["side_full"], 1)

        def piece_dve(dve, chunk, swap, use, n):
            dve.wait_ge(m["side_full"], use + 1)
            if not swap:
                dve.wait_ge(m["low_ready"], n)
            dst, table = ((by_cos, cos), (by_sin, sin))[swap]
            nc.vector.tensor_tensor(dst[:], side[:], table[:, bass.ds(chunk * CH, CH)], ALU.mult)\
                .then_inc(m["side_free"], 1)

        def part_of(kind, chunk, part, rows=slice(0, P)):
            return k_part[rows, part] if kind == 0 else q_pair[rows, part, bass.ds(chunk * CH, CH)]

        def piece_pool_add(pool, use, n):
            pool.wait_ge(m["side_free"], use + 2)
            nc.gpsimd.tensor_tensor(by_cos[:], by_cos[:], by_sin[:], ALU.add).then_inc(m["roped"], 1)

        def piece_act(act, kind, chunk, n, k_sent):
            act.wait_ge(m["roped"], n + 1)
            if kind == 0:
                act.wait_ge(m["k_loaded"], k_sent)
            nc.scalar.activation(part_of(kind, chunk, 0), by_cos[:], ACT.Copy).then_inc(m["high_ready"], 1)

        def piece_pool_low(pool, kind, chunk, n):
            pool.wait_ge(m["high_ready"], n + 1)
            nc.gpsimd.tensor_tensor(part_of(kind, chunk, 1), by_cos[:], part_of(kind, chunk, 0).bitcast(F32),
                                    ALU.subtract).then_inc(m["low_ready"], 1)

        def send_k(sync, turn, chunk, n):
            sync.wait_ge(m["low_ready"], n + 1)
            for head in range(2):
                for part in range(2):
                    sync.dma_start(keys[part * 64:(part + 1) * 64, turn, head, bass.ds(chunk * CH, CH)].bitcast(F32),
                                   k_part[head * 64:(head + 1) * 64, part].bitcast(F32)).then_inc(m["k_loaded"], 16)

        def send_q(sync, w, chunk):
            for head in range(2):
                for half in range(2):
                    sync.dma_start(q_unit[half * 64:(half + 1) * 64, w, head].bitcast(F32),
                                   q_pair[head * 64:(head + 1) * 64, :, bass.ds(chunk * IW, IW)].bitcast(F32))\
                        .then_inc(q_loaded[w], 16)

        def load_w(sync, pair):
            sync.dma_start(w_raw[:], dram["w_up"][bass.ds(pair, 1), :, :].rearrange("a p n -> (a p) n"))\
                .then_inc(m["w_loaded"], 16)

        def split_w(pool, turn, count):
            pool.wait_ge(m["w_loaded"], 16 * count)
            nc.gpsimd.tensor_tensor(w_up[:, turn, 0], w_raw[:], zero[:].broadcast_to([P, 4 * P]), ALU.add)\
                .then_inc(m["w_ready"], 1)
            pool.wait_ge(m["w_ready"], 2 * count - 1)
            nc.gpsimd.tensor_tensor(w_up[:, turn, 1], w_raw[:], w_up[:, turn, 0].bitcast(F32), ALU.subtract)\
                .then_inc(m["w_ready"], 1)

        cos_part = probs[:, 0, 0:2 * CH].rearrange("p (a n) -> p a n", a=2)
        sin_part = probs[:, 1, 0:2 * CH].rearrange("p (a n) -> p a n", a=2)
        with nc.Block() as block:

            @block.sync
            def _(sync):
                load_w(sync, 0)
                sync.wait_ge(m["w_ready"], 2)
                load_w(sync, 1)
                for c_ in range(NC):
                    send_k(sync, 0, c_, 2 * c_)
                sync.wait_ge(m["low_ready"], PIECES)
                for w in range(2):
                    send_q(sync, w, w)

            @block.gpsimd
            def _(pool):
                nc.gpsimd.memset(zero[:], 0.0).then_inc(m["zeroed"], 1)
                pool.wait_ge(m["zeroed"], 1)
                split_w(pool, 0, 1)
                for n in range(PIECES):
                    pool.wait_ge(m["side_free"], 2 * n + 2)
                    nc.gpsimd.tensor_tensor(cos_part[:, n % 2], cos_part[:, n % 2], sin_part[:, n % 2], ALU.add)\
                        .then_inc(m["roped"], 1)
                split_w(pool, 1, 2)
                nc.gpsimd.memset(mixed[:], 0.0)
                nc.gpsimd.memset(mixer[:], 0.0)
                nc.gpsimd.memset(probsT[:, 1], 0.0)
                nc.gpsimd.memset(sums[:], 1.0)
                nc.gpsimd.memset(recip[:], 1.0)

            @block.tensor
            def _(pe):
                pe.wait_ge(m["w_ready"], 2)
                for n in range(PIECES):
                    kind, c_ = n % 2, n // 2
                    for swap in range(2):
                        use = 2 * n + swap
                        if use >= 4:
                            pe.wait_ge(m["side_free"], use - 3)
                        at = ((2, 3), (0, 1))[kind][swap]
                        for part in range(2):
                            ins = nc.tensor.matmul(score[:, use % 4], w_up[:, 0, part, at * P:(at + 1) * P],
                                                   (c_k, c_q)[kind][:, c_ * CH:(c_ + 1) * CH], start=(part == 0),
                                                   stop=(part == 1))
                        ins.then_inc(m["side_full"], 1)

            @block.vector
            def _(dve):
                def rest(n):
                    kind, c_ = n % 2, n // 2
                    dve.wait_ge(m["high_ready"], n + 1)
                    nc.vector.tensor_tensor(part_of(kind, c_, 1), cos_part[:, n % 2],
                                            part_of(kind, c_, 0).bitcast(F32), ALU.subtract)\
                        .then_inc(m["low_ready"], 1)

                dve.wait_ge(cos_loaded, 32)
                for n in range(PIECES):
                    c_ = n // 2
                    if n >= 2:
                        dve.wait_ge(m["low_ready"], n - 1)
                    for swap, (dst, table) in enumerate(((cos_part, cos), (sin_part, sin))):
                        use = 2 * n + swap
                        dve.wait_ge(m["side_full"], use + 1)
                        nc.vector.tensor_tensor(dst[:, n % 2], score[:, use % 4], table[:, c_ * CH:(c_ + 1) * CH],
                                                ALU.mult).then_inc(m["side_free"], 1)
                    if n:
                        rest(n - 1)
                rest(PIECES - 1)

            @block.scalar
            def _(act):
                for n in range(PIECES):
                    kind, c_ = n % 2, n // 2
                    act.wait_ge(m["roped"], n + 1)
                    if kind == 0 and c_:
                        act.wait_ge(m["k_loaded"], 64 * c_)
                    nc.scalar.activation(part_of(kind, c_, 0), cos_part[:, n % 2], ACT.Copy)\
                        .then_inc(m["high_ready"], 1)

        def rows_of(r):
            return r // 2, r % 2

        def scores(pe, q, k_of, first, rest):
            if first is not None:
                pe.wait_ge(m["exp_done"], first)
            for b in range(4):
                if b == 2 and rest is not None:
                    pe.wait_ge(m["exp_done"], rest)
                for part in range(2):
                    ins = nc.tensor.matmul(score[:, b], q[:, part], k_of(b), start=(part == 0), stop=(part == 1))
                if b:
                    ins.then_inc(m["score_done"], 1)

        def row_max(dve, slot, before):
            for k, banks in enumerate((slice(0, 2), slice(2, 3), slice(3, 4))):
                dve.wait_ge(m["score_done"], before + k + 1)
                nc.vector.tensor_reduce(most[:, slot, k:k + 1], score[:, banks], AX.XY, ALU.max, negate=True)\
                    .then_inc(m["maxes"], 1)
            dve.wait_ge(m["maxes"], before + 3)
            nc.vector.scalar_tensor_tensor(out=bias[:, slot:slot + 1], in0=most[:, slot, 0:1],
                                           scalar=most[:, slot, 1:2], in1=most[:, slot, 2:3], op0=ALU.min,
                                           op1=ALU.min).then_inc(m["bias_ready"], 1)

        def exps(act, slot, w, r, count):
            act.wait_ge(m["bias_ready"], count)
            for k in range(2):
                nc.scalar.activation(probs[:, slot, k * 2 * CH:(k + 1) * 2 * CH],
                                     score[:, 2 * k:2 * k + 2].rearrange("p b n -> p (b n)"), ACT.Exp,
                                     bias=bias[:, slot:slot + 1],
                                     accum_out=sums[:, w, r, k:k + 1]).then_inc(m["exp_done"], 1)

        def copied(w, r, q):
            head, tile = rows_of(r)
            return (probsT[:, w, head, MERGED * q:MERGED * (q + 1), tile * P:(tile + 1) * P],
                    turned[:, q % 2].rearrange("p (t n) -> p t n", n=P))

        def mix(pe, w, tiles):
            for t in tiles:
                for head in range(2):
                    ins = nc.tensor.matmul(mix_ps[head * 64:(head + 1) * 64, 0:IW], values[:, t],
                                           probsT[:, w, head, t], start=(t == 0), stop=(t == T - 1))
            if T - 1 in tiles:
                ins.then_inc(m["mix_done"], 1)

        def take_mixed(act, count):
            act.wait_ge(m["mix_done"], count)
            for head in range(2):
                rows = slice(head * 64, (head + 1) * 64)
                ins = nc.scalar.activation(mixed[rows, head], mix_ps[rows, 0:IW], ACT.Copy)
            ins.then_inc(m["mixed_ready"], 1)

        def output(pe):
            for r in range(RT):
                head, tile = rows_of(r)
                ins = nc.tensor.matmul(side[:, r * D:(r + 1) * D], mixed[:, head, tile * P:(tile + 1) * P], mixer[:],
                                       start=True, stop=True)
            ins.then_inc(m["side_full"], 1)

        def reciprocals(dve, w, U):
            nc.vector.tensor_tensor(recip[:], sums[:, w, :, 0], sums[:, w, :, 1], ALU.add)\
                .then_inc(m["sums_added"], 1)
            dve.wait_ge(m["sums_added"], 2 * U + 1)
            nc.vector.reciprocal(recip[:], recip[:]).then_inc(m["sums_added"], 1)
            dve.wait_ge(m["sums_added"], 2 * U + 2)

        def add_output(dve, U, slot, full):
            dve.wait_ge(m["side_full"], full)
            for r in range(RT):
                _, tile = rows_of(r)
                if r == 2:
                    dve.wait_ge(m["added"], 3 * U + 2)
                a = acc[:, bass.ds(2 * slot + tile, 1)].rearrange("p a d -> p (a d)")
                nc.vector.scalar_tensor_tensor(out=a, in0=side[:, r * D:(r + 1) * D], scalar=recip[:, r:r + 1], in1=a,
                                               op0=ALU.mult, op1=ALU.add)\
                    .then_inc(m["side_free"] if r == RT - 1 else m["added"], 1)

        MIXED_AT = (range(0, 3), range(3, 6), range(6, 10), range(10, T))
        KTURN = 2 * S
        kflat = keys[:].rearrange("p a h n -> p (a h n)")

        with nc.Block() as block:

            @block.sync
            def _(sync):
                with sync.Fori(0, PAIRS_G // 2) as i:
                    for turn in range(2):
                        g = 2 * i + turn
                        sync.wait_ge(m["w_ready"], 2 * g + 4)
                        load_w(sync, g + 2)
                        with sync.Fori(0, NC) as j:
                            for w in range(2):
                                U = 8 * g + 2 * j + w
                                if w == 0:
                                    send_k(sync, 1 - turn, j, PIECES + U)
                                sync.wait_ge(m["score_done"], 12 * U + 12)
                                send_q(sync, w, (2 * j + w + 2) % UNITS)
                sync.wait_ge(q_loaded[0], 64 * (4 * PAIRS_G + 1))
                sync.wait_ge(q_loaded[1], 64 * (4 * PAIRS_G + 1))

            @block.gpsimd
            def _(pool):
                pool.sem_inc(m["mixer_ready"], 1)
                with pool.Fori(0, PAIRS_G // 2) as i:
                    for turn in range(2):
                        g = 2 * i + turn
                        pool.wait_ge(m["side_full"], SIDE0 + 24 * g)
                        split_w(pool, turn, g + 3)
                        with pool.Fori(0, NC) as j:
                            for w in range(2):
                                U = 8 * g + 2 * j + w
                                piece_pool_add(pool, SIDE0 + 3 * U + 1, PIECES + U)
                                piece_pool_low(pool, w, j, PIECES + U)
                                if w == 1:
                                    pool.wait_ge(m["side_full"], SIDE0 + 3 * U + 1)
                                    pool.wait_ge(m["side_full"], SIDE0)
                                    nc.gpsimd.tensor_copy(mixer[:], mixers[:, bass.ds(g, 1)]
                                                          .rearrange("p a n -> p (a n)")).then_inc(m["mixer_ready"], 1)

            @block.tensor
            def _(pe):
                pe.wait_ge(q_loaded[0], 64)
                pe.wait_ge(m["k_loaded"], 256)
                scores(pe, q_unit[:, 0, 0, :, 0:P], lambda b: keys[:, 0, 0, b * CH:(b + 1) * CH], None, None)
                with pe.Fori(0, PAIRS_G // 2) as i:
                    for turn in range(2):
                        g = 2 * i + turn
                        with pe.Fori(0, NC) as j:
                            for w in range(2):
                                U = 8 * g + 2 * j + w
                                for r in range(RT):
                                    G = 4 * U + r
                                    if r < RT - 1:
                                        head, tile = rows_of(r + 1)
                                        q = q_unit[:, w, head, :, tile * P:(tile + 1) * P]
                                        k_of = lambda b, head=head: keys[:, turn, head, b * CH:(b + 1) * CH]
                                    else:
                                        q = q_unit[:, 1 - w, 0, :, 0:P]
                                        if w == 0:
                                            pe.wait_ge(q_loaded[1], 64 * (4 * g + j + 1))
                                            k_of = lambda b: keys[:, turn, 0, b * CH:(b + 1) * CH]
                                        else:
                                            last = (j + 1) // NC
                                            pe.wait_ge(q_loaded[0], 64 * (4 * g + j + 2))
                                            pe.wait_ge(m["k_loaded"], 256 * (g + 1 + last))
                                            base = last * KTURN if turn == 0 else last * -KTURN + KTURN
                                            k_of = lambda b, base=base: kflat[:, bass.ds(base + b * CH, CH)]
                                    scores(pe, q, k_of, 2 * G + 1, 2 * G + 2)

                                    def turn_group(k):
                                        pe.wait_ge(m["odd_copied" if k % 2 else "even_copied"], 2 * G + k // 2 + 1)
                                        for t in range(MERGED):
                                            ins = nc.tensor.transpose(turned[:, k % 2, t * P:(t + 1) * P],
                                                                      probs[:, r % 2, (MERGED * k + t) * P:
                                                                            (MERGED * k + t + 1) * P], ident[:])
                                        ins.then_inc(m["turn_done"], 1)

                                    turn_group(0)
                                    turn_group(1)
                                    if r == 0:
                                        pe.wait_ge(m["side_free"], SIDE0 + 3 * U)
                                        pe.wait_ge(m["mixed_ready"], U + 1)
                                        if w == 0:
                                            pe.wait_ge(m["mixer_ready"], 4 * g + j + 1)
                                        output(pe)
                                    mix(pe, 1 - w, MIXED_AT[r])
                                    if r in (1, 2):
                                        pe.wait_ge(m["w_ready"], 2 * g + 4)
                                        piece_pe(pe, 1 - turn, w, j, r - 1, SIDE0 + 3 * U + r)
                                    turn_group(2)
                                    turn_group(3)
                UL = PAIRS_G * UNITS
                pe.wait_ge(m["side_free"], SIDE0 + 3 * UL)
                pe.wait_ge(m["mixed_ready"], UL + 1)
                pe.wait_ge(m["mixer_ready"], NC * PAIRS_G + 1)
                output(pe)
                pe.wait_ge(m["even_copied"], 8 * UL + 1)
                pe.wait_ge(m["odd_copied"], 8 * UL + 1)
                mix(pe, 1, range(T))
                pe.wait_ge(m["mixed_ready"], UL + 2)
                pe.wait_ge(m["side_free"], SIDE0 + 3 * UL + 1)
                output(pe)

            @block.vector
            def _(dve):
                dve.sem_inc(m["even_copied"], 1)
                row_max(dve, 0, 0)
                with dve.Fori(0, PAIRS_G // 2) as i:
                    for turn in range(2):
                        g = 2 * i + turn
                        with dve.Fori(0, NC) as j:
                            for w in range(2):
                                U = 8 * g + 2 * j + w
                                for r in range(RT):
                                    G = 4 * U + r
                                    row_max(dve, (r + 1) % 2, 3 * G + 3)
                                    dve.wait_ge(m["turn_done"], 4 * G + 1)
                                    nc.vector.tensor_copy(*copied(w, r, 0)).then_inc(m["even_copied"], 1)
                                    if r == 0:
                                        add_output(dve, U, 2 * j + w, SIDE0 + 3 * U + 1)
                                    if r in (1, 2):
                                        piece_dve(dve, j, r - 1, SIDE0 + 3 * U + r, PIECES + U)
                                    if r == 1:
                                        reciprocals(dve, 1 - w, U)
                                    dve.wait_ge(m["turn_done"], 4 * G + 3)
                                    nc.vector.tensor_copy(*copied(w, r, 2)).then_inc(m["even_copied"], 1)
                UL = PAIRS_G * UNITS
                add_output(dve, UL, 0, SIDE0 + 3 * UL + 1)
                dve.wait_ge(m["side_free"], SIDE0 + 3 * UL + 1)
                reciprocals(dve, 1, UL)
                add_output(dve, UL + 1, 1, SIDE0 + 3 * UL + 2)

            @block.scalar
            def _(act):
                act.sem_inc(m["odd_copied"], 1)
                act.sem_inc(m["mixed_ready"], 1)
                exps(act, 0, 0, 0, 1)
                with act.Fori(0, PAIRS_G // 2) as i:
                    for turn in range(2):
                        g = 2 * i + turn
                        with act.Fori(0, NC) as j:
                            for w in range(2):
                                U = 8 * g + 2 * j + w
                                for r in range(RT):
                                    G = 4 * U + r
                                    act.wait_ge(m["turn_done"], 4 * G + 2)
                                    nc.scalar.activation(*copied(w, r, 1), ACT.Copy).then_inc(m["odd_copied"], 1)
                                    exps(act, (r + 1) % 2, w if r < RT - 1 else 1 - w, (r + 1) % RT, G + 2)
                                    act.wait_ge(m["turn_done"], 4 * G + 4)
                                    nc.scalar.activation(*copied(w, r, 3), ACT.Copy).then_inc(m["odd_copied"], 1)
                                    if r == 3:
                                        piece_act(act, w, j, PIECES + U, 64 * (4 * (g + 1) + j))
                                        take_mixed(act, U + 1)
                take_mixed(act, PAIRS_G * UNITS + 1)

    with nc.Block() as block:

        @block.vector
        def _(dve):
            nc.vector.tensor_copy(x[:, 0:T - LATE], acc[:, LATE:T])
            nc.vector.tensor_copy(x[:, T - LATE:T], acc[:, 0:LATE])
    normalise(nc, "n2", x, x)
    clear_semaphores(nc)



EXPERTS, TOP, HID_E = 16, 4, 64
ROUTE = 2.5
GROUPS = EXPERTS // 2 + 1


def experts(nc, dram, const, x):
    ident = const["ident"]
    E = EXPERTS
    with Space(nc, "e") as sp:
        xT = sp.sb("xT", [P, S])
        w_gate = sp.sb("w_gate", [P, GROUPS, P])
        w_up = sp.sb("w_up", [P, GROUPS, P])
        w_down = sp.sb("w_down", [P, GROUPS, D])
        combT = sp.sb("combT", [64, S])
        parts = sp.sb("parts", [64, S], F32R)
        copy = sp.sb("copy", [64, EXPERTS // 2, P], F32R)
        w_loaded = sp.sem("w_loaded")
        with Space(nc, "ea") as s:
            router = s.sb("router", [P, E])
            rows = s.sb("rows", [P, E])
            lower = s.sb("lower", [P, E, E])
            lower16 = s.sb("lower16", [P, E, E], BF16)
            copy32 = s.sb("copy32", [64, EXPERTS // 2, P])
            score = s.sb("score", [P, T, E])
            biased = s.sb("biased", [P, T, E])
            above = s.sb("above", [P, T, E, E], BF16)
            ties = s.sb("ties", [P, T, E, E], BF16)
            rank = s.sb("rank", [P, T, E])
            total = s.sb("total", [P, T])
            comb = s.sb("comb", [P, T, 64])
            turned = s.ps("turned", [P, 2, CH])
            score_ps = s.ps("score_ps", [P, CH])
            comb_ps = s.ps("comb_ps", [P, 4, CH])
            m = {n: s.sem(n) for n in ("loaded", "turn_done", "xT_ready", "score_done", "score_ready", "zeroed",
                                       "comb_ready", "comb_done", "order", "combT_ready", "high_ready")}
            with nc.Block() as block:

                @block.sync
                def _(sync):
                    for d, n in ((router, "router"), (rows, "router_bias"), (lower, "lower"), (copy32, "head_copy")):
                        sync.dma_start(d[:], dram[n]).then_inc(m["loaded"], 16)
                    for d, n in ((w_gate, "w_gate"), (w_up, "w_up_e"), (w_down, "w_down_e")):
                        sync.dma_start(d[:], dram[n]).then_inc(w_loaded, 16)

                @block.tensor
                def _(pe):
                    for g in range(NC):
                        if g >= 2:
                            pe.wait_ge(m["xT_ready"], g - 1)
                        for k in range(4):
                            ins = nc.tensor.transpose(turned[:, g % 2, k * P:(k + 1) * P], x[:, 4 * g + k], ident[:])
                        ins.then_inc(m["turn_done"], 1)
                    pe.wait_ge(m["loaded"], 4 * 16)
                    pe.wait_ge(m["xT_ready"], NC)
                    for t in range(T):
                        ins = nc.tensor.matmul(score_ps[:, t * E:(t + 1) * E], xT[:, t * P:(t + 1) * P], router[:],
                                               start=True, stop=True)
                    ins.then_inc(m["score_done"], 1)
                    pe.wait_ge(m["comb_ready"], 1)
                    for t in range(T):
                        ins = nc.tensor.transpose(comb_ps[0:64, t // 4, (t % 4) * P:(t % 4 + 1) * P], comb[:, t],
                                                  ident[:])
                    ins.then_inc(m["comb_done"], 1)

                @block.scalar
                def _(act):
                    for g in range(NC):
                        act.wait_ge(m["turn_done"], g + 1)
                        nc.scalar.activation(xT[:, g * CH:(g + 1) * CH], turned[:, g % 2], ACT.Copy)\
                            .then_inc(m["xT_ready"], 1)
                    act.wait_ge(m["score_done"], 1)
                    nc.scalar.activation(score[:].rearrange("p t e -> p (t e)"), score_ps[:, 0:T * E], ACT.Sigmoid)\
                        .then_inc(m["score_ready"], 1)

                @block.gpsimd
                def _(pool):
                    nc.gpsimd.memset(comb[:], 0.0).then_inc(m["zeroed"], 1)

                @block.vector
                def _(dve):
                    link = Chain(dve, m["order"])
                    dve.wait_ge(m["loaded"], 4 * 16)
                    nc.vector.tensor_copy(lower16[:], lower[:])
                    nc.vector.tensor_copy(copy[:], copy32[:])
                    dve.wait_ge(m["score_ready"], 1)
                    link(nc.vector.tensor_tensor(biased[:], score[:], rows[:].unsqueeze(1).broadcast_to([P, T, E]),
                                                 ALU.add))
                    other = biased[:].unsqueeze(2).broadcast_to([P, T, E, E])
                    mine = biased[:].unsqueeze(3).broadcast_to([P, T, E, E])
                    nc.vector.tensor_tensor(above[:], other, mine, ALU.is_gt)
                    link(nc.vector.tensor_tensor(ties[:], other, mine, ALU.is_equal))
                    link(nc.vector.tensor_tensor(ties[:], ties[:], lower16[:].unsqueeze(1).broadcast_to([P, T, E, E]),
                                                 ALU.mult))
                    link(nc.vector.tensor_tensor(above[:], above[:], ties[:], ALU.add))
                    link(nc.vector.tensor_reduce(rank[:], above[:], AX.X, ALU.add))
                    link(nc.vector.scalar_tensor_tensor(out=score[:], in0=rank[:], scalar=float(TOP), in1=score[:],
                                                        op0=ALU.is_lt, op1=ALU.mult))
                    link(nc.vector.tensor_reduce(total[:], score[:], AX.X, ALU.add))
                    link(nc.vector.reciprocal(total[:], total[:]))
                    link(nc.vector.tensor_tensor(score[:], score[:], total[:].unsqueeze(2).broadcast_to([P, T, E]),
                                                 ALU.mult))
                    dve.wait_ge(m["zeroed"], 1)
                    for k in (0, 32):
                        ins = nc.vector.tensor_scalar(comb[:, :, k:k + E], score[:], ROUTE, None, ALU.mult)
                    ins.then_inc(m["comb_ready"], 1)
                    dve.wait_ge(m["comb_done"], 1)
                    nc.vector.tensor_copy(combT[:].rearrange("p (b n) -> p b n", b=4), comb_ps[0:64])\
                        .then_inc(m["combT_ready"], 1)
                    dve.wait_ge(m["combT_ready"], 1)
                    nc.vector.tensor_copy(parts[:], combT[:]).then_inc(m["high_ready"], 1)
                    dve.wait_ge(m["high_ready"], 1)
                    nc.vector.tensor_tensor(parts[32:64], combT[32:64], parts[32:64].bitcast(F32), ALU.subtract)

        with Space(nc, "eb") as s:
            hidden = s.sb("hidden", [P, GROUPS, S])
            gated = s.sb("gated", [P, 2, CH])
            g_ps = s.ps("g_ps", [P, 2, CH])
            u_ps = s.ps("u_ps", [P, 2, CH])
            c_ps = s.ps("c_ps", [P, 2, CH])
            prod = s.ps("prod", [P, 2, CH])
            m = {n: s.sem(n) for n in ("g_done", "u_done", "silu_ready", "mult_done", "hidden_ready", "prod_done",
                                       "added")}
            with nc.Block() as block:

                @block.tensor
                def _(pe):
                    pe.wait_ge(w_loaded, 3 * 16)

                    def up(n):
                        c, g = divmod(n, GROUPS)
                        cols = slice(c * CH, (c + 1) * CH)
                        if n >= 2:
                            pe.wait_ge(m["hidden_ready"], n - 1)
                        nc.tensor.matmul(g_ps[:, n % 2], w_gate[:, g], xT[:, cols], start=True, stop=True)\
                            .then_inc(m["g_done"], 1)
                        if g < GROUPS - 1:
                            nc.tensor.matmul(c_ps[:, n % 2], copy[:, g], parts[:, cols], start=True, stop=True)
                        nc.tensor.matmul(u_ps[:, n % 2], w_up[:, g], xT[:, cols], start=True, stop=True)\
                            .then_inc(m["u_done"], 1)

                    def down(t):
                        pe.wait_ge(m["hidden_ready"], GROUPS * (t // 4 + 1))
                        if t >= 2:
                            pe.wait_ge(m["added"], t - 1)
                        for g in range(GROUPS):
                            ins = nc.tensor.matmul(prod[:, t % 2, 0:D], hidden[:, g, t * P:(t + 1) * P], w_down[:, g],
                                                   start=(g == 0), stop=(g == GROUPS - 1))
                        ins.then_inc(m["prod_done"], 1)

                    for c in range(NC + 1):
                        for g in range(GROUPS):
                            if c < NC:
                                up(c * GROUPS + g)
                            if c and g >= 2 and g % 2 == 0:
                                down(4 * (c - 1) + g // 2 - 1)

                @block.scalar
                def _(act):
                    for n in range(NC * GROUPS):
                        act.wait_ge(m["g_done"], n + 1)
                        if n >= 2:
                            act.wait_ge(m["mult_done"], n - 1)
                        nc.scalar.activation(gated[:, n % 2], g_ps[:, n % 2], ACT.Silu).then_inc(m["silu_ready"], 1)

                @block.vector
                def _(dve):
                    def multiply(n):
                        c, g = divmod(n, GROUPS)
                        out = hidden[:, g, c * CH:(c + 1) * CH]
                        dve.wait_ge(m["silu_ready"], n + 1)
                        dve.wait_ge(m["u_done"], n + 1)
                        nc.vector.tensor_tensor(out, gated[:, n % 2], u_ps[:, n % 2], ALU.mult)\
                            .then_inc(m["mult_done"], 1)

                    def weigh(n):
                        c, g = divmod(n, GROUPS)
                        out = hidden[:, g, c * CH:(c + 1) * CH]
                        dve.wait_ge(m["mult_done"], n + 1)
                        if g < GROUPS - 1:
                            nc.vector.tensor_tensor(out, out, c_ps[:, n % 2], ALU.mult)\
                                .then_inc(m["hidden_ready"], 1)
                        else:
                            dve.sem_inc(m["hidden_ready"], 1)

                    def add(t):
                        dve.wait_ge(m["prod_done"], t + 1)
                        nc.vector.tensor_tensor(x[:, t], x[:, t], prod[:, t % 2, 0:D], ALU.add).then_inc(m["added"], 1)

                    for c in range(NC + 1):
                        for g in range(GROUPS):
                            if c < NC:
                                multiply(c * GROUPS + g)
                                weigh(c * GROUPS + g)
                            if c and g >= 2 and g % 2 == 0:
                                add(4 * (c - 1) + g // 2 - 1)
    normalise(nc, "n3", x, x)


def build(nc, dram, out, stages=4):
    with Space(nc, "top") as top:
        x_tok = top.sb("x_tok", [P, T, D])
        const = {n: top.sb(n, [P, P]) for n in ("ident", "upto", "after", "ones")}
        const["ident16"] = top.sb("ident16", [P, P], BF16)
        const["x_loaded"], const["loaded"] = nc.alloc_semaphore("x_loaded"), nc.alloc_semaphore("consts_loaded")
        const["count"] = 3 * 16
        stored = nc.alloc_semaphore("stored")
        Space.used = []
        with nc.Block() as block:

            @block.sync
            def _(sync):
                sync.dma_start(x_tok[:], dram["x"].rearrange("(t p) d -> p t d", p=P)).then_inc(const["x_loaded"], 16)
                for n in ("ident", "upto", "after"):
                    sync.dma_start(const[n][:], dram[n]).then_inc(const["loaded"], 16)

            @block.vector
            def _(dve):
                nc.vector.memset(const["ones"][:], 1.0)
                dve.wait_ge(const["loaded"], const["count"])
                nc.vector.tensor_copy(const["ident16"][:], const["ident"][:])

        with Space(nc, "mid") as mid:
            y_tok = mid.sb("y_tok", [P, T, D])
            state_space(nc, dram, const, x_tok, y_tok)
            if stages >= 2:
                local_transformer(nc, dram, const, y_tok, x_tok)
            if stages >= 3:
                latent_attention(nc, dram, const, y_tok, x_tok)
            if stages >= 4:
                experts(nc, dram, const, y_tok)
            last = y_tok
            with nc.Block() as block:

                @block.sync
                def _(sync):
                    sync.dma_start(out.rearrange("(t p) d -> p t d", p=P), last[:]).then_inc(stored, 16)
                    sync.wait_ge(stored, 16)


def _layout(i):
    f = {k: np.asarray(v) for k, v in i.items()}
    a = {}

    def rows(*vs):
        return np.ascontiguousarray(np.broadcast_to(np.concatenate([v.reshape(-1) for v in vs])[None],
                                                    (P, sum(v.size for v in vs))))

    k = np.arange(P)
    a["ident"] = np.eye(P, dtype=np.float32)
    a["upto"] = (k[:, None] <= k[None]).astype(np.float32)
    a["after"] = (k[:, None] > k[None]).astype(np.float32)
    a["x"] = f["L0_attn_x"].reshape(S, D)
    w = f["L0_attn_in_proj_w"]
    a["w_xbc"] = w[INNER:3 * INNER].T
    a["w_zdt"] = np.concatenate([w[:INNER], w[3 * INNER:]]).T
    a["conv_w"] = f["L0_attn_conv_w"].reshape(4, P, TAPS).transpose(1, 0, 2)
    a["conv_b"] = f["L0_attn_conv_b"].reshape(4, P).T
    a["ss_rows"] = rows(f["L0_attn_dt_bias"], f["L0_attn_A_log"], f["L0_attn_D"], f["L0_attn_ln_w"], f["L0_attn_ln_b"])
    a["norm_w"] = f["L0_attn_norm_w"].reshape(2, P).T
    a["w_out_s"] = f["L0_attn_out_proj_w"].T.reshape(2, P, D).transpose(1, 0, 2)
    F = 2 * PAIRS
    half = np.arange(0, HEAD_L, 2, dtype=np.float32)
    freqs = np.arange(S, dtype=np.float32)[:, None] * (1.0 / 10000.0 ** (half / HEAD_L)).astype(np.float32)[None]
    base = (half + 0.4 * HEAD_L) / (1.4 * HEAD_L)
    power = (np.arange(S, dtype=np.float32) - S // 2) / (WINDOW // 2)
    scale = base[None].astype(np.float64) ** power[:, None]
    cos, sin = np.cos(freqs.astype(np.float64)), np.sin(freqs.astype(np.float64))

    def by_channel(first, second):
        return np.concatenate([first.T, second.T, first.T, second.T]).astype(np.float32)

    a["cos"] = np.stack([by_channel(cos * scale, cos * scale), by_channel(cos / scale, cos / scale)], 1)
    a["sin"] = np.stack([by_channel(-sin * scale, sin * scale), by_channel(-sin / scale, sin / scale)], 1)
    i, j = np.arange(P)[:, None], np.arange(KEYS)[None] - WINDOW
    band = np.where((i < j) | (i > j + WINDOW), np.float32(MASKED), np.float32(0))
    a["band"] = np.concatenate([band, band], 1)
    head_sum = np.zeros((P, F, 64), np.float32)
    for g in range(F):
        for h in range(2):
            for r in (0, 32):
                head_sum[h * 64:(h + 1) * 64, g, r + 2 * g + h] = 1.0
    a["head_sum"], a["head_copy"] = head_sum, head_sum.transpose(2, 1, 0)
    swap = np.r_[HEAD_L // 2:HEAD_L, 0:HEAD_L // 2]
    for n in range(DEPTH):
        w = f["L0_ffn_wqkv"][n]
        a[f"wqkv{n}"] = w
        a[f"wrot{n}"] = w[:, :2 * INNER_L].reshape(D, 2 * HEADS_L, HEAD_L)[:, :, swap].reshape(D, 2 * INNER_L)
        q, k = f["L0_ffn_q_scale"][n], f["L0_ffn_k_scale"][n]
        a[f"scales{n}"] = np.stack([np.tile(q, 2), np.tile(q[swap], 2), np.tile(k, 2), np.tile(k[swap], 2)], 1)
        a[f"wo{n}"] = f["L0_ffn_wo"][n].reshape(PAIRS, P, D).transpose(1, 0, 2)
        pad = HID_T * P - HIDDEN
        a[f"w1{n}"] = np.pad(f["L0_ffn_w1"][n].reshape(D, 2, HIDDEN), ((0, 0), (0, 0), (0, pad)))
        a[f"b1{n}"] = np.pad(f["L0_ffn_b1"][n].reshape(2, HIDDEN), ((0, 0), (0, pad)))\
            .reshape(2, HID_T, P).transpose(2, 0, 1)
        a[f"w2{n}"] = np.pad(f["L0_ffn_w2"][n], ((0, pad), (0, 0))).reshape(HID_T, P, D).transpose(1, 0, 2)
        a[f"b2{n}"] = rows(f["L0_ffn_b2"][n])
        a[f"ffn_norm{n}"] = np.stack([f["L0_ffn_ln_g"][n], f["L0_ffn_ln_b"][n]], 1)
    a["g_norm"] = np.stack([f["L1_attn_ln_scale"], f["L1_attn_ln_bias"]], 1)
    a["w_down"] = np.concatenate([f["L1_attn_w_down_q"], f["L1_attn_w_down_kv"]]).T
    a["w_v"] = f["L1_attn_w_up_v"].reshape(PAIRS_G, P, LATENT).transpose(1, 0, 2)
    a["w_o"] = f["L1_attn_w_out"].T.reshape(PAIRS_G, P, D).transpose(1, 0, 2)
    order = np.r_[0:HEAD_G:2, 1:HEAD_G:2]
    turned = np.r_[1:HEAD_G:2, 0:HEAD_G:2]
    ups = []
    for name in ("L1_attn_w_up_q", "L1_attn_w_up_k"):
        w = f[name].reshape(PAIRS_G, 2, HEAD_G, LATENT)
        for o in (order, turned):
            ups.append(w[:, :, o].reshape(PAIRS_G, P, LATENT).transpose(0, 2, 1))
    up = np.concatenate(ups, 2)
    up = np.concatenate([up, up], 1)
    a["w_up"] = np.concatenate([up, up[:2]])
    inv = 1.0 / 10000.0 ** (np.arange(0, HEAD_G, 2, dtype=np.float32) / HEAD_G)
    freqs = np.outer(np.arange(S, dtype=np.float32), inv)
    cos, sin = (np.concatenate([t(freqs), t(freqs)], 1)[:, ::2] for t in (np.cos, np.sin))
    a["g_cos"] = np.concatenate([cos.T] * 4).astype(np.float32)
    a["g_sin"] = np.concatenate([-sin.T, sin.T] * 2).astype(np.float32)
    a["router"] = f["L1_ffn_gate_w"].T
    a["router_bias"] = rows(f["L1_ffn_gate_b"])
    e = np.arange(EXPERTS)
    a["lower"] = rows((e[None] < e[:, None]).astype(np.float32)).reshape(P, EXPERTS, EXPERTS)
    w13 = np.concatenate([f["L1_ffn_w13"], f["L1_ffn_w13_s"][None], np.zeros((1, P, D), np.float32)])
    w13 = w13.reshape(GROUPS, 2, 2, HID_E, D)
    a["w_gate"] = w13[:, :, 0].reshape(GROUPS, P, D).transpose(2, 0, 1)
    a["w_up_e"] = w13[:, :, 1].reshape(GROUPS, P, D).transpose(2, 0, 1)
    w2 = np.concatenate([f["L1_ffn_w2"], f["L1_ffn_w2_s"][None], np.zeros((1, D, HID_E), np.float32)])
    a["w_down_e"] = w2.transpose(0, 2, 1).reshape(GROUPS, P, D).transpose(1, 0, 2)
    return {n: np.ascontiguousarray(v) for n, v in a.items()}


def kernel(**inputs):
    import numpy as _np
    import concourse.bacc as _bacc
    from concourse import mybir as _mybir
    from concourse.bass_utils import run_bass_kernel_spmd as _run

    nc = _bacc.Bacc("TRN2", target_bir_lowering=False, num_devices=1)
    arrays = _layout(inputs)
    dram = {n: nc.dram_tensor(n, a.shape, _mybir.dt.from_np(a.dtype), kind="ExternalInput").ap()
            for n, a in arrays.items()}
    out = nc.dram_tensor("out", (S, D), _mybir.dt.from_np(_np.dtype("float32")), kind="ExternalOutput").ap()
    build(nc, dram, out)
    result = _run(nc, [arrays], core_ids=[0])
    return result.results[0]["out"].reshape(1, S, D)
```
